# Optimizing a Trainium2 kernel written in Bass

```python
import numpy as np
import jax
import jax.numpy as jnp

def _softmax(x, axis=-1):
    return jax.nn.softmax(x, axis=axis)

def _gelu(x):
    return jax.nn.gelu(x, approximate=True)

def _silu(x):
    return jax.nn.silu(x)

def _sigmoid(x):
    return jax.nn.sigmoid(x)

def _layernorm(x, axis=-1, eps=1e-05):
    m = jnp.mean(x, axis=axis, keepdims=True)
    v = jnp.var(x, axis=axis, keepdims=True)
    return (x - m) / jnp.sqrt(v + eps)

def _scatter_add(tgt, idx, src, axis=0):
    return tgt.at[idx].add(src)

def _segment_sum(src, seg, n):
    return jax.ops.segment_sum(src, seg, n)
kernel_name = 'mk_gnn_resnorm_d4_gnn_r64_22c685'

def setup_inputs(seed: int=0):
    np.random.seed(seed)
    _w = jnp.asarray

    def _rec_inputs():
        import jax
        import jax.numpy as jnp
        _gk = jax.random.key(seed)
        x = -0.000202 + 1 * jax.random.normal(jax.random.fold_in(_gk, 1), (50000, 128), jnp.float32)
        src = jax.random.randint(jax.random.fold_in(_gk, 2), (25000,), 0, 50000, jnp.int32)
        dst = jnp.minimum((50000 * jax.random.uniform(jax.random.fold_in(_gk, 3), (25000,)) ** 2.0).astype(jnp.int32), 49999)
        _o = jnp.argsort(dst, stable=True)
        src = src[_o]
        dst = dst[_o]
        return (x, src, dst)
    x, src, dst = _rec_inputs()

    def _L0_gnn_setup():
        import jax, jax.numpy as jnp
        import numpy as np
        N_NODES = 50000
        N_EDGES = 12500
        DIM = 128
        BN_EPS = 1e-05
        key = jax.random.key(seed)
        ks = jax.random.split(key, 12)
        d = DIM
        s = 1.0 / np.sqrt(d)
        x = jax.random.normal(ks[0], (N_NODES, d), dtype=jnp.float32)
        edge_index = jax.random.randint(ks[1], (2, N_EDGES), 0, N_NODES, dtype=jnp.int64)
        W_msg = jax.random.uniform(ks[2], (d, d), jnp.float32, -s, s)
        b_msg = jax.random.uniform(ks[3], (d,), jnp.float32, -s, s)
        sa = 1.0 / np.sqrt(2 * d)
        W_att = jax.random.uniform(ks[4], (2 * d, 1), jnp.float32, -sa, sa)
        b_att = jax.random.uniform(ks[5], (1,), jnp.float32, -sa, sa)
        W_ih = jax.random.uniform(ks[6], (3 * d, d), jnp.float32, -s, s)
        b_ih = jax.random.uniform(ks[7], (3 * d,), jnp.float32, -s, s)
        W_hh = jax.random.uniform(ks[8], (3 * d, d), jnp.float32, -s, s)
        b_hh = jax.random.uniform(ks[9], (3 * d,), jnp.float32, -s, s)
        gamma = jnp.ones((d,), jnp.float32)
        beta = jnp.zeros((d,), jnp.float32)
        return {'x': x, 'edge_index': edge_index, 'W_msg': W_msg, 'b_msg': b_msg, 'W_att': W_att, 'b_att': b_att, 'W_ih': W_ih, 'b_ih': b_ih, 'W_hh': W_hh, 'b_hh': b_hh, 'gamma': gamma, 'beta': beta}
    _L0_gnn_all = _L0_gnn_setup()
    _L0_gnn_in = {k: v for k, v in _L0_gnn_all.items() if k in ('W_msg', 'b_msg', 'W_att', 'b_att', 'W_ih', 'b_ih', 'W_hh', 'b_hh', 'gamma', 'beta')}
    del _L0_gnn_all

    def _L1_gnn_setup():
        import jax, jax.numpy as jnp
        import numpy as np
        N_NODES = 100000
        N_EDGES = 10000
        IN_DIM = 128
        OUT_DIM = 128
        key = jax.random.key(seed)
        k1, k2, k3, k4 = jax.random.split(key, 4)
        x = jax.random.normal(k1, (N_NODES, IN_DIM), dtype=jnp.float32)
        edge_index = jax.random.randint(k2, (2, N_EDGES), 0, N_NODES, dtype=jnp.int64)
        bound = 1.0 / np.sqrt(IN_DIM)
        W = jax.random.uniform(k3, (OUT_DIM, IN_DIM), minval=-bound, maxval=bound, dtype=jnp.float32)
        b = jax.random.uniform(k4, (OUT_DIM,), minval=-bound, maxval=bound, dtype=jnp.float32)
        return {'x': x, 'edge_index': edge_index, 'W': W, 'b': b}
    _L1_gnn_all = _L1_gnn_setup()
    _L1_gnn_in = {k: v for k, v in _L1_gnn_all.items() if k in ('W', 'b')}
    del _L1_gnn_all

    def _L2_gnn_setup():
        import jax, jax.numpy as jnp
        import numpy as np
        N_NODES = 50000
        N_EDGES = 9375
        IN_DIM = 128
        OUT_DIM = 128
        EPS = 1e-05

        def _layernorm(x, gamma, beta):
            mu = jnp.mean(x, axis=-1, keepdims=True)
            var = jnp.mean(jnp.square(x - mu), axis=-1, keepdims=True)
            return (x - mu) * jax.lax.rsqrt(var + EPS) * gamma + beta
        key = jax.random.key(seed)
        k1, k2, k3 = jax.random.split(key, 3)
        h = jax.random.normal(k1, (N_NODES, IN_DIM), dtype=jnp.float32)
        edge_index = jax.random.randint(k2, (2, N_EDGES), 0, N_NODES, dtype=jnp.int64)
        ln_gamma = jnp.ones((IN_DIM,), dtype=jnp.float32)
        ln_beta = jnp.zeros((IN_DIM,), dtype=jnp.float32)
        W = jax.random.normal(k3, (OUT_DIM, 2 * IN_DIM), dtype=jnp.float32) * (1.0 / np.sqrt(2 * IN_DIM))
        b = jnp.zeros((OUT_DIM,), dtype=jnp.float32)
        return {'h': h, 'edge_index': edge_index, 'ln_gamma': ln_gamma, 'ln_beta': ln_beta, 'W': W, 'b': b}
    _L2_gnn_all = _L2_gnn_setup()
    _L2_gnn_in = {k: v for k, v in _L2_gnn_all.items() if k in ('ln_gamma', 'ln_beta', 'W', 'b')}
    del _L2_gnn_all

    def _L3_gnn_setup():
        import jax, jax.numpy as jnp
        import numpy as np
        N = 50000
        E = 6250
        D_IN = 128
        H = 4
        C = 64
        HC = H * C
        H3 = 6
        D_OUT = 128

        def _gat(x, src, dst, W, a_src, a_dst, b, concat):
            n = x.shape[0]
            h_, c_ = a_src.shape
            h = (x @ W).reshape(n, h_, c_)
            e = (h * a_src).sum(-1)[src] + (h * a_dst).sum(-1)[dst]
            e = jnp.where(e > 0, e, 0.2 * e)
            m = jax.ops.segment_max(e, dst, num_segments=n)
            w = jnp.exp(e - m[dst])
            denom = jax.ops.segment_sum(w, dst, num_segments=n)
            alpha = w / (denom[dst] + 1e-16)
            out = jax.ops.segment_sum(h[src] * alpha[:, :, None], dst, num_segments=n)
            out = out.reshape(n, h_ * c_) if concat else out.mean(axis=1)
            return out + b
        key = jax.random.key(seed)
        ks = jax.random.split(key, 22)
        rn = lambda k, shape, s=0.05: jax.random.normal(k, shape, dtype=jnp.float32) * s
        return {'x': rn(ks[0], (N, D_IN), 1.0), 'edge_index': jax.random.randint(ks[1], (2, E), 0, N, dtype=jnp.int32), 'W1': rn(ks[2], (D_IN, HC)), 'as1': rn(ks[3], (H, C)), 'ad1': rn(ks[4], (H, C)), 'b1': jnp.zeros((HC,), jnp.float32), 's1W': rn(ks[5], (D_IN, HC)), 's1b': jnp.zeros((HC,), jnp.float32), 'W2': rn(ks[6], (HC, HC)), 'as2': rn(ks[7], (H, C)), 'ad2': rn(ks[8], (H, C)), 'b2': jnp.zeros((HC,), jnp.float32), 's2W': rn(ks[9], (HC, HC)), 's2b': jnp.zeros((HC,), jnp.float32), 'W3': rn(ks[10], (HC, H3 * D_OUT)), 'as3': rn(ks[11], (H3, D_OUT)), 'ad3': rn(ks[12], (H3, D_OUT)), 'b3': jnp.zeros((D_OUT,), jnp.float32), 's3W': rn(ks[13], (HC, D_OUT)), 's3b': jnp.zeros((D_OUT,), jnp.float32)}
    _L3_gnn_all = _L3_gnn_setup()
    _L3_gnn_in = {k: v for k, v in _L3_gnn_all.items() if k in ('W1', 'as1', 'ad1', 'b1', 's1W', 's1b', 'W2', 'as2', 'ad2', 'b2', 's2W', 's2b', 'W3', 'as3', 'ad3', 'b3', 's3W', 's3b')}
    del _L3_gnn_all
    return {'x': x, 'src': src, 'dst': dst, 'L0_gnn_W_msg': _L0_gnn_in['W_msg'], 'L0_gnn_b_msg': _L0_gnn_in['b_msg'], 'L0_gnn_W_att': _L0_gnn_in['W_att'], 'L0_gnn_b_att': _L0_gnn_in['b_att'], 'L0_gnn_W_ih': _L0_gnn_in['W_ih'], 'L0_gnn_b_ih': _L0_gnn_in['b_ih'], 'L0_gnn_W_hh': _L0_gnn_in['W_hh'], 'L0_gnn_b_hh': _L0_gnn_in['b_hh'], 'L0_gnn_gamma': _L0_gnn_in['gamma'], 'L0_gnn_beta': _L0_gnn_in['beta'], 'L1_gnn_W': _L1_gnn_in['W'], 'L1_gnn_b': _L1_gnn_in['b'], 'L2_gnn_ln_gamma': _L2_gnn_in['ln_gamma'], 'L2_gnn_ln_beta': _L2_gnn_in['ln_beta'], 'L2_gnn_W': _L2_gnn_in['W'], 'L2_gnn_b': _L2_gnn_in['b'], 'L3_gnn_W1': _L3_gnn_in['W1'], 'L3_gnn_as1': _L3_gnn_in['as1'], 'L3_gnn_ad1': _L3_gnn_in['ad1'], 'L3_gnn_b1': _L3_gnn_in['b1'], 'L3_gnn_s1W': _L3_gnn_in['s1W'], 'L3_gnn_s1b': _L3_gnn_in['s1b'], 'L3_gnn_W2': _L3_gnn_in['W2'], 'L3_gnn_as2': _L3_gnn_in['as2'], 'L3_gnn_ad2': _L3_gnn_in['ad2'], 'L3_gnn_b2': _L3_gnn_in['b2'], 'L3_gnn_s2W': _L3_gnn_in['s2W'], 'L3_gnn_s2b': _L3_gnn_in['s2b'], 'L3_gnn_W3': _L3_gnn_in['W3'], 'L3_gnn_as3': _L3_gnn_in['as3'], 'L3_gnn_ad3': _L3_gnn_in['ad3'], 'L3_gnn_b3': _L3_gnn_in['b3'], 'L3_gnn_s3W': _L3_gnn_in['s3W'], 'L3_gnn_s3b': _L3_gnn_in['s3b']}

def reference(x, src, dst, L0_gnn_W_msg, L0_gnn_b_msg, L0_gnn_W_att, L0_gnn_b_att, L0_gnn_W_ih, L0_gnn_b_ih, L0_gnn_W_hh, L0_gnn_b_hh, L0_gnn_gamma, L0_gnn_beta, L1_gnn_W, L1_gnn_b, L2_gnn_ln_gamma, L2_gnn_ln_beta, L2_gnn_W, L2_gnn_b, L3_gnn_W1, L3_gnn_as1, L3_gnn_ad1, L3_gnn_b1, L3_gnn_s1W, L3_gnn_s1b, L3_gnn_W2, L3_gnn_as2, L3_gnn_ad2, L3_gnn_b2, L3_gnn_s2W, L3_gnn_s2b, L3_gnn_W3, L3_gnn_as3, L3_gnn_ad3, L3_gnn_b3, L3_gnn_s3W, L3_gnn_s3b):
    import jax
    import jax.numpy as jnp

    def _L0_gnn_ref(x, edge_index, W_msg, b_msg, W_att, b_att, W_ih, b_ih, W_hh, b_hh, gamma, beta):
        import jax, jax.numpy as jnp
        import numpy as np
        N_NODES = 50000
        N_EDGES = 12500
        DIM = 128
        BN_EPS = 1e-05
        num_nodes, d = x.shape
        src = edge_index[0]
        dst = edge_index[1]
        xs = x[src]
        xd = x[dst]
        att = jax.nn.sigmoid(xs @ W_att[:d] + xd @ W_att[d:] + b_att)
        messages = (xs @ W_msg + b_msg) * att
        aggregated = jax.ops.segment_sum(messages, dst, num_segments=num_nodes)
        gi = aggregated @ W_ih.T + b_ih
        gh = x @ W_hh.T + b_hh
        i_r, i_z, i_n = jnp.split(gi, 3, axis=1)
        h_r, h_z, h_n = jnp.split(gh, 3, axis=1)
        r = jax.nn.sigmoid(i_r + h_r)
        z = jax.nn.sigmoid(i_z + h_z)
        n = jnp.tanh(i_n + r * h_n)
        h_new = (1.0 - z) * n + z * x
        mean = jnp.mean(h_new, axis=0)
        var = jnp.var(h_new, axis=0)
        return gamma * (h_new - mean) * jax.lax.rsqrt(var + BN_EPS) + beta

    def _L1_gnn_ref(x, edge_index, W, b):
        import jax, jax.numpy as jnp
        import numpy as np
        N_NODES = 100000
        N_EDGES = 10000
        IN_DIM = 128
        OUT_DIM = 128
        src = edge_index[0]
        dst = edge_index[1]
        messages = x[src]
        agg = jax.ops.segment_sum(messages, dst, num_segments=x.shape[0])
        out = jax.nn.relu(agg @ W.T + b)
        return out

    def _L2_gnn_ref(h, edge_index, ln_gamma, ln_beta, W, b):
        import jax, jax.numpy as jnp
        import numpy as np
        N_NODES = 50000
        N_EDGES = 9375
        IN_DIM = 128
        OUT_DIM = 128
        EPS = 1e-05

        def _layernorm(x, gamma, beta):
            mu = jnp.mean(x, axis=-1, keepdims=True)
            var = jnp.mean(jnp.square(x - mu), axis=-1, keepdims=True)
            return (x - mu) * jax.lax.rsqrt(var + EPS) * gamma + beta
        src, dst = (edge_index[0], edge_index[1])
        n = h.shape[0]
        hn = _layernorm(h, ln_gamma, ln_beta)
        ones = jnp.ones((src.shape[0],), dtype=h.dtype)
        deg_out = jnp.clip(jax.ops.segment_sum(ones, src, num_segments=n), 1.0)
        deg_in = jnp.clip(jax.ops.segment_sum(ones, dst, num_segments=n), 1.0)
        inv_sqrt_out = jax.lax.rsqrt(deg_out)
        inv_sqrt_in = jax.lax.rsqrt(deg_in)
        msg_src = hn * inv_sqrt_out[:, None]
        gathered = msg_src[src]
        agg = jax.ops.segment_sum(gathered, dst, num_segments=n)
        message = agg * inv_sqrt_in[:, None]
        cat = jnp.concatenate([hn, message], axis=1)
        return cat @ W.T + b

    def _L3_gnn_ref(x, edge_index, W1, as1, ad1, b1, s1W, s1b, W2, as2, ad2, b2, s2W, s2b, W3, as3, ad3, b3, s3W, s3b):
        import jax, jax.numpy as jnp
        import numpy as np
        N = 50000
        E = 6250
        D_IN = 128
        H = 4
        C = 64
        HC = H * C
        H3 = 6
        D_OUT = 128

        def _gat(x, src, dst, W, a_src, a_dst, b, concat):
            n = x.shape[0]
            h_, c_ = a_src.shape
            h = (x @ W).reshape(n, h_, c_)
            e = (h * a_src).sum(-1)[src] + (h * a_dst).sum(-1)[dst]
            e = jnp.where(e > 0, e, 0.2 * e)
            m = jax.ops.segment_max(e, dst, num_segments=n)
            w = jnp.exp(e - m[dst])
            denom = jax.ops.segment_sum(w, dst, num_segments=n)
            alpha = w / (denom[dst] + 1e-16)
            out = jax.ops.segment_sum(h[src] * alpha[:, :, None], dst, num_segments=n)
            out = out.reshape(n, h_ * c_) if concat else out.mean(axis=1)
            return out + b
        n = x.shape[0]
        loops = jnp.arange(n, dtype=edge_index.dtype)
        src = jnp.concatenate([edge_index[0], loops])
        dst = jnp.concatenate([edge_index[1], loops])
        h = jax.nn.elu(_gat(x, src, dst, W1, as1, ad1, b1, True) + x @ s1W + s1b)
        h = jax.nn.elu(_gat(h, src, dst, W2, as2, ad2, b2, True) + h @ s2W + s2b)
        h = jax.nn.elu(_gat(h, src, dst, W3, as3, ad3, b3, False) + h @ s3W + s3b)
        return h
    edge_index = jnp.stack([src, dst])
    x = _layernorm(x + _L0_gnn_ref(x, edge_index, L0_gnn_W_msg, L0_gnn_b_msg, L0_gnn_W_att, L0_gnn_b_att, L0_gnn_W_ih, L0_gnn_b_ih, L0_gnn_W_hh, L0_gnn_b_hh, L0_gnn_gamma, L0_gnn_beta), axis=-1)
    x = _layernorm(x + _L1_gnn_ref(x, edge_index, L1_gnn_W, L1_gnn_b), axis=-1)
    x = _layernorm(x + _L2_gnn_ref(x, edge_index, L2_gnn_ln_gamma, L2_gnn_ln_beta, L2_gnn_W, L2_gnn_b), axis=-1)
    x = _layernorm(x + _L3_gnn_ref(x, edge_index, L3_gnn_W1, L3_gnn_as1, L3_gnn_ad1, L3_gnn_b1, L3_gnn_s1W, L3_gnn_s1b, L3_gnn_W2, L3_gnn_as2, L3_gnn_ad2, L3_gnn_b2, L3_gnn_s2W, L3_gnn_s2b, L3_gnn_W3, L3_gnn_as3, L3_gnn_ad3, L3_gnn_b3, L3_gnn_s3W, L3_gnn_s3b), axis=-1)
    return x

_drawn_inputs = setup_inputs


def setup_inputs(seed=0):
    import zlib

    import numpy as np

    out = dict(_drawn_inputs(seed))
    spreads = {'L0_gnn_gamma': (1.0, 0.2),
     'L0_gnn_beta': (0.0, 0.1),
     'L2_gnn_ln_gamma': (1.0, 0.2),
     'L2_gnn_ln_beta': (0.0, 0.1),
     'L2_gnn_b': (0.0, 0.1),
     'L3_gnn_b1': (0.0, 0.1),
     'L3_gnn_s1b': (0.0, 0.1),
     'L3_gnn_b2': (0.0, 0.1),
     'L3_gnn_s2b': (0.0, 0.1),
     'L3_gnn_b3': (0.0, 0.1),
     'L3_gnn_s3b': (0.0, 0.1)}
    factors = {'L0_gnn_b_msg': 8.0,
     'L0_gnn_W_att': 4.359,
     'L0_gnn_b_ih': 5.658,
     'L0_gnn_b_hh': 6.341,
     'L3_gnn_as1': 4.303,
     'L3_gnn_ad1': 23.086,
     'L3_gnn_as2': 6.794,
     'L3_gnn_ad2': 75.513,
     'L3_gnn_as3': 8.0,
     'L3_gnn_ad3': 200.0}
    for name, (base, spread) in spreads.items():
        noise = np.random.default_rng([zlib.crc32(name.encode()), seed]).standard_normal(out[name].shape)
        drawn = base * np.exp(spread * noise) if base else spread * noise
        out[name] = jnp.asarray(drawn.astype(out[name].dtype))
    for name, factor in factors.items():
        out[name] = (out[name] * factor).astype(out[name].dtype)
    return out
```

```python
from contextlib import ExitStack, contextmanager

import numpy as np

import concourse.bass as bass
from concourse import mybir

P = 128
N = 50000
E = 25000
D = 128
PER = 4
GROUP = P * PER
GROUPS = -(-N // GROUP)
NPAD = GROUPS * GROUP
LAST_VALID = (N - (GROUPS - 1) * GROUP) // PER
T = 196
EPAD = P * T
RING = 4
ITERS = T // RING
NROW = NPAD + RING * P
PAIRS = GROUPS // 2
H1, C1 = 4, 64
HC = H1 * C1
H3 = 6
EPS = 1e-5
BIG = 1e30

F32 = mybir.dt.float32
F16 = mybir.dt.float16
I32 = mybir.dt.int32
ALU = mybir.AluOpType
ACT = mybir.ActivationFunctionType
AX = mybir.AxisListType

assert T % RING == 0 and GROUPS % 2 == 0 and EPAD >= E and (N - (GROUPS - 1) * GROUP) % PER == 0


@contextmanager
def phase(nc):
    sems = []
    with ExitStack() as ctx:
        yield ctx, sems
        with nc.Block() as block:
            @block.gpsimd
            def _(pool):
                for s in sems:
                    pool.sem_clear(s)


class Steps:

    def __init__(self, eng, sem):
        self.eng, self.sem, self.n, self.base = eng, sem, 0, 0

    def __call__(self, ins):
        ins.then_inc(self.sem, 1)
        self.n += 1
        self.eng.wait_ge(self.sem, self.base + self.n)

    def loop(self, i, per):
        self.base, self.per, self.start = i * per, per, self.n

    def done(self, times):
        assert self.n - self.start == self.per, (self.n - self.start, self.per)
        self.base, self.n = 0, self.start + self.per * times


def grouped(table):
    return table[0:NPAD, :].rearrange("(g p j) d -> g p (j d)", g=GROUPS, p=P, j=PER)


def build(nc, A, out):
    ctx = ExitStack()
    with ctx:
        def sb(name, shape, dt=F32):
            return ctx.enter_context(nc.sbuf_tensor(name, shape, dt))

        def sem(name):
            return ctx.enter_context(nc.semaphore(name))

        def dram(name, shape):
            return nc.dram_tensor(name, shape, F32).ap()

        K = {"x": A["x"], "dma_sem": sem}
        K["agg0"] = dram("agg0", (NROW, D))
        K["agg1"] = dram("agg1", (NROW, D))
        K["hT"] = dram("hT", (D, NPAD))
        K["x1"] = dram("x1", (NPAD, D))
        K["msg"] = dram("msg", (NPAD, D))
        K["pre2"] = dram("pre2", (NROW, D))
        K["x3"] = dram("x3", (NPAD, D))
        K["pre3"] = dram("pre3", (NROW, HC))
        K["sc3"] = dram("sc3", (NPAD, 2 * H1))
        K["h4"] = dram("h4", (NPAD, HC))
        K["pre4"] = dram("pre4", (NROW, HC))
        K["sc4"] = dram("sc4", (NPAD, 2 * H1))
        K["h5"] = dram("h5", (NPAD, HC))
        K["pre5"] = dram("pre5", (NROW, D))
        K["sc5"] = dram("sc5", (NPAD, 2 * H3))
        K["ident"] = sb("ident", [P, P])
        K["ones"] = sb("ones", [P, P])
        K["eps"] = sb("eps", [P, 1])
        K["edge_idx"] = sb("edge_idx", [P, T + RING, 2], I32)
        K["scat_idx"] = sb("scat_idx", [P, T], I32)
        K["fin_idx"] = sb("fin_idx", [P, 1], I32)
        for m in ("cont", "cnext", "pcont", "pnext", "lead", "trail", "inner", "plead", "ptrail", "isq_in"):
            K[m] = sb(m, [P, T])
        for m in ("LF", "FF", "LL", "FL", "pLF", "pFF", "pLL", "pFL"):
            K[m] = sb("m" + m, [P, P])
        K["nosingle"] = sb("nosingle", [P, 1])
        K["isq_out"] = sb("isq_out", [P, GROUPS * PER])
        K["whh"] = sb("whh", [D, 3 * D])
        K["wih"] = sb("wih", [D, 3 * D])
        K["wmsg"] = sb("wmsg", [D, D])
        K["w1"] = sb("w1", [D, D])
        K["w2a"] = sb("w2a", [D, D])
        K["w2b"] = sb("w2b", [D, D])
        K["att"] = sb("att", [P, 2 * D])
        K["batt"] = sb("batt", [P, 1])
        K["bmsg"] = sb("bmsg", [P, D])
        K["brz"] = sb("brz", [D, 4])
        K["bn"] = sb("bn", [D, 2])
        K["bnss"] = sb("bnss", [D, 2])
        K["b1"] = sb("b1", [P, D])
        K["ln_g"] = sb("ln_g", [P, D])
        K["ln_b"] = sb("ln_b", [P, D])
        K["b2"] = sb("b2", [P, D])
        K["g1w"] = sb("g1w", [D, HC])
        K["g1d"] = sb("g1d", [D, HC + 2 * H1])
        K["g1b"] = sb("g1b", [P, HC])
        K["g2w"] = sb("g2w", [D, 2, HC])
        K["g2d"] = sb("g2d", [D, 2, HC + 2 * H1])
        K["g2b"] = sb("g2b", [P, HC])
        K["g3w"] = sb("g3w", [D, 2, H3 * D])
        K["g3d"] = sb("g3d", [D, 2, D + 2 * H3])
        K["g3b"] = sb("g3b", [P, D])
        K["stats"] = sb("stats", [D, GROUPS, 6])

        prepare(nc, A, K)
        out_degree(nc, A, K)
        edges(nc, K, "e0", A["x"], K["wmsg"], K["agg0"])
        gru(nc, A, K)
        norm0(nc, A, K)
        edges(nc, K, "e1", K["x1"], K["w1"], K["agg1"])
        dense1(nc, K)
        edges(nc, K, "e2", K["msg"], K["w2b"], K["pre2"])
        dense2(nc, K)
        for n, (h, kb, w) in enumerate(((H1, 1, K["g1w"]), (H1, 2, K["g2w"]), (H3, 2, K["g3w"]))):
            table = (K["x3"], K["h4"], K["h5"])[n]
            scores, pre = K[f"sc{n + 3}"], K[f"pre{n + 3}"]
            with nc.sbuf_tensor(f"alpha{n}", [P, h, T], F32) as alpha:
                edge_scores(nc, K, n, h, scores, alpha)
                edge_messages(nc, K, n, h, kb, w, table, pre, alpha)
            if n < 2:
                dense_gat(nc, K, n, pre, K[f"h{n + 4}"], (K["g2d"], K["g3d"])[n], (K["g2b"], K["g3b"])[n],
                          K[f"pre{n + 4}"], K[f"sc{n + 4}"])
        final(nc, K, out)


def prepare(nc, A, K):
    with phase(nc) as (ctx, sems):
        def sb(name, shape, dt=F32):
            return ctx.enter_context(nc.sbuf_tensor("prep_" + name, shape, dt))

        def sem(name):
            s = ctx.enter_context(nc.semaphore("prep_" + name))
            sems.append(s)
            return s

        ZC = NROW // P * D // 12
        assert ZC * 12 * P == NROW * D
        zero = sb("zero", [P, ZC])
        dstF = sb("dstF", [P, T])
        nxtI = sb("nxtI", [P, T], I32)
        nxtF = sb("nxtF", [P, 1])
        dumI = sb("dumI", [P, T], I32)
        dum = sb("dum", [P, T])
        tmp = sb("tmp", [P, T])
        tmp2 = sb("tmp2", [P, T])
        idx = sb("idx", [P, 2, T], I32)
        lb = sb("lb", [P, P])
        fb = sb("fb", [P, P])
        bt = sb("bt", [D, 6])
        ts = sb("ts", [P, 2])
        s1w = sb("s1w", [D, HC])
        s2w = sb("s2w", [D, 2, HC])
        s3w = sb("s3w", [D, 2, D])
        avs = sb("avs", [P, 2, HC])
        avs2 = sb("avs2", [P, 2, HC])
        avs3 = sb("avs3", [P, 2, H3 * D])
        prod = sb("prod", [D, H3 * D])
        sbias = [sb(f"sbias{i}", [P, w]) for i, w in enumerate((HC, HC, D))]
        pfirst = ctx.enter_context(nc.psum_tensor("prep_pfirst", [P, 512], F32))
        plast = ctx.enter_context(nc.psum_tensor("prep_plast", [P, 512], F32))
        ptot = ctx.enter_context(nc.psum_tensor("prep_ptot", [P, 2, 512], F32))
        s_zero, s_ld, s_idx, s_zst, s_iota = sem("zero"), sem("ld"), sem("idx"), sem("zst"), sem("iota")
        s_id, s_fl, s_flT, s_tot, s_totp, s_sq, s_sqd, s_v = (
            sem("id"), sem("fl"), sem("flT"), sem("tot"), sem("totp"), sem("sq"), sem("sqd"), sem("v"))

        loads = [
            (K["whh"][:, :], A["w_hhT"]), (K["wih"][:, :], A["w_ihT"]), (K["wmsg"][:, :], A["w_msg"]),
            (K["w1"][:, :], A["w1T"]), (K["w2a"][:, :], A["w2T"][0:D, :]), (K["w2b"][:, :], A["w2T"][D:2 * D, :]),
            (K["att"][:, :], A["w_att"].partition_broadcast(P)), (K["batt"][:, :], A["b_att"].partition_broadcast(P)),
            (K["bmsg"][:, :], A["b_msg"].partition_broadcast(P)),
            (bt[:, 0:3], A["b_ih"]), (bt[:, 3:6], A["b_hh"]),
            (K["bn"][:, 0:1], A["gamma"]), (K["bn"][:, 1:2], A["beta"]),
            (K["b1"][:, :], A["b1"].partition_broadcast(P)), (K["ln_g"][:, :], A["ln_g"].partition_broadcast(P)),
            (K["ln_b"][:, :], A["ln_b"].partition_broadcast(P)), (K["b2"][:, :], A["b2"].partition_broadcast(P)),
            (K["g1w"][:, :], A["g1w"]), (s1w[:, :], A["s1w"]),
            (K["g2w"][:, :, :], A["g2w"].rearrange("(k p) n -> p k n", p=D)),
            (s2w[:, :, :], A["s2w"].rearrange("(k p) n -> p k n", p=D)),
            (K["g3w"][:, :, :], A["g3w"].rearrange("(k p) n -> p k n", p=D)),
            (s3w[:, :, :], A["s3w"].rearrange("(k p) n -> p k n", p=D)),
            (avs[:, 0, :], A["as1"].partition_broadcast(P)), (avs[:, 1, :], A["ad1"].partition_broadcast(P)),
            (avs2[:, 0, :], A["as2"].partition_broadcast(P)), (avs2[:, 1, :], A["ad2"].partition_broadcast(P)),
            (avs3[:, 0, :], A["as3"].partition_broadcast(P)), (avs3[:, 1, :], A["ad3"].partition_broadcast(P)),
            (K["g1b"][:, :], A["g1b"].partition_broadcast(P)), (sbias[0][:, :], A["s1b"].partition_broadcast(P)),
            (K["g2b"][:, :], A["g2b"].partition_broadcast(P)), (sbias[1][:, :], A["s2b"].partition_broadcast(P)),
            (K["g3b"][:, :], A["g3b"].partition_broadcast(P)), (sbias[2][:, :], A["s3b"].partition_broadcast(P)),
        ]
        zeros = []
        for name in ("agg0", "agg1"):
            flat = K[name].rearrange("(p r) d -> p (r d)", p=P)
            zeros += [(flat[:, c * ZC:(c + 1) * ZC], zero[:, :]) for c in range(12)]
        for name, w in (("pre2", D), ("pre3", HC), ("pre4", HC), ("pre5", D)):
            spare = K[name][NPAD:NROW, :].rearrange("(p r) d -> p (r d)", p=P)
            zeros.append((spare, zero[:, 0:RING * w]))

        with nc.Block() as block:

            @block.sync
            def _(sp):
                sp.dma_start(idx[:, 0, :], A["src"][0:EPAD].rearrange("(p t) -> p t", t=T)).then_inc(s_idx, 16)
                sp.dma_start(idx[:, 1, :], A["dst"][0:EPAD].rearrange("(p t) -> p t", t=T)).then_inc(s_idx, 16)
                sp.dma_start(nxtI[:, :], A["dst"][T:T + EPAD].rearrange("(p t) -> p t", t=T)).then_inc(s_idx, 16)
                for dst, src in loads:
                    sp.dma_start(dst, src).then_inc(s_ld, 16)
                sp.wait_ge(s_zero, 1)
                for dst, src in zeros:
                    sp.dma_start(dst, src).then_inc(s_zst, 16)
                sp.wait_ge(s_zst, 16 * len(zeros))

            @block.gpsimd
            def _(pool):
                pool.memset(zero[:, :], 0.0).then_inc(s_zero, 1)
                pool.memset(K["ident"][:, :], 0.0).then_inc(s_id, 1)
                pool.iota(dumI[:, :], pattern=[[0, ITERS], [P, RING]], base=NPAD, channel_multiplier=1).then_inc(s_iota, 1)
                pool.wait_ge(s_id, 1)
                pool.affine_select(out=K["ident"][:, :], in_=K["ident"][:, :], compare_op=ALU.not_equal, fill=1.0,
                                   base=0, pattern=[[-1, P]], channel_multiplier=1).then_inc(s_id, 1)

            @block.vector
            def _(v):
                step = Steps(v, s_v)
                v.memset(K["ones"][:, :], 1.0)
                v.memset(K["eps"][:, :], EPS)
                step(v.memset(K["edge_idx"][:, :, :], 0))
                v.wait_ge(s_idx, 48)
                v.tensor_copy(K["edge_idx"][:, 0:T, :], idx[:, :, :].rearrange("p s t -> p t s"))
                v.tensor_copy(dstF[:, :], idx[:, 1, :])
                step(v.tensor_copy(nxtF[:, :], nxtI[:, T - 1:T]))
                first, last = dstF[:, 0:1], dstF[:, T - 1:T]
                v.tensor_scalar(lb[:, :], K["ones"][:, :], last, None, ALU.mult)
                v.tensor_scalar(fb[:, :], K["ones"][:, :], first, None, ALU.mult).then_inc(s_fl, 1)
                v.memset(K["cont"][:, 0:1], 0.0)
                v.memset(K["cnext"][:, T - 1:T], 0.0)
                v.tensor_tensor(K["cont"][:, 1:T], dstF[:, 1:T], dstF[:, 0:T - 1], ALU.is_equal)
                step(v.tensor_tensor(K["cnext"][:, 0:T - 1], dstF[:, 1:T], dstF[:, 0:T - 1], ALU.is_equal))
                v.tensor_scalar(K["pcont"][:, :], K["cont"][:, :], -1.0, BIG, ALU.add, ALU.mult)
                v.tensor_scalar(K["pnext"][:, :], K["cnext"][:, :], -1.0, BIG, ALU.add, ALU.mult)
                v.wait_ge(s_iota, 1)
                step(v.tensor_copy(dum[:, :], dumI[:, :]))
                v.tensor_scalar(tmp2[:, :], K["cnext"][:, :], -1.0, 1.0, ALU.mult, ALU.add)
                step(v.tensor_tensor(tmp[:, :], dstF[:, :], dum[:, :], ALU.subtract))
                step(v.memset(tmp2[:, T - 1:T], 0.0))
                step(v.tensor_tensor(tmp2[:, :], tmp[:, :], tmp2[:, :], ALU.mult))
                step(v.tensor_tensor(K["scat_idx"][:, :], tmp2[:, :], dum[:, :], ALU.add))
                step(v.tensor_tensor(ts[:, 0:1], nxtF[:, :], last, ALU.not_equal))
                step(v.tensor_tensor(ts[:, 1:2], last, dum[:, 0:1], ALU.subtract))
                step(v.tensor_tensor(ts[:, 1:2], ts[:, 0:1], ts[:, 1:2], ALU.mult))
                step(v.tensor_tensor(K["fin_idx"][:, :], ts[:, 1:2], dum[:, 0:1], ALU.add))
                v.tensor_scalar(K["lead"][:, :], dstF[:, :], first, None, ALU.is_equal)
                step(v.tensor_scalar(tmp[:, :], dstF[:, :], last, None, ALU.is_equal))
                v.tensor_scalar(K["ptrail"][:, :], tmp[:, :], -1.0, BIG, ALU.add, ALU.mult)
                v.tensor_scalar(K["plead"][:, :], K["lead"][:, :], -1.0, BIG, ALU.add, ALU.mult)
                step(v.tensor_tensor(tmp2[:, :], tmp[:, :], K["lead"][:, :], ALU.mult))
                step(v.tensor_tensor(K["trail"][:, :], tmp[:, :], tmp2[:, :], ALU.subtract))
                step(v.tensor_tensor(tmp2[:, :], K["trail"][:, :], K["lead"][:, :], ALU.add))
                v.tensor_scalar(K["inner"][:, :], tmp2[:, :], -1.0, 1.0, ALU.mult, ALU.add)
                v.tensor_tensor(K["nosingle"][:, :], first, last, ALU.not_equal)
                v.wait_ge(s_flT, 1)
                for m, ps, s in (("LF", plast, first), ("FF", pfirst, first), ("LL", plast, last), ("FL", pfirst, last)):
                    ins = v.tensor_scalar(K[m][:, :], ps[:, 0:P], s, None, ALU.is_equal)
                step(ins)
                for m in ("LF", "FF", "LL", "FL"):
                    ins = v.tensor_scalar(K["p" + m][:, :], K[m][:, :], -1.0, BIG, ALU.add, ALU.mult)
                step(ins)
                v.tensor_tensor_scan(tmp[:, :], K["cont"][:, :], K["ones"][:, 0:1].to_broadcast([P, T]), 0.0, ALU.mult, ALU.add)
                step(v.tensor_tensor_scan(tmp2[:, ::-1], K["cnext"][:, ::-1], K["ones"][:, 0:1].to_broadcast([P, T]), 0.0, ALU.mult, ALU.add))
                v.tensor_copy(ts[:, 0:1], tmp[:, T - 1:T])
                step(v.tensor_tensor(ts[:, 1:2], tmp2[:, 0:1], K["nosingle"][:, :], ALU.mult))
                step(v.tensor_tensor(tmp[:, :], tmp[:, :], tmp2[:, :], ALU.add))
                step(v.tensor_scalar(tmp[:, :], tmp[:, :], -1.0, None, ALU.add))
                v.tensor_tensor(tmp[:, :], tmp[:, :], K["inner"][:, :], ALU.mult).then_inc(s_tot, 1)
                v.wait_ge(s_tot, 1)
                v.wait_ge(s_totp, 1)
                step(v.tensor_copy(ts[:, 0:2], ptot[:, :, 0]))
                step(v.scalar_tensor_tensor(tmp[:, :], K["lead"][:, :], ts[:, 0:1], tmp[:, :], ALU.mult, ALU.add))
                step(v.scalar_tensor_tensor(tmp[:, :], K["trail"][:, :], ts[:, 1:2], tmp[:, :], ALU.mult, ALU.add))
                v.tensor_scalar(tmp[:, :], tmp[:, :], 1.0, None, ALU.max).then_inc(s_sq, 1)
                v.wait_ge(s_sqd, 1)
                step(v.reciprocal(K["isq_in"][:, :], tmp2[:, :]))
                v.wait_ge(s_ld, 16 * len(loads))
                v.tensor_tensor(K["brz"][:, 0:2], bt[:, 0:2], bt[:, 3:5], ALU.add)
                v.tensor_copy(K["brz"][:, 2:3], bt[:, 2:3])
                v.tensor_copy(K["brz"][:, 3:4], bt[:, 5:6])
                v.tensor_tensor(K["g1b"][:, :], K["g1b"][:, :], sbias[0][:, :], ALU.add)
                v.tensor_tensor(K["g2b"][:, :], K["g2b"][:, :], sbias[1][:, :], ALU.add)
                v.tensor_tensor(K["g3b"][:, :], K["g3b"][:, :], sbias[2][:, :], ALU.add)
                v.tensor_tensor(K["g1d"][:, 0:HC], K["g1w"][:, :], s1w[:, :], ALU.add)
                step(v.tensor_tensor(K["g2d"][:, :, 0:HC], K["g2w"][:, :, :], s2w[:, :, :], ALU.add))
                for kb in range(2):
                    w = K["g3w"][:, kb, :]
                    step(v.tensor_reduce(prod[:, 0:D], w.rearrange("p (h c) -> p c h", h=H3), AX.X, ALU.add))
                    step(v.scalar_tensor_tensor(K["g3d"][:, kb, 0:D], prod[:, 0:D], 1.0 / H3, s3w[:, kb, :], ALU.mult, ALU.add))
                for w, a, h, o in ([(K["g1w"][:, :], avs, H1, K["g1d"][:, HC:])]
                                   + [(K["g2w"][:, kb, :], avs2, H1, K["g2d"][:, kb, HC:]) for kb in range(2)]
                                   + [(K["g3w"][:, kb, :], avs3, H3, K["g3d"][:, kb, D:]) for kb in range(2)]):
                    n = w.shape[1]
                    for side in range(2):
                        step(v.tensor_tensor(prod[:, 0:n], w, a[:, side, :], ALU.mult))
                        step(v.tensor_reduce(o[:, side * h:(side + 1) * h], prod[:, 0:n].rearrange("p (h c) -> p h c", h=h),
                                             AX.X, ALU.add))

            @block.tensor
            def _(pe):
                pe.wait_ge(s_id, 2)
                pe.wait_ge(s_fl, 1)
                pe.transpose(plast[:, 0:P], lb[:, :], K["ident"][:, :])
                pe.transpose(pfirst[:, 0:P], fb[:, :], K["ident"][:, :]).then_inc(s_flT, 1)
                pe.wait_ge(s_tot, 1)
                pe.matmul(ptot[:, 0, 0:1], K["FL"][:, :], ts[:, 0:1], start=True, stop=False)
                pe.matmul(ptot[:, 0, 0:1], K["FF"][:, :], ts[:, 1:2], start=False, stop=True)
                pe.matmul(ptot[:, 1, 0:1], K["LL"][:, :], ts[:, 0:1], start=True, stop=False)
                pe.matmul(ptot[:, 1, 0:1], K["LF"][:, :], ts[:, 1:2], start=False, stop=True).then_inc(s_totp, 1)

            @block.scalar
            def _(act):
                act.wait_ge(s_sq, 1)
                act.activation(tmp2[:, :], tmp[:, :], ACT.Sqrt).then_inc(s_sqd, 1)


def out_degree(nc, A, K):
    with phase(nc) as (ctx, sems):
        def sb(name, shape, dt=F32):
            return ctx.enter_context(nc.sbuf_tensor("deg_" + name, shape, dt))

        def sem(name):
            s = ctx.enter_context(nc.semaphore("deg_" + name))
            sems.append(s)
            return s

        HI = GROUPS * PER
        loI, hiI, lowI = sb("loI", [P, T], I32), sb("hiI", [P, T], I32), sb("lowI", [P, T], I32)
        lo, hi = sb("lo", [P, T]), sb("hi", [P, T])
        iotaI, iota = sb("iotaI", [P, HI], I32), sb("iota", [P, HI], F16)
        oh_lo, oh_hi = sb("oh_lo", [P, RING, P], F16), sb("oh_hi", [P, RING, HI], F16)
        count = ctx.enter_context(nc.psum_tensor("deg_count", [P, 512], F32))
        deg = sb("deg", [P, HI])
        s_iota, s_v, s_oh, s_mm, s_deg, s_sq = sem("iota"), sem("v"), sem("oh"), sem("mm"), sem("d"), sem("sq")
        with nc.Block() as block:

            @block.gpsimd
            def _(pool):
                pool.iota(iotaI[:, :], pattern=[[1, HI]], base=0, channel_multiplier=0).then_inc(s_iota, 1)

            @block.vector
            def _(v):
                step = Steps(v, s_v)
                src = K["edge_idx"][:, 0:T, 0]
                v.tensor_scalar(loI[:, :], src, 2, P - 1, ALU.logical_shift_right, ALU.bitwise_and)
                v.tensor_scalar(hiI[:, :], src, 9, 2, ALU.logical_shift_right, ALU.logical_shift_left)
                step(v.tensor_scalar(lowI[:, :], src, 3, None, ALU.bitwise_and))
                v.tensor_copy(lo[:, :], loI[:, :])
                v.tensor_tensor(hi[:, :], hiI[:, :], lowI[:, :], ALU.add)
                v.wait_ge(s_iota, 1)
                step(v.tensor_copy(iota[:, :], iotaI[:, :]))

                def one_hot(k, t):
                    v.tensor_scalar(oh_lo[:, k, :], iota[:, 0:P], lo[:, t], None, ALU.is_equal)
                    v.tensor_scalar(oh_hi[:, k, :], iota[:, :], hi[:, t], None, ALU.is_equal).then_inc(s_oh, 1)

                for k in range(RING):
                    one_hot(k, slice(k, k + 1))
                with v.Fori(1, ITERS) as i:
                    for k in range(RING):
                        v.wait_ge(s_mm, i * RING + (k + 1 - RING))
                        one_hot(k, bass.ds(i * RING + k, 1))
                v.wait_ge(s_mm, T)
                v.tensor_scalar(deg[:, :], count[:, 0:HI], 1.0, None, ALU.max).then_inc(s_deg, 1)
                v.wait_ge(s_sq, 1)
                v.reciprocal(K["isq_out"][:, :], deg[:, :]).then_inc(s_deg, 1)

            @block.tensor
            def _(pe):
                for k in range(RING):
                    pe.wait_ge(s_oh, k + 1)
                    pe.matmul(count[:, 0:HI], oh_lo[:, k, :], oh_hi[:, k, :], start=(k == 0), stop=False,
                              skip_group_check=True).then_inc(s_mm, 1)
                with pe.Fori(1, ITERS) as i:
                    for k in range(RING):
                        pe.wait_ge(s_oh, i * RING + (k + 1))
                        pe.matmul(count[:, 0:HI], oh_lo[:, k, :], oh_hi[:, k, :], start=False, stop=False,
                                  skip_group_check=True).then_inc(s_mm, 1)

            @block.scalar
            def _(act):
                act.wait_ge(s_deg, 1)
                act.activation(deg[:, :], deg[:, :], ACT.Sqrt).then_inc(s_sq, 1)


def gather(pool, dst, table, idx):
    return pool.indirect_dma_start(dst, None, table, bass.IndirectOffsetOnAxis(idx, 0))


def scatter_add(pool, table, idx, src):
    return pool.indirect_dma_start(table, bass.IndirectOffsetOnAxis(idx, 0), src, None, compute_op=ALU.add)


def edges(nc, K, tag, table, weight, target):
    W = D + 1 if tag == "e0" else D
    with phase(nc) as (ctx, sems):
        def sb(name, shape, dt=F32):
            return ctx.enter_context(nc.sbuf_tensor(f"{tag}_{name}", shape, dt))

        def sem(name):
            s = ctx.enter_context(nc.semaphore(f"{tag}_{name}"))
            sems.append(s)
            return s

        m = sb("m", [P, RING, W])
        prime = sb("prime", [P, RING, 4])
        slot, out_slot = sb("slot", [P, RING, 2], I32), sb("oslot", [P, RING, 1], I32)
        xs, acc = sb("xs", [P, RING, W]), sb("acc", [P, RING, W])
        accT, res = sb("accT", [D, RING, P]), sb("res", [P, RING, D])
        fin = sb("fin", [P, D])
        psT = ctx.enter_context(nc.psum_tensor(f"{tag}_psT", [P, 2, 512], F32))
        psY = ctx.enter_context(nc.psum_tensor(f"{tag}_psY", [P, RING, 512], F32))
        psF = ctx.enter_context(nc.psum_tensor(f"{tag}_psF", [P, 512], F32))
        s_src = [K["dma_sem"](f"{tag}_src{k}") for k in range(RING)]
        s_put = [K["dma_sem"](f"{tag}_put{k}") for k in range(RING)]
        s_slot = sem("slot")
        s_walk = sem("walk")
        s_turn, s_mm = sem("turn"), sem("mm")
        s_evac = sem("evac")
        s_oslot, s_res = sem("oslot"), sem("res")
        s_fin, s_finp, s_go = sem("fin"), sem("finp"), sem("go")
        s_finput = K["dma_sem"](f"{tag}_finput")
        s_v, s_logit, s_att = sem("v"), sem("logit"), sem("att_s")
        if tag == "e0":
            s_dst = [K["dma_sem"](f"{tag}_dst{k}") for k in range(RING)]
            xd, junk, junk2 = sb("xd", [P, RING, D]), sb("junk", [P, RING, D]), sb("junk2", [P, RING, D])
            logit, att = sb("logit", [P, 2, RING]), sb("attv", [P, RING])
        with nc.Block() as block:

            @block.gpsimd
            def _(pool):
                def fetch(i, k):
                    pool.wait_ge(s_slot, i * RING + (k + 1))
                    pool.sem_inc(s_go, 1)
                    if tag == "e0":
                        gather(pool, xd[:, k, :], table, slot[:, k, 1:2]).then_inc(s_dst[k], 16)
                    gather(pool, xs[:, k, 0:D], table, slot[:, k, 0:1]).then_inc(s_src[k], 16)

                def put(i, k):
                    pool.wait_ge(s_oslot, i * RING + (k + 1))
                    pool.wait_ge(s_res, i * RING + (k + 1 + RING))
                    pool.sem_inc(s_go, 1)
                    scatter_add(pool, target, out_slot[:, k, :], res[:, k, :]).then_inc(s_put[k], 16)

                for k in range(RING):
                    pool.dma_start(prime[:, k, :], K["x"][0:P, 0:4]).then_inc(s_put[k], 16)
                for k in range(RING):
                    fetch(0, k)
                with pool.Fori(1, ITERS) as i:
                    for k in range(RING):
                        fetch(i, k)
                        put(i - 1, k)
                for k in range(RING):
                    put(ITERS - 1, k)
                for k in range(RING):
                    pool.wait_ge(s_put[k], 16 * (ITERS + 1))
                pool.wait_ge(s_fin, 1)
                scatter_add(pool, target, K["fin_idx"][:, :], fin[:, :]).then_inc(s_finput, 16)
                pool.wait_ge(s_finput, 16)

            @block.vector
            def _(v):
                v.tensor_copy(slot[:, :, :], K["edge_idx"][:, 0:RING, :]).then_inc(s_slot, RING)
                if tag == "e0":
                    v.memset(xs[:, :, D:W], 1.0)
                v.memset(acc[:, RING - 1, :], 0.0).then_inc(s_walk, RING)
                step = Steps(v, s_v)
                with v.Fori(0, ITERS) as i:
                    if tag == "e0":
                        step.loop(i, 1 + RING)
                        for k in range(RING):
                            v.wait_ge(s_dst[k], 16 * i + 16)
                            v.tensor_tensor_reduce(junk[:, k, :], xd[:, k, :], K["att"][:, D:2 * D], 1.0, 0.0, ALU.mult, ALU.add,
                                                   logit[:, 1, k:k + 1])
                            v.wait_ge(s_src[k], 16 * i + 16)
                            last = v.tensor_tensor_reduce(junk2[:, k, :], xs[:, k, 0:D], K["att"][:, 0:D], 1.0, 0.0, ALU.mult,
                                                          ALU.add, logit[:, 0, k:k + 1])
                        step(last)
                        v.tensor_tensor(logit[:, 0, :], logit[:, 0, :], logit[:, 1, :], ALU.add).then_inc(s_logit, 1)
                        v.wait_ge(s_att, i + 1)
                    for k in range(RING):
                        message = m[:, k, :] if tag == "e0" else xs[:, k, :]
                        if tag == "e0":
                            step(v.tensor_scalar(message, xs[:, k, :], att[:, k:k + 1], None, ALU.mult))
                        else:
                            v.wait_ge(s_src[k], 16 * i + 16)
                        v.wait_ge(s_turn, i * RING + (k + 1))
                        v.wait_ge(s_walk, i * RING + (k + RING))
                        v.scalar_tensor_tensor(acc[:, k, :], acc[:, (k - 1) % RING, :], K["cont"][:, bass.ds(i * RING + k, 1)],
                                               message, ALU.mult, ALU.add).then_inc(s_walk, 1)
                        v.tensor_copy(slot[:, k, :], K["edge_idx"][:, bass.ds(i * RING + (k + RING), 1), :].rearrange("p a b -> p (a b)")).then_inc(s_slot, 1)
                    if tag == "e0":
                        for k in range(RING):
                            v.wait_ge(s_mm, i * RING + (k + 1 + RING))
                            v.wait_ge(s_put[k], 16 * i + 16)
                            v.scalar_tensor_tensor(res[:, k, :], K["bmsg"][:, :], acc[:, k, D:W], psY[:, k, 0:D],
                                                   ALU.mult, ALU.add).then_inc(s_res, 1)
                if tag == "e0":
                    step.done(ITERS)
                v.wait_ge(s_finp, 1)
                v.tensor_copy(fin[:, :], psF[:, 0:D]).then_inc(s_fin, 1)

            @block.tensor
            def _(pe):
                pe.sem_inc(s_turn, RING)
                pe.sem_inc(s_mm, RING)
                with pe.Fori(0, ITERS) as i:
                    for k in range(RING):
                        pe.wait_ge(s_walk, i * RING + (k + 1 + RING))
                        pe.wait_ge(s_evac, i * RING + (k + 1))
                        pe.transpose(psT[:, k % 2, 0:P], acc[:, k, 0:D], K["ident"][:, :]).then_inc(s_turn, 1)
                        pe.wait_ge(s_evac, i * RING + (k + 3))
                        pe.wait_ge(s_res, i * RING + (k + 1))
                        pe.matmul(psY[:, k, 0:D], accT[:, k, :], weight[:, :], start=True, stop=True).then_inc(s_mm, 1)
                pe.wait_ge(s_res, T + RING)
                pe.matmul(psF[:, 0:D], K["LL"][:, :], res[:, RING - 1, :], start=True, stop=True).then_inc(s_finp, 1)

            @block.scalar
            def _(act):
                act.sem_inc(s_evac, 2)
                act.sem_inc(s_res, RING)
                with act.Fori(0, ITERS) as i:
                    if tag == "e0":
                        act.wait_ge(s_logit, i + 1)
                        act.activation(att[:, :], logit[:, 0, :], ACT.Sigmoid, bias=K["batt"][:, 0:1]).then_inc(s_att, 1)
                    for k in range(RING):
                        act.wait_ge(s_turn, i * RING + (k + 1 + RING))
                        act.wait_ge(s_mm, i * RING + (k + 1))
                        act.copy(accT[:, k, :], psT[:, k % 2, 0:P]).then_inc(s_evac, 1)
                        act.wait_ge(s_put[k], 16 * i + 16)
                        act.copy(out_slot[:, k, :], K["scat_idx"][:, bass.ds(i * RING + k, 1)]).then_inc(s_oslot, 1)
                        if tag != "e0":
                            act.wait_ge(s_mm, i * RING + (k + 1 + RING))
                            if tag == "e1":
                                act.copy(res[:, k, :], psY[:, k, 0:D]).then_inc(s_res, 1)
                            else:
                                act.activation(res[:, k, :], psY[:, k, 0:D], ACT.Copy,
                                               scale=K["isq_in"][:, bass.ds(i * RING + k, 1)]).then_inc(s_res, 1)


def gru(nc, A, K):
    with phase(nc) as (ctx, sems):
        def sb(name, shape, dt=F32):
            return ctx.enter_context(nc.sbuf_tensor("gru_" + name, shape, dt))

        def ps(name):
            return ctx.enter_context(nc.psum_tensor("gru_" + name, [P, GROUP], F32))

        def sem(name):
            s = ctx.enter_context(nc.semaphore("gru_" + name))
            sems.append(s)
            return s

        x, agg = sb("x", [P, 2, PER, D]), sb("agg", [P, 2, PER, D])
        xT, aT = sb("xT", [D, 2, GROUP]), sb("aT", [D, 2, GROUP])
        r, z, n, t, h = (sb(c, [D, 2, GROUP]) for c in "rznth")
        pxT, paT, pr, pz, pi, ph = (ps(c) for c in ("pxT", "paT", "pr", "pz", "pi", "ph"))
        mv = sb("mv", [D, 2])
        sd = sb("sd", [D, 2])
        s_ld = [sem("ld0"), sem("ld1")]
        s_st = [sem("st0"), sem("st1")]
        s_turn = sem("turn")
        s_xT, s_aT = sem("xT"), sem("aT")
        s_mm = sem("mm")
        s_r, s_z, s_n = sem("r"), sem("z"), sem("n")
        s_t = sem("t")
        s_h = sem("h")
        s_v, s_var, s_sd = sem("v"), sem("var"), sem("sd")
        with nc.Block() as block:
            xg, ag = grouped(A["x"]), grouped(K["agg0"])
            hg = K["hT"].rearrange("d (g n) -> g d n", g=GROUPS)

            @block.sync
            def _(sp):
                def load(g, b):
                    sp.dma_start(x[:, b].rearrange("p j d -> p (j d)"), xg[g]).then_inc(s_ld[b], 16)
                    sp.dma_start(agg[:, b].rearrange("p j d -> p (j d)"), ag[g]).then_inc(s_ld[b], 16)

                def store(g, b):
                    sp.dma_start(hg[g], h[:, b]).then_inc(s_st[b], 16)

                for b in range(2):
                    sp.sem_inc(s_st[b], 16)
                    load(b, b)
                with sp.Fori(1, PAIRS) as i:
                    for b in range(2):
                        sp.wait_ge(s_turn, 2 * i + (b - 1))
                        load(2 * i + b, b)
                        sp.wait_ge(s_h, 2 * i + (b + 1))
                        store(2 * i + (b - 2), b)
                for b in range(2):
                    sp.wait_ge(s_h, GROUPS + 1 + b)
                    store(GROUPS - 2 + b, b)
                for b in range(2):
                    sp.wait_ge(s_st[b], 16 * (PAIRS + 1))

            @block.tensor
            def _(pe):
                with pe.Fori(0, PAIRS) as i:
                    for b in range(2):
                        pe.wait_ge(s_ld[b], 32 * i + 32)
                        pe.wait_ge(s_xT, 2 * i + (b + 1))
                        pe.wait_ge(s_aT, 2 * i + (b + 1))
                        for j in range(PER):
                            pe.transpose(pxT[:, j * P:(j + 1) * P], x[:, b, j, :], K["ident"][:, :])
                            last = pe.transpose(paT[:, j * P:(j + 1) * P], agg[:, b, j, :], K["ident"][:, :])
                        last.then_inc(s_turn, 1)
                        pe.wait_ge(s_xT, 2 * i + (b + 2))
                        pe.wait_ge(s_aT, 2 * i + (b + 2))
                        pe.wait_ge(s_z, 2 * i + (b + 1))
                        pe.wait_ge(s_t, 2 * i + (b + 1))
                        for c, p in ((0, pr), (1, pz)):
                            pe.matmul(p[:, :], K["wih"][:, c * D:(c + 1) * D], aT[:, b, :], start=True, stop=False)
                            pe.matmul(p[:, :], K["whh"][:, c * D:(c + 1) * D], xT[:, b, :], start=False, stop=True)
                        pe.matmul(pi[:, :], K["wih"][:, 2 * D:3 * D], aT[:, b, :], start=True, stop=True)
                        pe.matmul(ph[:, :], K["whh"][:, 2 * D:3 * D], xT[:, b, :], start=True, stop=True).then_inc(s_mm, 1)

            @block.scalar
            def _(act):
                act.sem_inc(s_xT, 1)
                act.sem_inc(s_z, 1)
                with act.Fori(0, PAIRS) as i:
                    for b in range(2):
                        act.wait_ge(s_turn, 2 * i + (b + 1))
                        act.wait_ge(s_h, 2 * i + (b + 1))
                        act.copy(xT[:, b, :], pxT[:, :]).then_inc(s_xT, 1)
                        act.wait_ge(s_mm, 2 * i + (b + 1))
                        act.activation(r[:, b, :], pr[:, :], ACT.Sigmoid, bias=K["brz"][:, 0:1]).then_inc(s_r, 1)
                        act.activation(z[:, b, :], pz[:, :], ACT.Sigmoid, bias=K["brz"][:, 1:2]).then_inc(s_z, 1)
                        act.wait_ge(s_t, 2 * i + (b + 2))
                        act.activation(n[:, b, :], t[:, b, :], ACT.Tanh, bias=K["brz"][:, 2:3]).then_inc(s_n, 1)
                act.wait_ge(s_var, 1)
                act.activation(sd[:, 0:1], mv[:, 1:2], ACT.Sqrt, bias=K["eps"][:, 0:1]).then_inc(s_sd, 1)

            @block.vector
            def _(v):
                v.sem_inc(s_aT, 1)
                v.sem_inc(s_t, 1)
                v.sem_inc(s_h, 2)
                step = Steps(v, s_v)
                with v.Fori(0, PAIRS) as i:
                    step.loop(i, 6)
                    for b in range(2):
                        v.wait_ge(s_turn, 2 * i + (b + 1))
                        v.tensor_copy(aT[:, b, :], paT[:, :]).then_inc(s_aT, 1)
                        v.wait_ge(s_mm, 2 * i + (b + 1))
                        v.wait_ge(s_r, 2 * i + (b + 1))
                        step(v.scalar_tensor_tensor(t[:, b, :], ph[:, :], K["brz"][:, 3:4], r[:, b, :], ALU.add, ALU.mult))
                        v.tensor_tensor(t[:, b, :], t[:, b, :], pi[:, :], ALU.add).then_inc(s_t, 1)
                        v.wait_ge(s_n, 2 * i + (b + 1))
                        step(v.tensor_tensor(r[:, b, :], xT[:, b, :], n[:, b, :], ALU.subtract))
                        v.wait_ge(s_z, 2 * i + (b + 2))
                        step(v.tensor_tensor(r[:, b, :], r[:, b, :], z[:, b, :], ALU.mult))
                        v.wait_ge(s_st[b], 16 * i + 16)
                        v.tensor_tensor(h[:, b, :], r[:, b, :], n[:, b, :], ALU.add).then_inc(s_h, 1)
                        v.wait_ge(s_h, 2 * i + (b + 3))
                        v.bn_stats(K["stats"][:, bass.ds(2 * i + b, 1), :].rearrange("p a b -> p (a b)"), h[:, b, :])
                step.done(PAIRS)
                v.drain()
                valid = h[:, 1, :].rearrange("d (j p) -> d j p", j=PER)[:, :, 0:LAST_VALID]
                step(v.bn_stats(K["stats"][:, GROUPS - 1, :], valid))
                v.bn_aggr(mv[:, :], K["stats"][:, :, :].rearrange("p a b -> p (a b)")).then_inc(s_var, 1)
                v.wait_ge(s_sd, 1)
                step(v.reciprocal(sd[:, 1:2], sd[:, 0:1]))
                step(v.tensor_tensor(K["bnss"][:, 0:1], sd[:, 1:2], K["bn"][:, 0:1], ALU.mult))
                step(v.tensor_tensor(mv[:, 0:1], mv[:, 0:1], K["bnss"][:, 0:1], ALU.mult))
                step(v.tensor_tensor(K["bnss"][:, 1:2], K["bn"][:, 1:2], mv[:, 0:1], ALU.subtract))


class Norm:

    def __init__(self, sb, sem, tag):
        self.st, self.mv = sb(tag + "st", [P, PER, 6]), sb(tag + "mv", [P, PER, 2])
        self.sd, self.rs = sb(tag + "sd", [P, PER]), sb(tag + "rs", [P, PER])
        self.s_mv, self.s_sd, self.s_gate = sem(tag + "mv"), sem(tag + "sd"), sem(tag + "gate")

    def stats(self, v, step, u):
        for j in range(PER):
            last = v.bn_stats(self.st[:, j, :], u[:, j, :])
        step(last)
        v.sem_inc(self.s_gate, 1)
        for j in range(PER):
            last = v.bn_aggr(self.mv[:, j, :], self.st[:, j, :])
        last.then_inc(self.s_mv, 1)

    def root(self, act, K, n):
        act.wait_ge(self.s_mv, n)
        act.activation(self.sd[:, :], self.mv[:, :, 1], ACT.Sqrt, bias=K["eps"][:, 0:1]).then_inc(self.s_sd, 1)

    def rows(self, v, step, n, out, u):
        v.wait_ge(self.s_sd, n)
        step(v.reciprocal(self.rs[:, :], self.sd[:, :]))
        for j in range(PER):
            last = v.tensor_scalar(out[:, j, :], u[:, j, :], self.mv[:, j, 0:1], self.rs[:, j:j + 1],
                                   ALU.subtract, ALU.mult)
        return last


def stream(sp, s_ld, s_st, used, done, load, store):
    for b in range(2):
        sp.sem_inc(s_st[b], 16 * len(store))
        for f in load:
            f(b, b).then_inc(s_ld[b], 16)
    with sp.Fori(1, PAIRS) as i:
        for b in range(2):
            sp.wait_ge(used[0], 2 * i + (b - 1 + used[1]))
            for f in load:
                f(2 * i + b, b).then_inc(s_ld[b], 16)
            for s, start in done:
                sp.wait_ge(s, 2 * i + (b - 1 + start))
            for f in store:
                f(2 * i + (b - 2), b).then_inc(s_st[b], 16)
    for b in range(2):
        for s, start in done:
            sp.wait_ge(s, GROUPS - 1 + b + start)
        for f in store:
            f(GROUPS - 2 + b, b).then_inc(s_st[b], 16)
    for b in range(2):
        sp.wait_ge(s_st[b], 16 * len(store) * (PAIRS + 1))


def flat(ap):
    return ap.rearrange("p j d -> p (j d)")


def rows4(ap):
    return ap.unsqueeze(1).to_broadcast([P, PER, ap.shape[1]])


def norm0(nc, A, K):
    with phase(nc) as (ctx, sems):
        def sb(name, shape, dt=F32):
            return ctx.enter_context(nc.sbuf_tensor("n0_" + name, shape, dt))

        def sem(name):
            s = ctx.enter_context(nc.semaphore("n0_" + name))
            sems.append(s)
            return s

        x, hT, bT = sb("x", [P, 2, PER, D]), sb("hT", [D, 2, GROUP]), sb("bT", [D, 2, GROUP])
        u, y = sb("u", [P, 2, PER, D]), sb("y", [P, 2, PER, D])
        pb = ctx.enter_context(nc.psum_tensor("n0_pb", [P, 2, PER, D], F32))
        norm = Norm(sb, sem, "")
        s_ld, s_st = [sem("ld0"), sem("ld1")], [sem("st0"), sem("st1")]
        s_bT = sem("bT")
        s_turn = sem("turn")
        s_sum = sem("sum")
        s_done, s_v = sem("done"), sem("v")
        with nc.Block() as block:
            xg, yg = grouped(A["x"]), grouped(K["x1"])
            hg = K["hT"].rearrange("d (g n) -> g d n", g=GROUPS)

            @block.sync
            def _(sp):
                stream(sp, s_ld, s_st, (s_sum, 2), [(s_done, 0)],
                       [lambda g, b: sp.dma_start(flat(x[:, b]), xg[g]), lambda g, b: sp.dma_start(hT[:, b], hg[g])],
                       [lambda g, b: sp.dma_start(yg[g], flat(y[:, b]))])

            @block.scalar
            def _(act):
                with act.Fori(0, PAIRS) as i:
                    for b in range(2):
                        act.wait_ge(s_ld[b], 32 * i + 32)
                        act.wait_ge(s_turn, 2 * i + (b + 1))
                        act.activation(bT[:, b, :], hT[:, b, :], ACT.Identity, scale=K["bnss"][:, 0:1],
                                       bias=K["bnss"][:, 1:2]).then_inc(s_bT, 1)
                        norm.root(act, K, 2 * i + (b + 1))

            @block.tensor
            def _(pe):
                pe.sem_inc(s_turn, 2)
                with pe.Fori(0, PAIRS) as i:
                    for b in range(2):
                        pe.wait_ge(s_bT, 2 * i + (b + 1))
                        pe.wait_ge(s_sum, 2 * i + (b + 1))
                        for j in range(PER):
                            last = pe.transpose(pb[:, b, j, :], bT[:, b, j * P:(j + 1) * P], K["ident"][:, :])
                        last.then_inc(s_turn, 1)

            @block.vector
            def _(v):
                v.sem_inc(s_sum, 2)
                step = Steps(v, s_v)
                with v.Fori(0, PAIRS) as i:
                    step.loop(i, 4)
                    for b in range(2):
                        v.wait_ge(s_ld[b], 32 * i + 32)
                        v.wait_ge(s_turn, 2 * i + (b + 3))
                        v.tensor_tensor(u[:, b], pb[:, b], x[:, b], ALU.add).then_inc(s_sum, 1)
                        v.wait_ge(s_sum, 2 * i + (b + 3))
                        norm.stats(v, step, u[:, b])
                        v.wait_ge(s_st[b], 16 * i + 16)
                        norm.rows(v, step, 2 * i + (b + 1), y[:, b], u[:, b]).then_inc(s_done, 1)
                step.done(PAIRS)


def dense1(nc, K):
    with phase(nc) as (ctx, sems):
        def sb(name, shape, dt=F32):
            return ctx.enter_context(nc.sbuf_tensor("d1_" + name, shape, dt))

        def sem(name):
            s = ctx.enter_context(nc.semaphore("d1_" + name))
            sems.append(s)
            return s

        x, agg = sb("x", [P, 2, PER, D]), sb("agg", [P, 2, PER, D])
        u, x2, w = sb("u", [P, 2, PER, D]), sb("x2", [P, 2, PER, D]), sb("w", [P, 2, PER, D])
        hn, msg, hT = sb("hn", [P, 2, PER, D]), sb("msg", [P, 2, PER, D]), sb("hT", [D, 2, GROUP])
        prod, pre = sb("prod", [P, 2, PER, D]), sb("pre", [P, 2, PER, D])
        pT = ctx.enter_context(nc.psum_tensor("d1_pT", [P, 2, GROUP], F32))
        pP = ctx.enter_context(nc.psum_tensor("d1_pP", [P, 2, PER, D], F32))
        na, nb = Norm(sb, sem, "a"), Norm(sb, sem, "b")
        s_ld, s_st = [sem("ld0"), sem("ld1")], [sem("st0"), sem("st1")]
        s_used = sem("used")
        s_w = sem("w")
        s_hn = sem("hn")
        s_msg = sem("msg")
        s_turn, s_hT = sem("turn"), sem("hT")
        s_mm, s_prod = sem("mm"), sem("prod")
        s_done = sem("done")
        s_v, s_g = sem("v"), sem("g")
        with nc.Block() as block:
            xg, ag, mg, pg = (grouped(K[t]) for t in ("x1", "agg1", "msg", "pre2"))

            @block.sync
            def _(sp):
                stream(sp, s_ld, s_st, (s_used, 0), [(s_msg, 2), (s_done, 2)],
                       [lambda g, b: sp.dma_start(flat(x[:, b]), xg[g]), lambda g, b: sp.dma_start(flat(agg[:, b]), ag[g])],
                       [lambda g, b: sp.dma_start(mg[g], flat(msg[:, b])), lambda g, b: sp.dma_start(pg[g], flat(pre[:, b]))])

            @block.vector
            def _(v):
                step = Steps(v, s_v)
                v.sem_inc(s_msg, 2)
                with v.Fori(0, PAIRS) as i:
                    step.loop(i, 14)
                    for b in range(2):
                        v.wait_ge(s_ld[b], 32 * i + 32)
                        step(v.tensor_tensor(u[:, b], agg[:, b], rows4(K["b1"][:, :]), ALU.add))
                        step(v.scalar_tensor_tensor(flat(u[:, b]), flat(u[:, b]), 0.0, flat(x[:, b]), ALU.max, ALU.add))
                        v.sem_inc(s_used, 1)
                        na.stats(v, step, u[:, b])
                        v.wait_ge(s_done, 2 * i + (b + 1))
                        step(na.rows(v, step, 2 * i + (b + 1), x2[:, b], u[:, b]))
                        nb.stats(v, step, x2[:, b])
                        nb.rows(v, step, 2 * i + (b + 1), w[:, b], x2[:, b]).then_inc(s_w, 1)
                        v.wait_ge(s_hn, 2 * i + (b + 1))
                        v.wait_ge(s_st[b], 32 * i + 32)
                        for j in range(PER):
                            last = v.tensor_scalar(msg[:, b, j, :], hn[:, b, j, :],
                                                   K["isq_out"][:, bass.ds(8 * i + (4 * b + j), 1)], None, ALU.mult)
                        last.then_inc(s_msg, 1)
                step.done(PAIRS)

            @block.gpsimd
            def _(g):
                g.sem_inc(s_done, 2)
                step = Steps(g, s_g)
                with g.Fori(0, PAIRS) as i:
                    step.loop(i, 4)
                    for b in range(2):
                        g.wait_ge(s_w, 2 * i + (b + 1))
                        step(g.tensor_tensor(w[:, b], w[:, b], rows4(K["ln_g"][:, :]), ALU.mult))
                        g.wait_ge(s_turn, 2 * i + (b + 1))
                        g.wait_ge(s_msg, 2 * i + (b + 1))
                        g.tensor_tensor(hn[:, b], w[:, b], rows4(K["ln_b"][:, :]), ALU.add).then_inc(s_hn, 1)
                        step(g.tensor_tensor(x2[:, b], x2[:, b], rows4(K["b2"][:, :]), ALU.add))
                        g.wait_ge(s_prod, 2 * i + (b + 3))
                        g.wait_ge(s_st[b], 32 * i + 32)
                        g.tensor_tensor(pre[:, b], prod[:, b], x2[:, b], ALU.add).then_inc(s_done, 1)
                step.done(PAIRS)

            @block.tensor
            def _(pe):
                pe.sem_inc(s_turn, 2)
                pe.sem_inc(s_mm, 2)
                with pe.Fori(0, PAIRS) as i:
                    for b in range(2):
                        pe.wait_ge(s_hn, 2 * i + (b + 1))
                        pe.wait_ge(s_hT, 2 * i + (b + 1))
                        for j in range(PER):
                            last = pe.transpose(pT[:, b, j * P:(j + 1) * P], hn[:, b, j, :], K["ident"][:, :])
                        last.then_inc(s_turn, 1)
                        pe.wait_ge(s_hT, 2 * i + (b + 3))
                        pe.wait_ge(s_prod, 2 * i + (b + 1))
                        for j in range(PER):
                            last = pe.matmul(pP[:, b, j, :], hT[:, b, j * P:(j + 1) * P], K["w2a"][:, :], start=True, stop=True)
                        last.then_inc(s_mm, 1)

            @block.scalar
            def _(act):
                act.sem_inc(s_hT, 2)
                act.sem_inc(s_prod, 2)
                with act.Fori(0, PAIRS) as i:
                    for b in range(2):
                        na.root(act, K, 2 * i + (b + 1))
                        nb.root(act, K, 2 * i + (b + 1))
                        act.wait_ge(s_turn, 2 * i + (b + 3))
                        act.wait_ge(s_mm, 2 * i + (b + 1))
                        act.copy(hT[:, b, :], pT[:, b, :]).then_inc(s_hT, 1)
                        act.wait_ge(s_mm, 2 * i + (b + 3))
                        act.wait_ge(s_done, 2 * i + (b + 1))
                        act.copy(prod[:, b], pP[:, b]).then_inc(s_prod, 1)


def dense2(nc, K):
    W = HC + 2 * H1
    with phase(nc) as (ctx, sems):
        def sb(name, shape, dt=F32):
            return ctx.enter_context(nc.sbuf_tensor("d2_" + name, shape, dt))

        def sem(name):
            s = ctx.enter_context(nc.semaphore("d2_" + name))
            sems.append(s)
            return s

        u, x3, xT = sb("u", [P, 2, PER, D]), sb("x3", [P, 2, PER, D]), sb("xT", [D, 2, GROUP])
        pre, sc = sb("pre", [P, 2, PER, HC]), sb("sc", [P, 2, PER, 2 * H1])
        pT = ctx.enter_context(nc.psum_tensor("d2_pT", [P, 2, GROUP], F32))
        pP = ctx.enter_context(nc.psum_tensor("d2_pP", [P, PER, 512], F32))
        norm = Norm(sb, sem, "")
        s_ld, s_st = [sem("ld0"), sem("ld1")], [sem("st0"), sem("st1")]
        s_x3 = sem("x3")
        s_turn, s_xT, s_mm = sem("turn"), sem("xT"), sem("mm")
        s_pre = sem("pre")
        s_v = sem("v")
        with nc.Block() as block:
            pg, xg, og, sg = (grouped(K[t]) for t in ("pre2", "x3", "pre3", "sc3"))

            @block.sync
            def _(sp):
                stream(sp, s_ld, s_st, (s_x3, 0), [(s_pre, 1)],
                           [lambda g, b: sp.dma_start(flat(u[:, b]), pg[g])],
                           [lambda g, b: sp.dma_start(xg[g], flat(x3[:, b])), lambda g, b: sp.dma_start(og[g], flat(pre[:, b])),
                            lambda g, b: sp.dma_start(sg[g], flat(sc[:, b]))])

            @block.vector
            def _(v):
                v.sem_inc(s_pre, 1)
                step = Steps(v, s_v)
                with v.Fori(0, PAIRS) as i:
                    step.loop(i, 4)
                    for b in range(2):
                        v.wait_ge(s_ld[b], 16 * i + 16)
                        norm.stats(v, step, u[:, b])
                        v.wait_ge(s_st[b], 48 * i + 48)
                        norm.rows(v, step, 2 * i + (b + 1), x3[:, b], u[:, b]).then_inc(s_x3, 1)
                        v.wait_ge(s_mm, 2 * i + (b + 1))
                        v.tensor_copy(sc[:, b], pP[:, :, HC:W])
                        v.tensor_tensor(pre[:, b], pP[:, :, 0:HC], rows4(K["g1b"][:, :]), ALU.add).then_inc(s_pre, 1)
                step.done(PAIRS)

            @block.tensor
            def _(pe):
                with pe.Fori(0, PAIRS) as i:
                    for b in range(2):
                        pe.wait_ge(s_x3, 2 * i + (b + 1))
                        pe.wait_ge(s_xT, 2 * i + (b + 1))
                        for j in range(PER):
                            last = pe.transpose(pT[:, b, j * P:(j + 1) * P], x3[:, b, j, :], K["ident"][:, :])
                        last.then_inc(s_turn, 1)
                        pe.wait_ge(s_xT, 2 * i + (b + 3))
                        pe.wait_ge(s_pre, 2 * i + (b + 1))
                        for j in range(PER):
                            last = pe.matmul(pP[:, j, 0:W], xT[:, b, j * P:(j + 1) * P], K["g1d"][:, :], start=True, stop=True)
                        last.then_inc(s_mm, 1)

            @block.scalar
            def _(act):
                act.sem_inc(s_xT, 2)
                with act.Fori(0, PAIRS) as i:
                    for b in range(2):
                        norm.root(act, K, 2 * i + (b + 1))
                        act.wait_ge(s_turn, 2 * i + (b + 1))
                        act.copy(xT[:, b, :], pT[:, b, :]).then_inc(s_xT, 1)


def edge_scores(nc, K, n, H, scores, alpha):
    with phase(nc) as (ctx, sems):
        def sb(name, shape, dt=F32):
            return ctx.enter_context(nc.sbuf_tensor(f"es{n}_{name}", shape, dt))

        def sem(name):
            s = ctx.enter_context(nc.semaphore(f"es{n}_{name}"))
            sems.append(s)
            return s

        slot = sb("slot", [P, RING, 2], I32)
        got = sb("got", [P, RING, 2, 2 * H])
        rows = sb("rows", [P, T, 2, 2 * H])
        s, sf, F, B, M, junk = (sb(c, [P, H, T]) for c in ("s", "self", "F", "B", "M", "junk"))
        bc = sb("bc", [P, 2 * H, P])
        ends = sb("ends", [P, 2, H])
        mx = sb("mx", [P, 4, H])
        pb = ctx.enter_context(nc.psum_tensor(f"es{n}_pb", [P, 2 * H, P], F32))
        pt = ctx.enter_context(nc.psum_tensor(f"es{n}_pt", [P, 2, 512], F32))
        s_got = [K["dma_sem"](f"es{n}_got{k}") for k in range(RING)]
        s_slot, s_v, s_go, s_bc, s_pb, s_ends, s_pt = (sem("slot"), sem("v"), sem("go"), sem("bc"), sem("pb"),
                                                       sem("ends"), sem("pt"))
        s_arg, s_exp = sem("arg"), sem("exp")
        with nc.Block() as block:

            @block.gpsimd
            def _(pool):
                def fetch(i, k):
                    pool.wait_ge(s_slot, i * RING + (k + 1))
                    pool.sem_inc(s_go, 1)
                    for side in range(2):
                        gather(pool, got[:, k, side, :], scores[:, :], slot[:, k, side:side + 1]).then_inc(s_got[k], 16)

                for k in range(RING):
                    fetch(0, k)
                with pool.Fori(1, ITERS) as i:
                    for k in range(RING):
                        fetch(i, k)

            @block.vector
            def _(v):
                v.tensor_copy(slot[:, :, :], K["edge_idx"][:, 0:RING, :]).then_inc(s_slot, RING)
                with v.Fori(0, ITERS) as i:
                    for k in range(RING):
                        v.wait_ge(s_got[k], 32 * i + 32)
                        v.tensor_copy(rows[:, bass.ds(i * RING + k, 1), :, :].rearrange("p t s h -> p (t s h)"),
                                      got[:, k, :, :].rearrange("p s h -> p (s h)"))
                        v.tensor_copy(slot[:, k, :], K["edge_idx"][:, bass.ds(i * RING + (k + RING), 1), :].rearrange("p a b -> p (a b)")).then_inc(s_slot, 1)
                v.wait_ge(s_slot, T + RING)
                step = Steps(v, s_v)

                def part(side, which):
                    return rows[:, :, side, which * H:(which + 1) * H].rearrange("p t h -> p h t")

                v.tensor_tensor(s[:, :, :], part(0, 0), part(1, 1), ALU.add)
                step(v.tensor_tensor(sf[:, :, :], part(1, 0), part(1, 1), ALU.add))
                for a in (s, sf):
                    step(v.scalar_tensor_tensor(a[:, :, :], a[:, :, :], 0.2, a[:, :, :], ALU.mult, ALU.max))
                step(v.tensor_tensor(M[:, :, :], s[:, :, :], sf[:, :, :], ALU.max))
                for h in range(H):
                    v.tensor_tensor_scan(F[:, h, :], K["pcont"][:, :], M[:, h, :], -BIG, ALU.add, ALU.max)
                    last = v.tensor_tensor_scan(B[:, h, ::-1], K["pnext"][:, ::-1], M[:, h, ::-1], -BIG, ALU.add, ALU.max)
                step(last)
                for h in range(H):
                    v.tensor_scalar(bc[:, 2 * h, :], K["ones"][:, :], F[:, h, T - 1:T], None, ALU.mult)
                    v.tensor_scalar(bc[:, 2 * h + 1, :], K["ones"][:, :], B[:, h, 0:1], None, ALU.mult).then_inc(s_bc, 1)
                step(v.tensor_tensor(M[:, :, :], F[:, :, :], B[:, :, :], ALU.max))
                v.wait_ge(s_pb, H)
                for h in range(H):
                    for c, (half, pen) in enumerate(((0, "pLF"), (1, "pFF"), (0, "pLL"), (1, "pFL"))):
                        last = v.tensor_tensor_reduce(junk[:, 0, 0:P], pb[:, 2 * h + half, :], K[pen][:, :], 1.0, -BIG,
                                                      ALU.add, ALU.max, mx[:, c, h:h + 1])
                        step(last)
                step(v.tensor_tensor(mx[:, 0, :], mx[:, 0, :], mx[:, 1, :], ALU.max))
                step(v.tensor_tensor(mx[:, 2, :], mx[:, 2, :], mx[:, 3, :], ALU.max))
                for c, pen in ((0, "plead"), (2, "ptrail")):
                    for h in range(H):
                        last = v.scalar_tensor_tensor(M[:, h, :], K[pen][:, :], mx[:, c, h:h + 1], M[:, h, :], ALU.add, ALU.max)
                    step(last)
                v.tensor_tensor(s[:, :, :], s[:, :, :], M[:, :, :], ALU.subtract)
                v.tensor_tensor(sf[:, :, :], sf[:, :, :], M[:, :, :], ALU.subtract).then_inc(s_arg, 1)
                v.wait_ge(s_exp, 1)
                for h in range(H):
                    v.tensor_tensor_scan(F[:, h, :], K["cont"][:, :], s[:, h, :], 0.0, ALU.mult, ALU.add)
                    last = v.tensor_tensor_scan(B[:, h, ::-1], K["cnext"][:, ::-1], s[:, h, ::-1], 0.0, ALU.mult, ALU.add)
                step(last)
                v.tensor_copy(ends[:, 0, :], F[:, :, T - 1])
                v.tensor_scalar(ends[:, 1, :], B[:, :, 0], K["nosingle"][:, 0:1], None, ALU.mult).then_inc(s_ends, 1)
                step(v.tensor_tensor(M[:, :, :], F[:, :, :], B[:, :, :], ALU.add))
                step(v.tensor_tensor(M[:, :, :], M[:, :, :], s[:, :, :], ALU.subtract))
                step(v.tensor_tensor(M[:, :, :], M[:, :, :], K["inner"][:, :].unsqueeze(1).to_broadcast([P, H, T]), ALU.mult))
                v.wait_ge(s_pt, 1)
                step(v.tensor_copy(mx[:, 0:2, :], pt[:, :, 0:H]))
                for c, mask in enumerate(("lead", "trail")):
                    for h in range(H):
                        last = v.scalar_tensor_tensor(M[:, h, :], K[mask][:, :], mx[:, c, h:h + 1], M[:, h, :], ALU.mult, ALU.add)
                    step(last)
                step(v.tensor_tensor(M[:, :, :], M[:, :, :], sf[:, :, :], ALU.add))
                step(v.tensor_scalar(M[:, :, :], M[:, :, :], 1e-16, None, ALU.add))
                step(v.reciprocal(M[:, :, :], M[:, :, :]))
                v.scalar_tensor_tensor(alpha[:, :, :], s[:, :, :], 1.0 / H if n == 2 else 1.0, M[:, :, :], ALU.mult, ALU.mult)

            @block.tensor
            def _(pe):
                for h in range(H):
                    pe.wait_ge(s_bc, h + 1)
                    pe.transpose(pb[:, 2 * h, :], bc[:, 2 * h, :], K["ident"][:, :])
                    pe.transpose(pb[:, 2 * h + 1, :], bc[:, 2 * h + 1, :], K["ident"][:, :]).then_inc(s_pb, 1)
                pe.wait_ge(s_ends, 1)
                pe.matmul(pt[:, 0, 0:H], K["FL"][:, :], ends[:, 0, :], start=True, stop=False)
                pe.matmul(pt[:, 0, 0:H], K["FF"][:, :], ends[:, 1, :], start=False, stop=True)
                pe.matmul(pt[:, 1, 0:H], K["LL"][:, :], ends[:, 0, :], start=True, stop=False)
                pe.matmul(pt[:, 1, 0:H], K["LF"][:, :], ends[:, 1, :], start=False, stop=True).then_inc(s_pt, 1)

            @block.scalar
            def _(act):
                act.wait_ge(s_arg, 1)
                act.activation(s[:, :, :], s[:, :, :], ACT.Exp)
                act.activation(sf[:, :, :], sf[:, :, :], ACT.Exp).then_inc(s_exp, 1)


def edge_messages(nc, K, n, H, KB, weight, table, target, alpha):
    C = C1 if n < 2 else D
    W = H * C
    O = W if n < 2 else D
    with phase(nc) as (ctx, sems):
        def sb(name, shape, dt=F32):
            return ctx.enter_context(nc.sbuf_tensor(f"em{n}_{name}", shape, dt))

        def sem(name):
            s = ctx.enter_context(nc.semaphore(f"em{n}_{name}"))
            sems.append(s)
            return s

        prime = sb("prime", [P, RING, 4])
        slot, out_slot = sb("slot", [P, RING, 2], I32), sb("oslot", [P, RING, 1], I32)
        xs, xd, diff = (sb(c, [P, RING, KB * D]) for c in ("xs", "xd", "diff"))
        dT = sb("dT", [D, RING, KB, P])
        acc, part = sb("acc", [P, RING, O]), sb("part", [P, 2, O])
        fin = sb("fin", [P, O])
        psT = ctx.enter_context(nc.psum_tensor(f"em{n}_psT", [P, 2, 512], F32))
        psY = ctx.enter_context(nc.psum_tensor(f"em{n}_psY", [P, 2, 512 * (-(-W // 512))], F32))
        psF = ctx.enter_context(nc.psum_tensor(f"em{n}_psF", [P, 512], F32))
        s_got = [K["dma_sem"](f"em{n}_got{k}") for k in range(RING)]
        s_put = [K["dma_sem"](f"em{n}_put{k}") for k in range(RING)]
        s_slot, s_go = sem("slot"), sem("go")
        s_diff = sem("diff")
        s_turn = sem("turn")
        s_evac = sem("evac")
        s_mm = sem("mm")
        s_walk = sem("walk")
        s_oslot, s_v = sem("oslot"), sem("v")
        s_fin, s_finp = sem("fin"), sem("finp")
        s_finput = K["dma_sem"](f"em{n}_finput")
        with nc.Block() as block:

            @block.gpsimd
            def _(pool):
                def fetch(i, k):
                    pool.wait_ge(s_slot, i * RING + (k + 1))
                    pool.sem_inc(s_go, 1)
                    gather(pool, xs[:, k, :], table[:, :], slot[:, k, 0:1]).then_inc(s_got[k], 16)
                    gather(pool, xd[:, k, :], table[:, :], slot[:, k, 1:2]).then_inc(s_got[k], 16)

                def put(i, k):
                    pool.wait_ge(s_oslot, i * RING + (k + 1))
                    pool.wait_ge(s_walk, i * RING + (k + 3))
                    pool.sem_inc(s_go, 1)
                    scatter_add(pool, target[:, :], out_slot[:, k, :], acc[:, k, :]).then_inc(s_put[k], 16)

                for k in range(RING):
                    pool.dma_start(prime[:, k, :], K["x"][0:P, 0:4]).then_inc(s_put[k], 16)
                for k in range(RING):
                    fetch(0, k)
                with pool.Fori(1, ITERS) as i:
                    for k in range(RING):
                        fetch(i, k)
                        put(i - 1, k)
                for k in range(RING):
                    put(ITERS - 1, k)
                for k in range(RING):
                    pool.wait_ge(s_put[k], 16 * (ITERS + 1))
                pool.wait_ge(s_fin, 1)
                scatter_add(pool, target[:, :], K["fin_idx"][:, :], fin[:, :]).then_inc(s_finput, 16)
                pool.wait_ge(s_finput, 16)

            @block.vector
            def _(v):
                v.tensor_copy(slot[:, :, :], K["edge_idx"][:, 0:RING, :]).then_inc(s_slot, RING)
                step = Steps(v, s_v)
                step(v.memset(acc[:, RING - 1, :], 0.0))
                v.sem_inc(s_walk, 2)
                with v.Fori(0, ITERS) as i:
                    step.loop(i, RING * (1 if n < 2 else H))
                    for k in range(RING):
                        v.wait_ge(s_got[k], 32 * i + 32)
                        v.wait_ge(s_turn, i * RING + (k + 1))
                        v.tensor_tensor(diff[:, k, :], xs[:, k, :], xd[:, k, :], ALU.subtract).then_inc(s_diff, 1)
                        v.tensor_copy(slot[:, k, :], K["edge_idx"][:, bass.ds(i * RING + (k + RING), 1), :].rearrange("p a b -> p (a b)")).then_inc(s_slot, 1)
                    for k in range(RING):
                        t = bass.ds(i * RING + k, 1)
                        v.wait_ge(s_walk, i * RING + (k + 2))
                        a, b = part[:, 0, :], part[:, 1, :]
                        step(v.tensor_scalar(a, acc[:, (k - 1) % RING, :], K["cont"][:, t], None, ALU.mult))
                        v.wait_ge(s_put[k], 16 * i + 16)
                        v.wait_ge(s_mm, i * RING + (k + 1 + RING))
                        for h in range(H):
                            prod = psY[:, k % 2, h * C:(h + 1) * C]
                            scale = alpha[:, h, t]
                            if n < 2:
                                c = slice(h * C, (h + 1) * C)
                                ins = v.scalar_tensor_tensor(acc[:, k, c], prod, scale, a[:, c], ALU.mult, ALU.add)
                            else:
                                o = acc[:, k, :] if h == H - 1 else b
                                ins = v.scalar_tensor_tensor(o, prod, scale, a, ALU.mult, ALU.add)
                                a, b = b, a
                                if h < H - 1:
                                    step(ins)
                        ins.then_inc(s_walk, 1)
                step.done(ITERS)
                v.wait_ge(s_finp, 1)
                v.tensor_copy(fin[:, :], psF[:, 0:O]).then_inc(s_fin, 1)

            @block.tensor
            def _(pe):
                pe.sem_inc(s_turn, RING)
                pe.sem_inc(s_mm, RING)
                with pe.Fori(0, ITERS) as i:
                    for k in range(RING):
                        pe.wait_ge(s_diff, i * RING + (k + 1))
                        pe.wait_ge(s_evac, i * RING + (k + 1))
                        for kb in range(KB):
                            last = pe.transpose(psT[:, k % 2, kb * P:(kb + 1) * P], diff[:, k, kb * D:(kb + 1) * D],
                                                K["ident"][:, :])
                        last.then_inc(s_turn, 1)
                        pe.wait_ge(s_evac, i * RING + (k + 3))
                        pe.wait_ge(s_walk, i * RING + (k + 1))
                        for c0 in range(0, W, 512):
                            c1 = min(W, c0 + 512)
                            for kb in range(KB):
                                rhs = weight[:, c0:c1] if KB == 1 else weight[:, kb, c0:c1]
                                last = pe.matmul(psY[:, k % 2, c0:c1], dT[:, k, kb, :], rhs, start=(kb == 0), stop=(kb == KB - 1))
                        last.then_inc(s_mm, 1)
                pe.wait_ge(s_walk, T + 2)
                pe.matmul(psF[:, 0:O], K["LL"][:, :], acc[:, RING - 1, :], start=True, stop=True).then_inc(s_finp, 1)

            @block.scalar
            def _(act):
                act.sem_inc(s_evac, 2)
                with act.Fori(0, ITERS) as i:
                    for k in range(RING):
                        act.wait_ge(s_turn, i * RING + (k + 1 + RING))
                        act.wait_ge(s_mm, i * RING + (k + 1))
                        act.copy(dT[:, k].rearrange("d a b -> d (a b)"), psT[:, k % 2, 0:KB * P]).then_inc(s_evac, 1)
                        act.wait_ge(s_put[k], 16 * i + 16)
                        act.copy(out_slot[:, k, :], K["scat_idx"][:, bass.ds(i * RING + k, 1)]).then_inc(s_oslot, 1)


def dense_gat(nc, K, n, pre_in, table, weight, bias, pre_out, scores):
    H = (H1, H3)[n]
    O = (HC, D)[n]
    W = O + 2 * H
    with phase(nc) as (ctx, sems):
        def sb(name, shape, dt=F32):
            return ctx.enter_context(nc.sbuf_tensor(f"dg{n}_{name}", shape, dt))

        def sem(name):
            s = ctx.enter_context(nc.semaphore(f"dg{n}_{name}"))
            sems.append(s)
            return s

        x, e, h = (sb(c, [P, 2, PER, HC]) for c in "xeh")
        hT = sb("hT", [D, 2, 2, GROUP])
        pre, sc = sb("pre", [P, 2, PER, O]), sb("sc", [P, 2, PER, 2 * H])
        pT = ctx.enter_context(nc.psum_tensor(f"dg{n}_pT", [P, 2, GROUP], F32))
        pP = ctx.enter_context(nc.psum_tensor(f"dg{n}_pP", [P, PER, 512], F32))
        s_ld, s_st = [sem("ld0"), sem("ld1")], [sem("st0"), sem("st1")]
        s_e, s_h = sem("e"), sem("h")
        s_turn = sem("turn")
        s_hT = sem("hT")
        s_mm = sem("mm")
        s_pre = sem("pre")
        s_v = sem("v")
        with nc.Block() as block:
            ig, hg, og, sg = grouped(pre_in), grouped(table), grouped(pre_out), grouped(scores)

            @block.sync
            def _(sp):
                stream(sp, s_ld, s_st, (s_h, 0), [(s_pre, 1)],
                           [lambda g, b: sp.dma_start(flat(x[:, b]), ig[g])],
                           [lambda g, b: sp.dma_start(hg[g], flat(h[:, b])), lambda g, b: sp.dma_start(og[g], flat(pre[:, b])),
                            lambda g, b: sp.dma_start(sg[g], flat(sc[:, b]))])

            @block.scalar
            def _(act):
                act.sem_inc(s_hT, 1)
                with act.Fori(0, PAIRS) as i:
                    for b in range(2):
                        act.wait_ge(s_ld[b], 16 * i + 16)
                        act.activation(e[:, b], x[:, b], ACT.Exp).then_inc(s_e, 1)
                        act.wait_ge(s_turn, 2 * i + (b + 1))
                        act.copy(hT[:, b], pT[:, :, :]).then_inc(s_hT, 1)

            @block.vector
            def _(v):
                v.sem_inc(s_pre, 1)
                step = Steps(v, s_v)
                with v.Fori(0, PAIRS) as i:
                    step.loop(i, 2)
                    for b in range(2):
                        v.wait_ge(s_e, 2 * i + (b + 1))
                        step(v.tensor_scalar(flat(e[:, b]), flat(e[:, b]), 1.0, -1.0, ALU.min, ALU.add))
                        v.wait_ge(s_st[b], 48 * i + 48)
                        v.scalar_tensor_tensor(flat(h[:, b]), flat(x[:, b]), 0.0, flat(e[:, b]), ALU.max, ALU.add).then_inc(s_h, 1)
                        v.wait_ge(s_mm, 2 * i + (b + 1))
                        v.tensor_copy(sc[:, b], pP[:, :, O:W])
                        v.tensor_tensor(pre[:, b], pP[:, :, 0:O], rows4(bias[:, :]), ALU.add).then_inc(s_pre, 1)
                step.done(PAIRS)

            @block.tensor
            def _(pe):
                with pe.Fori(0, PAIRS) as i:
                    for b in range(2):
                        pe.wait_ge(s_h, 2 * i + (b + 1))
                        pe.wait_ge(s_hT, 2 * i + (b + 1))
                        for j in range(PER):
                            for kb in range(2):
                                last = pe.transpose(pT[:, kb, j * P:(j + 1) * P], h[:, b, j, kb * D:(kb + 1) * D], K["ident"][:, :])
                        last.then_inc(s_turn, 1)
                        pe.wait_ge(s_hT, 2 * i + (b + 2))
                        pe.wait_ge(s_pre, 2 * i + (b + 1))
                        for j in range(PER):
                            for kb in range(2):
                                last = pe.matmul(pP[:, j, 0:W], hT[:, b, kb, j * P:(j + 1) * P], weight[:, kb, :],
                                                 start=(kb == 0), stop=(kb == 1))
                        last.then_inc(s_mm, 1)


def final(nc, K, out):
    with phase(nc) as (ctx, sems):
        def sb(name, shape, dt=F32):
            return ctx.enter_context(nc.sbuf_tensor("l_" + name, shape, dt))

        def sem(name):
            s = ctx.enter_context(nc.semaphore("l_" + name))
            sems.append(s)
            return s

        x, p, e, u, y = (sb(c, [P, 2, PER, D]) for c in ("x", "p", "e", "u", "y"))
        norm = Norm(sb, sem, "")
        s_ld, s_st = [sem("ld0"), sem("ld1")], [sem("st0"), sem("st1")]
        s_e, s_u, s_done, s_v = sem("e"), sem("u"), sem("done"), sem("v")
        with nc.Block() as block:
            xg, pg, og = grouped(K["x3"]), grouped(K["pre5"]), grouped(out)

            @block.sync
            def _(sp):
                stream(sp, s_ld, s_st, (s_u, 0), [(s_done, 0)],
                       [lambda g, b: sp.dma_start(flat(x[:, b]), xg[g]), lambda g, b: sp.dma_start(flat(p[:, b]), pg[g])],
                       [lambda g, b: sp.dma_start(og[g], flat(y[:, b]))])

            @block.scalar
            def _(act):
                with act.Fori(0, PAIRS) as i:
                    for b in range(2):
                        act.wait_ge(s_ld[b], 32 * i + 32)
                        act.activation(e[:, b], p[:, b], ACT.Exp).then_inc(s_e, 1)
                        norm.root(act, K, 2 * i + (b + 1))

            @block.vector
            def _(v):
                step = Steps(v, s_v)
                with v.Fori(0, PAIRS) as i:
                    step.loop(i, 8)
                    for b in range(2):
                        v.wait_ge(s_e, 2 * i + (b + 1))
                        step(v.tensor_scalar(flat(e[:, b]), flat(e[:, b]), 1.0, -1.0, ALU.min, ALU.add))
                        step(v.scalar_tensor_tensor(flat(u[:, b]), flat(p[:, b]), 0.0, flat(e[:, b]), ALU.max, ALU.add))
                        v.tensor_tensor(u[:, b], u[:, b], x[:, b], ALU.add).then_inc(s_u, 1)
                        v.wait_ge(s_u, 2 * i + (b + 1))
                        norm.stats(v, step, u[:, b])
                        v.wait_ge(s_st[b], 16 * i + 16)
                        norm.rows(v, step, 2 * i + (b + 1), y[:, b], u[:, b]).then_inc(s_done, 1)
                step.done(PAIRS)


def kernel(**inputs):
    import concourse.bacc as bacc
    from concourse.bass_utils import run_bass_kernel_spmd

    a = {k: np.asarray(v) for k, v in inputs.items()}
    x = np.zeros((NPAD, D), np.float32)
    x[:N] = a["x"]
    src = np.full((EPAD,), N, np.int32)
    src[:E] = a["src"]
    dst = np.full((EPAD + T,), N, np.int32)
    dst[:E] = a["dst"]
    dst[EPAD:] = NPAD
    row = lambda v: np.ascontiguousarray(v).reshape(-1)
    turn = lambda v: np.ascontiguousarray(np.transpose(v))
    arrays = {
        "x": x, "src": src, "dst": dst,
        "w_hhT": turn(a["L0_gnn_W_hh"]), "w_ihT": turn(a["L0_gnn_W_ih"]), "w_msg": a["L0_gnn_W_msg"],
        "w1T": turn(a["L1_gnn_W"]), "w2T": turn(a["L2_gnn_W"]),
        "w_att": row(a["L0_gnn_W_att"]), "b_att": a["L0_gnn_b_att"], "b_msg": a["L0_gnn_b_msg"],
        "b_ih": turn(a["L0_gnn_b_ih"].reshape(3, D)), "b_hh": turn(a["L0_gnn_b_hh"].reshape(3, D)),
        "gamma": a["L0_gnn_gamma"].reshape(D, 1), "beta": a["L0_gnn_beta"].reshape(D, 1),
        "b1": a["L1_gnn_b"], "ln_g": a["L2_gnn_ln_gamma"], "ln_b": a["L2_gnn_ln_beta"], "b2": a["L2_gnn_b"],
    }
    for n in (1, 2, 3):
        arrays.update({f"g{n}w": a[f"L3_gnn_W{n}"], f"s{n}w": a[f"L3_gnn_s{n}W"], f"as{n}": row(a[f"L3_gnn_as{n}"]),
                       f"ad{n}": row(a[f"L3_gnn_ad{n}"]), f"g{n}b": a[f"L3_gnn_b{n}"], f"s{n}b": a[f"L3_gnn_s{n}b"]})
    nc = bacc.Bacc("TRN2", target_bir_lowering=False, num_devices=1)
    A = {k: nc.dram_tensor("in_" + k, v.shape, mybir.dt.from_np(v.dtype), kind="ExternalInput").ap()
         for k, v in arrays.items()}
    out = nc.dram_tensor("out", (NPAD, D), F32, kind="ExternalOutput").ap()
    build(nc, A, out)
    r = run_bass_kernel_spmd(nc, [{"in_" + k: v for k, v in arrays.items()}], core_ids=[0])
    return r.results[0]["out"][:N]
```

```python
from contextlib import ExitStack, contextmanager

import numpy as np

import concourse.bass as bass
from concourse import mybir

P = 128
N = 50000
E = 25000
D = 128
PER = 4
GROUP = P * PER
GROUPS = -(-N // GROUP)
NPAD = GROUPS * GROUP
LAST_VALID = (N - (GROUPS - 1) * GROUP) // PER
T = 196
EPAD = P * T
RING = 4
ITERS = T // RING
NROW = NPAD + RING * P
RG = RING
H1, C1 = 4, 64
HC = H1 * C1
H3 = 6
EPS = 1e-5
BIG = 1e30

F32 = mybir.dt.float32
F16 = mybir.dt.float16
I32 = mybir.dt.int32
ALU = mybir.AluOpType
ACT = mybir.ActivationFunctionType
AX = mybir.AxisListType

assert T % RING == 0 and EPAD >= E and (N - (GROUPS - 1) * GROUP) % PER == 0


@contextmanager
def phase(nc):
    sems = []
    with ExitStack() as ctx:
        yield ctx, sems
        with nc.Block() as block:
            @block.gpsimd
            def _(pool):
                for s in sems:
                    pool.sem_clear(s)


class Steps:

    def __init__(self, eng, sem):
        self.eng, self.sem, self.n, self.base = eng, sem, 0, 0

    def __call__(self, ins):
        ins.then_inc(self.sem, 1)
        self.n += 1
        self.eng.wait_ge(self.sem, self.base + self.n)

    def loop(self, i, per):
        self.base, self.per, self.start = i * per, per, self.n

    def done(self, times):
        assert self.n - self.start == self.per, (self.n - self.start, self.per)
        self.base, self.n = 0, self.start + self.per * times


def grouped(table):
    return table[0:NPAD, :].rearrange("(g p j) d -> g p (j d)", g=GROUPS, p=P, j=PER)


def build(nc, A, out):
    ctx = ExitStack()
    with ctx:
        def sb(name, shape, dt=F32):
            return ctx.enter_context(nc.sbuf_tensor(name, shape, dt))

        def sem(name):
            return ctx.enter_context(nc.semaphore(name))

        def dram(name, shape):
            return nc.dram_tensor(name, shape, F32).ap()

        K = {"x": A["x"], "dma_sem": sem}
        K["agg0"] = dram("agg0", (NROW, D))
        K["agg1"] = dram("agg1", (NROW, D))
        K["hT"] = dram("hT", (D, NPAD))
        K["x1"] = dram("x1", (NPAD, D))
        K["msg"] = dram("msg", (NPAD, D))
        K["pre2"] = dram("pre2", (NROW, D))
        K["x3"] = dram("x3", (NPAD, D))
        K["pre3"] = dram("pre3", (NROW, HC))
        K["sc3"] = dram("sc3", (NPAD, 2 * H1))
        K["h4"] = dram("h4", (NPAD, HC))
        K["pre4"] = dram("pre4", (NROW, HC))
        K["sc4"] = dram("sc4", (NPAD, 2 * H1))
        K["h5"] = dram("h5", (NPAD, HC))
        K["pre5"] = dram("pre5", (NROW, D))
        K["sc5"] = dram("sc5", (NPAD, 2 * H3))
        K["ident"] = sb("ident", [P, P])
        K["ones"] = sb("ones", [P, P])
        K["eps"] = sb("eps", [P, 1])
        K["edge_idx"] = sb("edge_idx", [P, T + RING, 2], I32)
        K["scat_idx"] = sb("scat_idx", [P, T], I32)
        K["fin_idx"] = sb("fin_idx", [P, 1], I32)
        for m in ("cont", "cnext", "pcont", "pnext", "lead", "trail", "inner", "plead", "ptrail", "isq_in"):
            K[m] = sb(m, [P, T])
        for m in ("LF", "FF", "LL", "FL", "pLF", "pFF", "pLL", "pFL"):
            K[m] = sb("m" + m, [P, P])
        K["nosingle"] = sb("nosingle", [P, 1])
        K["isq_out"] = sb("isq_out", [P, GROUPS * PER])
        K["whh"] = sb("whh", [D, 3 * D])
        K["wih"] = sb("wih", [D, 3 * D])
        K["wmsg"] = sb("wmsg", [D, D])
        K["w1"] = sb("w1", [D, D])
        K["w2a"] = sb("w2a", [D, D])
        K["w2b"] = sb("w2b", [D, D])
        K["att"] = sb("att", [P, 2 * D])
        K["batt"] = sb("batt", [P, 1])
        K["bmsg"] = sb("bmsg", [P, D])
        K["brz"] = sb("brz", [D, 4])
        K["bn"] = sb("bn", [D, 2])
        K["bnss"] = sb("bnss", [D, 2])
        K["b1"] = sb("b1", [P, D])
        K["ln_g"] = sb("ln_g", [P, D])
        K["ln_b"] = sb("ln_b", [P, D])
        K["b2"] = sb("b2", [P, D])
        K["g1w"] = sb("g1w", [D, HC])
        K["g1d"] = sb("g1d", [D, HC + 2 * H1])
        K["g1b"] = sb("g1b", [P, HC])
        K["g2w"] = sb("g2w", [D, 2, HC])
        K["g2d"] = sb("g2d", [D, 2, HC + 2 * H1])
        K["g2b"] = sb("g2b", [P, HC])
        K["g3w"] = sb("g3w", [D, 2, H3 * D])
        K["g3d"] = sb("g3d", [D, 2, D + 2 * H3])
        K["g3b"] = sb("g3b", [P, D])
        K["stats"] = sb("stats", [D, GROUPS, 6])

        prepare(nc, A, K)
        out_degree(nc, A, K)
        edges(nc, K, "e0", A["x"], K["wmsg"], K["agg0"])
        gru(nc, A, K)
        norm0(nc, A, K)
        edges(nc, K, "e1", K["x1"], K["w1"], K["agg1"])
        dense1(nc, K)
        edges(nc, K, "e2", K["msg"], K["w2b"], K["pre2"])
        dense2(nc, K)
        for n, (h, kb, w) in enumerate(((H1, 1, K["g1w"]), (H1, 2, K["g2w"]), (H3, 2, K["g3w"]))):
            table = (K["x3"], K["h4"], K["h5"])[n]
            scores, pre = K[f"sc{n + 3}"], K[f"pre{n + 3}"]
            with nc.sbuf_tensor(f"alpha{n}", [P, h, T], F32) as alpha:
                edge_scores(nc, K, n, h, scores, alpha)
                edge_messages(nc, K, n, h, kb, w, table, pre, alpha)
            if n < 2:
                dense_gat(nc, K, n, pre, K[f"h{n + 4}"], (K["g2d"], K["g3d"])[n], (K["g2b"], K["g3b"])[n],
                          K[f"pre{n + 4}"], K[f"sc{n + 4}"])
        final(nc, K, out)


def prepare(nc, A, K):
    with phase(nc) as (ctx, sems):
        def sb(name, shape, dt=F32):
            return ctx.enter_context(nc.sbuf_tensor("prep_" + name, shape, dt))

        def sem(name):
            s = ctx.enter_context(nc.semaphore("prep_" + name))
            sems.append(s)
            return s

        ZC = NROW // P * D // 12
        assert ZC * 12 * P == NROW * D
        zero = sb("zero", [P, ZC])
        dstF = sb("dstF", [P, T])
        nxtI = sb("nxtI", [P, T], I32)
        nxtF = sb("nxtF", [P, 1])
        dumI = sb("dumI", [P, T], I32)
        dum = sb("dum", [P, T])
        tmp = sb("tmp", [P, T])
        tmp2 = sb("tmp2", [P, T])
        idx = sb("idx", [P, 2, T], I32)
        lb = sb("lb", [P, P])
        fb = sb("fb", [P, P])
        bt = sb("bt", [D, 6])
        ts = sb("ts", [P, 2])
        s1w = sb("s1w", [D, HC])
        s2w = sb("s2w", [D, 2, HC])
        s3w = sb("s3w", [D, 2, D])
        avs = sb("avs", [P, 2, HC])
        avs2 = sb("avs2", [P, 2, HC])
        avs3 = sb("avs3", [P, 2, H3 * D])
        prod = sb("prod", [D, H3 * D])
        sbias = [sb(f"sbias{i}", [P, w]) for i, w in enumerate((HC, HC, D))]
        pfirst = ctx.enter_context(nc.psum_tensor("prep_pfirst", [P, 512], F32))
        plast = ctx.enter_context(nc.psum_tensor("prep_plast", [P, 512], F32))
        ptot = ctx.enter_context(nc.psum_tensor("prep_ptot", [P, 2, 512], F32))
        s_zero, s_ld, s_idx, s_zst, s_iota = sem("zero"), sem("ld"), sem("idx"), sem("zst"), sem("iota")
        s_id, s_fl, s_flT, s_tot, s_totp, s_sq, s_sqd, s_v = (
            sem("id"), sem("fl"), sem("flT"), sem("tot"), sem("totp"), sem("sq"), sem("sqd"), sem("v"))

        loads = [
            (K["whh"][:, :], A["w_hhT"]), (K["wih"][:, :], A["w_ihT"]), (K["wmsg"][:, :], A["w_msg"]),
            (K["w1"][:, :], A["w1T"]), (K["w2a"][:, :], A["w2T"][0:D, :]), (K["w2b"][:, :], A["w2T"][D:2 * D, :]),
            (K["att"][:, 0:D], A["w_att"][D:2 * D].partition_broadcast(P)),
            (K["att"][:, D:2 * D], A["w_att"][0:D].partition_broadcast(P)), (K["batt"][:, :], A["b_att"].partition_broadcast(P)),
            (K["bmsg"][:, :], A["b_msg"].partition_broadcast(P)),
            (bt[:, 0:3], A["b_ih"]), (bt[:, 3:6], A["b_hh"]),
            (K["bn"][:, 0:1], A["gamma"]), (K["bn"][:, 1:2], A["beta"]),
            (K["b1"][:, :], A["b1"].partition_broadcast(P)), (K["ln_g"][:, :], A["ln_g"].partition_broadcast(P)),
            (K["ln_b"][:, :], A["ln_b"].partition_broadcast(P)), (K["b2"][:, :], A["b2"].partition_broadcast(P)),
            (K["g1w"][:, :], A["g1w"]), (s1w[:, :], A["s1w"]),
            (K["g2w"][:, :, :], A["g2w"].rearrange("(k p) n -> p k n", p=D)),
            (s2w[:, :, :], A["s2w"].rearrange("(k p) n -> p k n", p=D)),
            (K["g3w"][:, :, :], A["g3w"].rearrange("(k p) n -> p k n", p=D)),
            (s3w[:, :, :], A["s3w"].rearrange("(k p) n -> p k n", p=D)),
            (avs[:, 0, :], A["as1"].partition_broadcast(P)), (avs[:, 1, :], A["ad1"].partition_broadcast(P)),
            (avs2[:, 0, :], A["as2"].partition_broadcast(P)), (avs2[:, 1, :], A["ad2"].partition_broadcast(P)),
            (avs3[:, 0, :], A["as3"].partition_broadcast(P)), (avs3[:, 1, :], A["ad3"].partition_broadcast(P)),
            (K["g1b"][:, :], A["g1b"].partition_broadcast(P)), (sbias[0][:, :], A["s1b"].partition_broadcast(P)),
            (K["g2b"][:, :], A["g2b"].partition_broadcast(P)), (sbias[1][:, :], A["s2b"].partition_broadcast(P)),
            (K["g3b"][:, :], A["g3b"].partition_broadcast(P)), (sbias[2][:, :], A["s3b"].partition_broadcast(P)),
        ]
        zeros = []
        for name in ("agg0", "agg1"):
            flat = K[name].rearrange("(p r) d -> p (r d)", p=P)
            zeros += [(flat[:, c * ZC:(c + 1) * ZC], zero[:, :]) for c in range(12)]
        for name, w in (("pre2", D), ("pre3", HC), ("pre4", HC), ("pre5", D)):
            spare = K[name][NPAD:NROW, :].rearrange("(p r) d -> p (r d)", p=P)
            zeros.append((spare, zero[:, 0:RING * w]))

        with nc.Block() as block:

            @block.sync
            def _(sp):
                sp.dma_start(idx[:, 0, :], A["src"][0:EPAD].rearrange("(p t) -> p t", t=T)).then_inc(s_idx, 16)
                sp.dma_start(idx[:, 1, :], A["dst"][0:EPAD].rearrange("(p t) -> p t", t=T)).then_inc(s_idx, 16)
                sp.dma_start(nxtI[:, :], A["dst"][T:T + EPAD].rearrange("(p t) -> p t", t=T)).then_inc(s_idx, 16)
                for dst, src in loads:
                    sp.dma_start(dst, src).then_inc(s_ld, 16)
                sp.wait_ge(s_zero, 1)
                for dst, src in zeros:
                    sp.dma_start(dst, src).then_inc(s_zst, 16)
                sp.wait_ge(s_zst, 16 * len(zeros))

            @block.gpsimd
            def _(pool):
                pool.memset(zero[:, :], 0.0).then_inc(s_zero, 1)
                pool.memset(K["ident"][:, :], 0.0).then_inc(s_id, 1)
                pool.iota(dumI[:, :], pattern=[[0, ITERS], [P, RING]], base=NPAD, channel_multiplier=1).then_inc(s_iota, 1)
                pool.wait_ge(s_id, 1)
                pool.affine_select(out=K["ident"][:, :], in_=K["ident"][:, :], compare_op=ALU.not_equal, fill=1.0,
                                   base=0, pattern=[[-1, P]], channel_multiplier=1).then_inc(s_id, 1)

            @block.vector
            def _(v):
                step = Steps(v, s_v)
                v.memset(K["ones"][:, :], 1.0)
                v.memset(K["eps"][:, :], EPS)
                step(v.memset(K["edge_idx"][:, :, :], 0))
                v.wait_ge(s_idx, 48)
                v.tensor_copy(K["edge_idx"][:, 0:T, :], idx[:, :, :].rearrange("p s t -> p t s"))
                v.tensor_copy(dstF[:, :], idx[:, 1, :])
                step(v.tensor_copy(nxtF[:, :], nxtI[:, T - 1:T]))
                first, last = dstF[:, 0:1], dstF[:, T - 1:T]
                v.tensor_scalar(lb[:, :], K["ones"][:, :], last, None, ALU.mult)
                v.tensor_scalar(fb[:, :], K["ones"][:, :], first, None, ALU.mult).then_inc(s_fl, 1)
                v.memset(K["cont"][:, 0:1], 0.0)
                v.memset(K["cnext"][:, T - 1:T], 0.0)
                v.tensor_tensor(K["cont"][:, 1:T], dstF[:, 1:T], dstF[:, 0:T - 1], ALU.is_equal)
                step(v.tensor_tensor(K["cnext"][:, 0:T - 1], dstF[:, 1:T], dstF[:, 0:T - 1], ALU.is_equal))
                v.tensor_scalar(K["pcont"][:, :], K["cont"][:, :], -1.0, BIG, ALU.add, ALU.mult)
                v.tensor_scalar(K["pnext"][:, :], K["cnext"][:, :], -1.0, BIG, ALU.add, ALU.mult)
                v.wait_ge(s_iota, 1)
                step(v.tensor_copy(dum[:, :], dumI[:, :]))
                v.tensor_scalar(tmp2[:, :], K["cnext"][:, :], -1.0, 1.0, ALU.mult, ALU.add)
                step(v.tensor_tensor(tmp[:, :], dstF[:, :], dum[:, :], ALU.subtract))
                step(v.memset(tmp2[:, T - 1:T], 0.0))
                step(v.tensor_tensor(tmp2[:, :], tmp[:, :], tmp2[:, :], ALU.mult))
                step(v.tensor_tensor(K["scat_idx"][:, :], tmp2[:, :], dum[:, :], ALU.add))
                step(v.tensor_tensor(ts[:, 0:1], nxtF[:, :], last, ALU.not_equal))
                step(v.tensor_tensor(ts[:, 1:2], last, dum[:, 0:1], ALU.subtract))
                step(v.tensor_tensor(ts[:, 1:2], ts[:, 0:1], ts[:, 1:2], ALU.mult))
                step(v.tensor_tensor(K["fin_idx"][:, :], ts[:, 1:2], dum[:, 0:1], ALU.add))
                v.tensor_scalar(K["lead"][:, :], dstF[:, :], first, None, ALU.is_equal)
                step(v.tensor_scalar(tmp[:, :], dstF[:, :], last, None, ALU.is_equal))
                v.tensor_scalar(K["ptrail"][:, :], tmp[:, :], -1.0, BIG, ALU.add, ALU.mult)
                v.tensor_scalar(K["plead"][:, :], K["lead"][:, :], -1.0, BIG, ALU.add, ALU.mult)
                step(v.tensor_tensor(tmp2[:, :], tmp[:, :], K["lead"][:, :], ALU.mult))
                step(v.tensor_tensor(K["trail"][:, :], tmp[:, :], tmp2[:, :], ALU.subtract))
                step(v.tensor_tensor(tmp2[:, :], K["trail"][:, :], K["lead"][:, :], ALU.add))
                v.tensor_scalar(K["inner"][:, :], tmp2[:, :], -1.0, 1.0, ALU.mult, ALU.add)
                v.tensor_tensor(K["nosingle"][:, :], first, last, ALU.not_equal)
                v.wait_ge(s_flT, 1)
                for m, ps, s in (("LF", plast, first), ("FF", pfirst, first), ("LL", plast, last), ("FL", pfirst, last)):
                    ins = v.tensor_scalar(K[m][:, :], ps[:, 0:P], s, None, ALU.is_equal)
                step(ins)
                for m in ("LF", "FF", "LL", "FL"):
                    ins = v.tensor_scalar(K["p" + m][:, :], K[m][:, :], -1.0, BIG, ALU.add, ALU.mult)
                step(ins)
                v.tensor_tensor_scan(tmp[:, :], K["cont"][:, :], K["ones"][:, 0:1].to_broadcast([P, T]), 0.0, ALU.mult, ALU.add)
                step(v.tensor_tensor_scan(tmp2[:, ::-1], K["cnext"][:, ::-1], K["ones"][:, 0:1].to_broadcast([P, T]), 0.0, ALU.mult, ALU.add))
                v.tensor_copy(ts[:, 0:1], tmp[:, T - 1:T])
                step(v.tensor_tensor(ts[:, 1:2], tmp2[:, 0:1], K["nosingle"][:, :], ALU.mult))
                step(v.tensor_tensor(tmp[:, :], tmp[:, :], tmp2[:, :], ALU.add))
                step(v.tensor_scalar(tmp[:, :], tmp[:, :], -1.0, None, ALU.add))
                v.tensor_tensor(tmp[:, :], tmp[:, :], K["inner"][:, :], ALU.mult).then_inc(s_tot, 1)
                v.wait_ge(s_tot, 1)
                v.wait_ge(s_totp, 1)
                step(v.tensor_copy(ts[:, 0:2], ptot[:, :, 0]))
                step(v.scalar_tensor_tensor(tmp[:, :], K["lead"][:, :], ts[:, 0:1], tmp[:, :], ALU.mult, ALU.add))
                step(v.scalar_tensor_tensor(tmp[:, :], K["trail"][:, :], ts[:, 1:2], tmp[:, :], ALU.mult, ALU.add))
                v.tensor_scalar(tmp[:, :], tmp[:, :], 1.0, None, ALU.max).then_inc(s_sq, 1)
                v.wait_ge(s_sqd, 1)
                step(v.reciprocal(K["isq_in"][:, :], tmp2[:, :]))
                v.wait_ge(s_ld, 16 * len(loads))
                v.tensor_tensor(K["brz"][:, 0:2], bt[:, 0:2], bt[:, 3:5], ALU.add)
                v.tensor_copy(K["brz"][:, 2:3], bt[:, 2:3])
                v.tensor_copy(K["brz"][:, 3:4], bt[:, 5:6])
                v.tensor_tensor(K["g1b"][:, :], K["g1b"][:, :], sbias[0][:, :], ALU.add)
                v.tensor_tensor(K["g2b"][:, :], K["g2b"][:, :], sbias[1][:, :], ALU.add)
                v.tensor_tensor(K["g3b"][:, :], K["g3b"][:, :], sbias[2][:, :], ALU.add)
                v.tensor_tensor(K["g1d"][:, 0:HC], K["g1w"][:, :], s1w[:, :], ALU.add)
                step(v.tensor_tensor(K["g2d"][:, :, 0:HC], K["g2w"][:, :, :], s2w[:, :, :], ALU.add))
                for kb in range(2):
                    w = K["g3w"][:, kb, :]
                    step(v.tensor_reduce(prod[:, 0:D], w.rearrange("p (h c) -> p c h", h=H3), AX.X, ALU.add))
                    step(v.scalar_tensor_tensor(K["g3d"][:, kb, 0:D], prod[:, 0:D], 1.0 / H3, s3w[:, kb, :], ALU.mult, ALU.add))
                for w, a, h, o in ([(K["g1w"][:, :], avs, H1, K["g1d"][:, HC:])]
                                   + [(K["g2w"][:, kb, :], avs2, H1, K["g2d"][:, kb, HC:]) for kb in range(2)]
                                   + [(K["g3w"][:, kb, :], avs3, H3, K["g3d"][:, kb, D:]) for kb in range(2)]):
                    n = w.shape[1]
                    for side in range(2):
                        step(v.tensor_tensor(prod[:, 0:n], w, a[:, side, :], ALU.mult))
                        step(v.tensor_reduce(o[:, side * h:(side + 1) * h], prod[:, 0:n].rearrange("p (h c) -> p h c", h=h),
                                             AX.X, ALU.add))

            @block.tensor
            def _(pe):
                pe.wait_ge(s_id, 2)
                pe.wait_ge(s_fl, 1)
                pe.transpose(plast[:, 0:P], lb[:, :], K["ident"][:, :])
                pe.transpose(pfirst[:, 0:P], fb[:, :], K["ident"][:, :]).then_inc(s_flT, 1)
                pe.wait_ge(s_tot, 1)
                pe.matmul(ptot[:, 0, 0:1], K["FL"][:, :], ts[:, 0:1], start=True, stop=False)
                pe.matmul(ptot[:, 0, 0:1], K["FF"][:, :], ts[:, 1:2], start=False, stop=True)
                pe.matmul(ptot[:, 1, 0:1], K["LL"][:, :], ts[:, 0:1], start=True, stop=False)
                pe.matmul(ptot[:, 1, 0:1], K["LF"][:, :], ts[:, 1:2], start=False, stop=True).then_inc(s_totp, 1)

            @block.scalar
            def _(act):
                act.wait_ge(s_sq, 1)
                act.activation(tmp2[:, :], tmp[:, :], ACT.Sqrt).then_inc(s_sqd, 1)


def out_degree(nc, A, K):
    with phase(nc) as (ctx, sems):
        def sb(name, shape, dt=F32):
            return ctx.enter_context(nc.sbuf_tensor("deg_" + name, shape, dt))

        def sem(name):
            s = ctx.enter_context(nc.semaphore("deg_" + name))
            sems.append(s)
            return s

        HI = GROUPS * PER
        loI, hiI, lowI = sb("loI", [P, T], I32), sb("hiI", [P, T], I32), sb("lowI", [P, T], I32)
        lo, hi = sb("lo", [P, T]), sb("hi", [P, T])
        iotaI, iota = sb("iotaI", [P, HI], I32), sb("iota", [P, HI], F16)
        oh_lo, oh_hi = sb("oh_lo", [P, RING, P], F16), sb("oh_hi", [P, RING, HI], F16)
        count = ctx.enter_context(nc.psum_tensor("deg_count", [P, 512], F32))
        deg = sb("deg", [P, HI])
        s_iota, s_v, s_oh, s_mm, s_deg, s_sq = sem("iota"), sem("v"), sem("oh"), sem("mm"), sem("d"), sem("sq")
        with nc.Block() as block:

            @block.gpsimd
            def _(pool):
                pool.iota(iotaI[:, :], pattern=[[1, HI]], base=0, channel_multiplier=0).then_inc(s_iota, 1)

            @block.vector
            def _(v):
                step = Steps(v, s_v)
                src = K["edge_idx"][:, 0:T, 0]
                v.tensor_scalar(loI[:, :], src, 2, P - 1, ALU.logical_shift_right, ALU.bitwise_and)
                v.tensor_scalar(hiI[:, :], src, 9, 2, ALU.logical_shift_right, ALU.logical_shift_left)
                step(v.tensor_scalar(lowI[:, :], src, 3, None, ALU.bitwise_and))
                v.tensor_copy(lo[:, :], loI[:, :])
                v.tensor_tensor(hi[:, :], hiI[:, :], lowI[:, :], ALU.add)
                v.wait_ge(s_iota, 1)
                step(v.tensor_copy(iota[:, :], iotaI[:, :]))

                def one_hot(k, t):
                    v.tensor_scalar(oh_lo[:, k, :], iota[:, 0:P], lo[:, t], None, ALU.is_equal)
                    v.tensor_scalar(oh_hi[:, k, :], iota[:, :], hi[:, t], None, ALU.is_equal).then_inc(s_oh, 1)

                for k in range(RING):
                    one_hot(k, slice(k, k + 1))
                with v.Fori(1, ITERS) as i:
                    for k in range(RING):
                        v.wait_ge(s_mm, i * RING + (k + 1 - RING))
                        one_hot(k, bass.ds(i * RING + k, 1))
                v.wait_ge(s_mm, T)
                v.tensor_scalar(deg[:, :], count[:, 0:HI], 1.0, None, ALU.max).then_inc(s_deg, 1)
                v.wait_ge(s_sq, 1)
                v.reciprocal(K["isq_out"][:, :], deg[:, :]).then_inc(s_deg, 1)

            @block.tensor
            def _(pe):
                for k in range(RING):
                    pe.wait_ge(s_oh, k + 1)
                    pe.matmul(count[:, 0:HI], oh_lo[:, k, :], oh_hi[:, k, :], start=(k == 0), stop=False,
                              skip_group_check=True).then_inc(s_mm, 1)
                with pe.Fori(1, ITERS) as i:
                    for k in range(RING):
                        pe.wait_ge(s_oh, i * RING + (k + 1))
                        pe.matmul(count[:, 0:HI], oh_lo[:, k, :], oh_hi[:, k, :], start=False, stop=False,
                                  skip_group_check=True).then_inc(s_mm, 1)

            @block.scalar
            def _(act):
                act.wait_ge(s_deg, 1)
                act.activation(deg[:, :], deg[:, :], ACT.Sqrt).then_inc(s_sq, 1)


def turns(eng, count, ring, stages, step=None, per=0):
    lags = max(lag for _, lag in stages)
    peel = -(-lags // ring)

    def whole(i, k, edge):
        for f, lag in stages:
            back, slot = divmod(k - lag, ring)
            if not edge or 0 <= ring * (i + back) + slot < count:
                f(i + back, slot)

    for i in range(peel):
        for k in range(ring):
            whole(i, k, True)
    with eng.Fori(peel, count // ring) as i:
        if step:
            step.loop(i - peel, per * ring)
        for k in range(ring):
            whole(i, k, False)
    if step:
        step.done(count // ring - peel)
    for i in range(count // ring, -(-(count + lags) // ring)):
        for k in range(ring):
            whole(i, k, True)


def prime(eng, *sems):
    for s in sems:
        eng.sem_inc(s, RG)


def upto(i, k, before=0):
    return RG * i + (k + 1 + RG - before)


def half_upto(i, k, half, before=0):
    return 2 * RG * i + (2 * k + half + 1 + 2 * RG - 2 * before)


def gather(pool, dst, table, idx):
    return pool.indirect_dma_start(dst, None, table, bass.IndirectOffsetOnAxis(idx, 0))


def next_index(K, i, k):
    return K["edge_idx"][:, bass.ds(i * RING + (k + RING), 1), :].rearrange("p a b -> p (a b)")


def scatter_add(pool, table, idx, src):
    return pool.indirect_dma_start(table, bass.IndirectOffsetOnAxis(idx, 0), src, None, compute_op=ALU.add)


def edges(nc, K, tag, table, weight, target):
    gated = tag == "e0"
    X = D if gated else 0
    W = D + 1 if gated else D
    with phase(nc) as (ctx, sems):
        def sb(name, shape, dt=F32):
            return ctx.enter_context(nc.sbuf_tensor(f"{tag}_{name}", shape, dt))

        def sem(name):
            s = ctx.enter_context(nc.semaphore(f"{tag}_{name}"))
            sems.append(s)
            return s

        prime_tile = sb("prime", [P, RING, 4])
        slot, out_slot = sb("slot", [P, RING, 2], I32), sb("oslot", [P, RING, 1], I32)
        xs = sb("xs", [P, RING, X + W])
        m, acc = sb("m", [P, RING, W]), sb("acc", [P, RING, W])
        accT, res = sb("accT", [D, RING, P]), sb("res", [P, RING, D])
        fin = sb("fin", [P, D])
        junk, logit, att = sb("junk", [P, RING, 2 * D]), sb("logit", [P, RING]), sb("attv", [P, RING])
        psT = ctx.enter_context(nc.psum_tensor(f"{tag}_psT", [P, 2, 512], F32))
        psY = ctx.enter_context(nc.psum_tensor(f"{tag}_psY", [P, RING, 512], F32))
        psF = ctx.enter_context(nc.psum_tensor(f"{tag}_psF", [P, 512], F32))
        s_got = [K["dma_sem"](f"{tag}_got{k}") for k in range(RING)]
        s_put = [K["dma_sem"](f"{tag}_put{k}") for k in range(RING)]
        s_finput = K["dma_sem"](f"{tag}_finput")
        s_slot = sem("slot")
        s_oslot = sem("oslot")
        s_logit, s_att = sem("logit"), sem("att_s")
        s_walk, s_turn, s_evac = sem("walk"), sem("turn"), sem("evac")
        s_mm, s_res = sem("mm"), sem("res")
        s_fin, s_finp, s_go, s_v = sem("fin"), sem("finp"), sem("go"), sem("v")
        tile_count = 32 if gated else 16

        with nc.Block() as block:

            @block.gpsimd
            def _(pool):
                def fetch(i, k):
                    pool.wait_ge(s_slot, i * RING + (k + 1))
                    pool.sem_inc(s_go, 1)
                    if gated:
                        gather(pool, xs[:, k, 0:X], table, slot[:, k, 1:2]).then_inc(s_got[k], 16)
                    gather(pool, xs[:, k, X:X + D], table, slot[:, k, 0:1]).then_inc(s_got[k], 16)

                def put(i, k):
                    pool.wait_ge(s_oslot, i * RING + (k + 1))
                    pool.wait_ge(s_res, upto(i, k))
                    pool.sem_inc(s_go, 1)
                    scatter_add(pool, target, out_slot[:, k, :], res[:, k, :]).then_inc(s_put[k], 16)

                for k in range(RING):
                    pool.dma_start(prime_tile[:, k, :], K["x"][0:P, 0:4]).then_inc(s_put[k], 16)
                turns(pool, T, RING, [(fetch, 0), (put, RING)])
                for k in range(RING):
                    pool.wait_ge(s_put[k], 16 * (ITERS + 1))
                pool.wait_ge(s_fin, 1)
                scatter_add(pool, target, K["fin_idx"][:, :], fin[:, :]).then_inc(s_finput, 16)
                pool.wait_ge(s_finput, 16)

            @block.vector
            def _(v):
                step = Steps(v, s_v)

                def dot(i, k):
                    v.wait_ge(s_got[k], tile_count * i + tile_count)
                    v.tensor_tensor_reduce(junk[:, k, :], xs[:, k, 0:2 * D], K["att"][:, :], 1.0, 0.0, ALU.mult, ALU.add,
                                           logit[:, k:k + 1]).then_inc(s_logit, 1)

                def walk(i, k):
                    message = m[:, k, :] if gated else xs[:, k, :]
                    if gated:
                        v.wait_ge(s_att, upto(i, k))
                        step(v.tensor_scalar(message, xs[:, k, X:X + W], att[:, k:k + 1], None, ALU.mult))
                        v.wait_ge(s_res, upto(i, k, RING))
                    else:
                        v.wait_ge(s_got[k], tile_count * i + tile_count)
                    v.wait_ge(s_turn, upto(i, k, RING))
                    v.wait_ge(s_walk, upto(i, k, 1))
                    v.scalar_tensor_tensor(acc[:, k, :], acc[:, (k - 1) % RING, :], K["cont"][:, bass.ds(i * RING + k, 1)],
                                           message, ALU.mult, ALU.add).then_inc(s_walk, 1)
                    v.tensor_copy(slot[:, k, :], next_index(K, i, k)).then_inc(s_slot, 1)

                def result(i, k):
                    v.wait_ge(s_mm, upto(i, k))
                    v.wait_ge(s_put[k], 16 * i + 16)
                    v.scalar_tensor_tensor(res[:, k, :], K["bmsg"][:, :], acc[:, k, D:W], psY[:, k, 0:D],
                                           ALU.mult, ALU.add).then_inc(s_res, 1)

                v.tensor_copy(slot[:, :, :], K["edge_idx"][:, 0:RING, :]).then_inc(s_slot, RING)
                if gated:
                    v.memset(xs[:, :, X + D:X + W], 1.0)
                step(v.memset(acc[:, RING - 1, :], 0.0))
                prime(v, s_walk)
                turns(v, T, RING, [(dot, 0), (walk, 1), (result, 3)] if gated else [(walk, 0)], step, int(gated))
                v.wait_ge(s_finp, 1)
                v.tensor_copy(fin[:, :], psF[:, 0:D]).then_inc(s_fin, 1)

            @block.tensor
            def _(pe):
                def turn(i, k):
                    pe.wait_ge(s_walk, upto(i, k))
                    pe.wait_ge(s_evac, upto(i, k, 2))
                    pe.transpose(psT[:, k % 2, 0:P], acc[:, k, 0:D], K["ident"][:, :]).then_inc(s_turn, 1)

                def product(i, k):
                    pe.wait_ge(s_evac, upto(i, k))
                    pe.wait_ge(s_res, upto(i, k, RING))
                    pe.matmul(psY[:, k, 0:D], accT[:, k, :], weight[:, :], start=True, stop=True).then_inc(s_mm, 1)

                prime(pe, s_turn, s_mm)
                turns(pe, T, RING, [(turn, 0), (product, 1)])
                pe.wait_ge(s_res, T + RING)
                pe.matmul(psF[:, 0:D], K["LL"][:, :], res[:, RING - 1, :], start=True, stop=True).then_inc(s_finp, 1)

            @block.scalar
            def _(act):
                def gate(i, k):
                    act.wait_ge(s_logit, i * RING + (k + 1))
                    act.activation(att[:, k:k + 1], logit[:, k:k + 1], ACT.Sigmoid, bias=K["batt"][:, 0:1]).then_inc(s_att, 1)

                def take(i, k):
                    act.wait_ge(s_turn, upto(i, k))
                    act.wait_ge(s_mm, upto(i, k, RING))
                    act.copy(accT[:, k, :], psT[:, k % 2, 0:P]).then_inc(s_evac, 1)
                    act.wait_ge(s_put[k], 16 * i + 16)
                    act.copy(out_slot[:, k, :], K["scat_idx"][:, bass.ds(i * RING + k, 1)]).then_inc(s_oslot, 1)

                def result(i, k):
                    act.wait_ge(s_mm, upto(i, k))
                    act.wait_ge(s_put[k], 16 * i + 16)
                    if tag == "e1":
                        act.copy(res[:, k, :], psY[:, k, 0:D]).then_inc(s_res, 1)
                    else:
                        act.activation(res[:, k, :], psY[:, k, 0:D], ACT.Copy,
                                       scale=K["isq_in"][:, bass.ds(i * RING + k, 1)]).then_inc(s_res, 1)

                prime(act, s_evac, s_res, s_att)
                turns(act, T, RING, [(gate, 0), (take, 2)] if gated else [(take, 0), (result, 2)])


def gru(nc, A, K):
    with phase(nc) as (ctx, sems):
        def sb(name, shape, dt=F32):
            return ctx.enter_context(nc.sbuf_tensor("gru_" + name, shape, dt))

        def ps(name, ring=1):
            return ctx.enter_context(nc.psum_tensor("gru_" + name, [P, ring, GROUP], F32))

        def sem(name):
            s = ctx.enter_context(nc.semaphore("gru_" + name))
            sems.append(s)
            return s

        x, agg = sb("x", [P, RG, PER, D]), sb("agg", [P, RG, PER, D])
        xT, aT = sb("xT", [D, RG, GROUP]), sb("aT", [D, RG, GROUP])
        r, z, n, t, h = (sb(c, [D, RG, GROUP]) for c in "rznth")
        pxT, paT = ps("pxT", 2), ps("paT", 2)
        pr, pz, pi, ph = (ps(c) for c in ("pr", "pz", "pi", "ph"))
        mv = sb("mv", [D, 2])
        sd = sb("sd", [D, 2])
        s_ld = [sem(f"ld{b}") for b in range(RG)]
        s_st = [sem(f"st{b}") for b in range(RG)]
        s_turn = sem("turn")
        s_xT, s_aT = sem("xT"), sem("aT")
        s_mr, s_mz, s_mi = sem("mr"), sem("mz"), sem("mi")
        s_r, s_z = sem("r"), sem("z")
        s_n = sem("n")
        s_t = sem("t")
        s_h = sem("h")
        s_v, s_var, s_sd = sem("v"), sem("var"), sem("sd")
        with nc.Block() as block:
            xg, ag = grouped(A["x"]), grouped(K["agg0"])
            hg = K["hT"].rearrange("d (g n) -> g d n", g=GROUPS)

            @block.sync
            def _(sp):
                def load(i, b):
                    sp.wait_ge(s_turn, upto(i, b, RG))
                    sp.dma_start(flat(x[:, b]), xg[RG * i + b]).then_inc(s_ld[b], 16)
                    sp.dma_start(flat(agg[:, b]), ag[RG * i + b]).then_inc(s_ld[b], 16)

                def store(i, b):
                    sp.wait_ge(s_h, upto(i, b))
                    sp.dma_start(hg[RG * i + b], h[:, b]).then_inc(s_st[b], 16)

                for b in range(RG):
                    sp.sem_inc(s_st[b], 16)
                turns(sp, GROUPS, RG, [(load, 0), (store, 4)])
                stored(sp, s_st)

            @block.tensor
            def _(pe):
                def turn(i, b):
                    pe.wait_ge(s_ld[b], 32 * i + 32)
                    pe.wait_ge(s_xT, upto(i, b, 2))
                    pe.wait_ge(s_aT, upto(i, b, 2))
                    for j in range(PER):
                        pe.transpose(pxT[:, b % 2, j * P:(j + 1) * P], x[:, b, j, :], K["ident"][:, :])
                        last = pe.transpose(paT[:, b % 2, j * P:(j + 1) * P], agg[:, b, j, :], K["ident"][:, :])
                    last.then_inc(s_turn, 1)

                def product(i, b):
                    pe.wait_ge(s_xT, upto(i, b))
                    pe.wait_ge(s_aT, upto(i, b))
                    for c, p, free, done in ((0, pr, s_r, s_mr), (1, pz, s_z, s_mz)):
                        pe.wait_ge(free, upto(i, b, 1))
                        pe.matmul(p[:, 0, :], K["wih"][:, c * D:(c + 1) * D], aT[:, b, :], start=True, stop=False)
                        pe.matmul(p[:, 0, :], K["whh"][:, c * D:(c + 1) * D], xT[:, b, :], start=False,
                                  stop=True).then_inc(done, 1)
                    pe.wait_ge(s_t, upto(i, b, 1))
                    pe.matmul(ph[:, 0, :], K["whh"][:, 2 * D:3 * D], xT[:, b, :], start=True, stop=True)
                    pe.matmul(pi[:, 0, :], K["wih"][:, 2 * D:3 * D], aT[:, b, :], start=True, stop=True).then_inc(s_mi, 1)

                prime(pe, s_turn, s_mr, s_mz, s_mi)
                turns(pe, GROUPS, RG, [(turn, 0), (product, 1)])

            @block.scalar
            def _(act):
                def take(i, b):
                    act.wait_ge(s_turn, upto(i, b))
                    act.wait_ge(s_h, upto(i, b, RG))
                    act.copy(xT[:, b, :], pxT[:, b % 2, :]).then_inc(s_xT, 1)

                def gates(i, b):
                    act.wait_ge(s_mr, upto(i, b))
                    act.activation(r[:, b, :], pr[:, 0, :], ACT.Sigmoid, bias=K["brz"][:, 0:1]).then_inc(s_r, 1)
                    act.wait_ge(s_mz, upto(i, b))
                    act.activation(z[:, b, :], pz[:, 0, :], ACT.Sigmoid, bias=K["brz"][:, 1:2]).then_inc(s_z, 1)

                def tanh(i, b):
                    act.wait_ge(s_t, upto(i, b))
                    act.activation(n[:, b, :], t[:, b, :], ACT.Tanh, bias=K["brz"][:, 2:3]).then_inc(s_n, 1)

                prime(act, s_xT, s_r, s_z, s_n)
                turns(act, GROUPS, RG, [(take, 0), (gates, 1), (tanh, 1)])
                act.wait_ge(s_var, 1)
                act.activation(sd[:, 0:1], mv[:, 1:2], ACT.Sqrt, bias=K["eps"][:, 0:1]).then_inc(s_sd, 1)

            @block.vector
            def _(v):
                step = Steps(v, s_v)

                def take(i, b):
                    v.wait_ge(s_turn, upto(i, b))
                    v.tensor_copy(aT[:, b, :], paT[:, b % 2, :]).then_inc(s_aT, 1)

                def argument(i, b):
                    v.wait_ge(s_mi, upto(i, b))
                    v.wait_ge(s_r, upto(i, b))
                    step(v.scalar_tensor_tensor(t[:, b, :], ph[:, 0, :], K["brz"][:, 3:4], r[:, b, :], ALU.add, ALU.mult))
                    v.tensor_tensor(t[:, b, :], t[:, b, :], pi[:, 0, :], ALU.add).then_inc(s_t, 1)

                def state(i, b):
                    v.wait_ge(s_n, upto(i, b))
                    step(v.tensor_tensor(r[:, b, :], xT[:, b, :], n[:, b, :], ALU.subtract))
                    v.wait_ge(s_z, upto(i, b))
                    step(v.tensor_tensor(r[:, b, :], r[:, b, :], z[:, b, :], ALU.mult))
                    v.wait_ge(s_st[b], 16 * i + 16)
                    v.tensor_tensor(h[:, b, :], r[:, b, :], n[:, b, :], ALU.add).then_inc(s_h, 1)

                def stats(i, b):
                    v.wait_ge(s_h, upto(i, b))
                    v.bn_stats(K["stats"][:, g_slot(i, b), :].rearrange("p a b -> p (a b)"), h[:, b, :])

                prime(v, s_aT, s_t, s_h)
                turns(v, GROUPS, RG, [(argument, 1), (take, 0), (state, 1), (stats, 1)], step, 3)
                v.drain()
                valid = h[:, (GROUPS - 1) % RG, :].rearrange("d (j p) -> d j p", j=PER)[:, :, 0:LAST_VALID]
                step(v.bn_stats(K["stats"][:, GROUPS - 1, :], valid))
                v.bn_aggr(mv[:, :], K["stats"][:, :, :].rearrange("p a b -> p (a b)")).then_inc(s_var, 1)
                v.wait_ge(s_sd, 1)
                step(v.reciprocal(sd[:, 1:2], sd[:, 0:1]))
                step(v.tensor_tensor(K["bnss"][:, 0:1], sd[:, 1:2], K["bn"][:, 0:1], ALU.mult))
                step(v.tensor_tensor(mv[:, 0:1], mv[:, 0:1], K["bnss"][:, 0:1], ALU.mult))
                step(v.tensor_tensor(K["bnss"][:, 1:2], K["bn"][:, 1:2], mv[:, 0:1], ALU.subtract))


def g_slot(i, b):
    return bass.ds(RG * i + b, 1)


class Norm:

    def __init__(self, sb, sem, tag):
        self.st, self.mv = sb(tag + "st", [P, RG, PER, 6]), sb(tag + "mv", [P, RG, PER, 2])
        self.sd, self.rs = sb(tag + "sd", [P, RG, PER]), sb(tag + "rs", [P, RG, PER])
        self.s_mv, self.s_sd, self.s_gate = sem(tag + "mv"), sem(tag + "sd"), sem(tag + "gate")

    def stats(self, v, step, b, u):
        for j in range(PER):
            last = v.bn_stats(self.st[:, b, j, :], u[:, j, :])
        step(last)
        v.sem_inc(self.s_gate, 1)
        for j in range(PER):
            last = v.bn_aggr(self.mv[:, b, j, :], self.st[:, b, j, :])
        last.then_inc(self.s_mv, 1)

    def root(self, act, K, i, b):
        act.wait_ge(self.s_mv, upto(i, b))
        act.activation(self.sd[:, b, :], self.mv[:, b, :, 1], ACT.Sqrt, bias=K["eps"][:, 0:1]).then_inc(self.s_sd, 1)

    def rows(self, v, step, i, b, out, u):
        v.wait_ge(self.s_sd, upto(i, b))
        step(v.reciprocal(self.rs[:, b, :], self.sd[:, b, :]))
        for j in range(PER):
            last = v.tensor_scalar(out[:, j, :], u[:, j, :], self.mv[:, b, j, 0:1], self.rs[:, b, j:j + 1],
                                   ALU.subtract, ALU.mult)
        return last


def last_half(i, k):
    return half_upto(i, k, 1)


def stored(sp, s_st):
    for b in range(RG):
        sp.wait_ge(s_st[b], 16 * (len(range(b, GROUPS, RG)) + 1))


def stream(sp, s_ld, s_used, loads, stores):
    def load(i, b):
        sp.wait_ge(s_used, upto(i, b, RG))
        for f in loads:
            f(RG * i + b, b).then_inc(s_ld[b], 16)

    stages = [(load, 0)]
    for lag, s_ready, value, s_st, f in stores:
        def store(i, b, s_ready=s_ready, value=value, s_st=s_st, f=f):
            sp.wait_ge(s_ready, value(i, b))
            f(RG * i + b, b).then_inc(s_st[b], 16)

        for b in range(RG):
            sp.sem_inc(s_st[b], 16)
        stages.append((store, lag))
    turns(sp, GROUPS, RG, stages)
    for _, _, _, s_st, _ in stores:
        stored(sp, s_st)


def flat(ap):
    return ap.rearrange("p j d -> p (j d)")


def rows_of(ap, n=PER):
    return ap.unsqueeze(1).to_broadcast([P, n, ap.shape[1]])


def norm0(nc, A, K):
    with phase(nc) as (ctx, sems):
        def sb(name, shape, dt=F32):
            return ctx.enter_context(nc.sbuf_tensor("n0_" + name, shape, dt))

        def sem(name):
            s = ctx.enter_context(nc.semaphore("n0_" + name))
            sems.append(s)
            return s

        x, hT, bT = sb("x", [P, RG, PER, D]), sb("hT", [D, RG, GROUP]), sb("bT", [D, RG, GROUP])
        u, y = sb("u", [P, RG, PER, D]), sb("y", [P, RG, PER, D])
        pb = ctx.enter_context(nc.psum_tensor("n0_pb", [P, 2, PER, D], F32))
        norm = Norm(sb, sem, "")
        s_ld, s_st = [sem(f"ld{b}") for b in range(RG)], [sem(f"st{b}") for b in range(RG)]
        s_bT = sem("bT")
        s_turn = sem("turn")
        s_sum = sem("sum")
        s_done = sem("done")
        s_v = sem("v")
        with nc.Block() as block:
            xg, yg = grouped(A["x"]), grouped(K["x1"])
            hg = K["hT"].rearrange("d (g n) -> g d n", g=GROUPS)

            @block.sync
            def _(sp):
                stream(sp, s_ld, s_sum,
                       [lambda g, b: sp.dma_start(flat(x[:, b]), xg[g]), lambda g, b: sp.dma_start(hT[:, b], hg[g])],
                       [(3, s_done, upto, s_st, lambda g, b: sp.dma_start(yg[g], flat(y[:, b])))])

            @block.scalar
            def _(act):
                def affine(i, b):
                    act.wait_ge(s_ld[b], 32 * i + 32)
                    act.wait_ge(s_turn, upto(i, b, RG))
                    act.activation(bT[:, b, :], hT[:, b, :], ACT.Identity, scale=K["bnss"][:, 0:1],
                                   bias=K["bnss"][:, 1:2]).then_inc(s_bT, 1)

                prime(act, s_bT, norm.s_sd)
                turns(act, GROUPS, RG, [(affine, 0), (lambda i, b: norm.root(act, K, i, b), 1)])

            @block.tensor
            def _(pe):
                def turn(i, b):
                    pe.wait_ge(s_bT, upto(i, b))
                    pe.wait_ge(s_sum, upto(i, b, 2))
                    for j in range(PER):
                        last = pe.transpose(pb[:, b % 2, j, :], bT[:, b, j * P:(j + 1) * P], K["ident"][:, :])
                    last.then_inc(s_turn, 1)

                prime(pe, s_turn)
                turns(pe, GROUPS, RG, [(turn, 0)])

            @block.vector
            def _(v):
                step = Steps(v, s_v)

                def total(i, b):
                    v.wait_ge(s_ld[b], 32 * i + 32)
                    v.wait_ge(s_turn, upto(i, b))
                    v.wait_ge(s_done, upto(i, b, RG))
                    v.tensor_tensor(u[:, b], pb[:, b % 2], x[:, b], ALU.add).then_inc(s_sum, 1)
                    v.wait_ge(s_sum, upto(i, b))
                    norm.stats(v, step, b, u[:, b])

                def rows(i, b):
                    v.wait_ge(s_st[b], 16 * i + 16)
                    norm.rows(v, step, i, b, y[:, b], u[:, b]).then_inc(s_done, 1)

                prime(v, s_sum, s_done, norm.s_mv)
                turns(v, GROUPS, RG, [(total, 0), (rows, 1)], step, 2)


def dense1(nc, K):
    with phase(nc) as (ctx, sems):
        def sb(name, shape, dt=F32):
            return ctx.enter_context(nc.sbuf_tensor("d1_" + name, shape, dt))

        def sem(name):
            s = ctx.enter_context(nc.semaphore("d1_" + name))
            sems.append(s)
            return s

        x, agg = sb("x", [P, RG, PER, D]), sb("agg", [P, RG, PER, D])
        u, x2, w = sb("u", [P, RG, PER, D]), sb("x2", [P, RG, PER, D]), sb("w", [P, RG, PER, D])
        hn, msg, hT = sb("hn", [P, RG, PER, D]), sb("msg", [P, RG, PER, D]), sb("hT", [D, RG, GROUP])
        prod, pre = sb("prod", [P, RG, PER, D]), sb("pre", [P, RG, PER, D])
        pT = ctx.enter_context(nc.psum_tensor("d1_pT", [P, 2, GROUP], F32))
        pP = ctx.enter_context(nc.psum_tensor("d1_pP", [P, 2, PER, D], F32))
        na, nb = Norm(sb, sem, "a"), Norm(sb, sem, "b")
        s_ld = [sem(f"ld{b}") for b in range(RG)]
        s_stm, s_stp = ([sem(f"st{c}{b}") for b in range(RG)] for c in "mp")
        s_used = sem("used")
        s_w = sem("w")
        s_hn = sem("hn")
        s_msg = sem("msg")
        s_turn, s_hT = sem("turn"), sem("hT")
        s_mm, s_prod = sem("mm"), sem("prod")
        s_done = sem("done")
        s_v, s_g = sem("v"), sem("g")
        with nc.Block() as block:
            xg, ag, mg, pg = (grouped(K[t]) for t in ("x1", "agg1", "msg", "pre2"))

            @block.sync
            def _(sp):
                stream(sp, s_ld, s_used,
                       [lambda g, b: sp.dma_start(flat(x[:, b]), xg[g]), lambda g, b: sp.dma_start(flat(agg[:, b]), ag[g])],
                       [(4, s_msg, upto, s_stm, lambda g, b: sp.dma_start(mg[g], flat(msg[:, b]))),
                        (4, s_done, upto, s_stp, lambda g, b: sp.dma_start(pg[g], flat(pre[:, b])))])

            @block.vector
            def _(v):
                step = Steps(v, s_v)

                def total(i, b):
                    v.wait_ge(s_ld[b], 32 * i + 32)
                    step(v.tensor_tensor(u[:, b], agg[:, b], rows_of(K["b1"][:, :]), ALU.add))
                    ins = v.scalar_tensor_tensor(flat(u[:, b]), flat(u[:, b]), 0.0, flat(x[:, b]), ALU.max, ALU.add)
                    ins.then_inc(s_used, 1)
                    v.wait_ge(s_used, upto(i, b))
                    na.stats(v, step, b, u[:, b])

                def first(i, b):
                    v.wait_ge(s_done, upto(i, b, RG))
                    step(na.rows(v, step, i, b, x2[:, b], u[:, b]))
                    nb.stats(v, step, b, x2[:, b])

                def second(i, b):
                    nb.rows(v, step, i, b, w[:, b], x2[:, b]).then_inc(s_w, 1)

                def messages(i, b):
                    v.wait_ge(s_hn, upto(i, b))
                    v.wait_ge(s_stm[b], 16 * i + 16)
                    for j in range(PER):
                        last = v.tensor_scalar(msg[:, b, j, :], hn[:, b, j, :],
                                               K["isq_out"][:, bass.ds(PER * RG * i + (PER * b + j), 1)], None, ALU.mult)
                    last.then_inc(s_msg, 1)

                prime(v, s_msg, s_used, s_w, na.s_mv, nb.s_mv)
                turns(v, GROUPS, RG, [(total, 0), (first, 1), (messages, 2), (second, 1)], step, 6)

            @block.gpsimd
            def _(g):
                step = Steps(g, s_g)

                def affine(i, b):
                    g.wait_ge(s_w, upto(i, b))
                    step(g.tensor_tensor(w[:, b], w[:, b], rows_of(K["ln_g"][:, :]), ALU.mult))
                    g.wait_ge(s_turn, upto(i, b, RG))
                    g.wait_ge(s_msg, upto(i, b, RG))
                    g.tensor_tensor(hn[:, b], w[:, b], rows_of(K["ln_b"][:, :]), ALU.add).then_inc(s_hn, 1)
                    step(g.tensor_tensor(x2[:, b], x2[:, b], rows_of(K["b2"][:, :]), ALU.add))

                def total(i, b):
                    g.wait_ge(s_prod, upto(i, b))
                    g.wait_ge(s_stp[b], 16 * i + 16)
                    g.tensor_tensor(pre[:, b], prod[:, b], x2[:, b], ALU.add).then_inc(s_done, 1)

                prime(g, s_done, s_hn)
                turns(g, GROUPS, RG, [(affine, 0), (total, 1)], step, 2)

            @block.tensor
            def _(pe):
                def turn(i, b):
                    pe.wait_ge(s_hn, upto(i, b))
                    pe.wait_ge(s_hT, upto(i, b, 2))
                    for j in range(PER):
                        last = pe.transpose(pT[:, b % 2, j * P:(j + 1) * P], hn[:, b, j, :], K["ident"][:, :])
                    last.then_inc(s_turn, 1)

                def product(i, b):
                    pe.wait_ge(s_hT, upto(i, b))
                    pe.wait_ge(s_prod, upto(i, b, 2))
                    for j in range(PER):
                        last = pe.matmul(pP[:, b % 2, j, :], hT[:, b, j * P:(j + 1) * P], K["w2a"][:, :], start=True, stop=True)
                    last.then_inc(s_mm, 1)

                prime(pe, s_turn, s_mm)
                turns(pe, GROUPS, RG, [(turn, 0), (product, 1)])

            @block.scalar
            def _(act):
                def take(i, b):
                    act.wait_ge(s_turn, upto(i, b))
                    act.wait_ge(s_mm, upto(i, b, RG))
                    act.copy(hT[:, b, :], pT[:, b % 2, :]).then_inc(s_hT, 1)

                def product(i, b):
                    act.wait_ge(s_mm, upto(i, b))
                    act.wait_ge(s_done, upto(i, b, RG))
                    act.copy(prod[:, b], pP[:, b % 2]).then_inc(s_prod, 1)

                prime(act, s_hT, s_prod, na.s_sd, nb.s_sd)
                turns(act, GROUPS, RG, [(product, 3), (lambda i, b: na.root(act, K, i, b), 0), (take, 2),
                                       (lambda i, b: nb.root(act, K, i, b), 1)])


def dense2(nc, K):
    W = HC + 2 * H1
    with phase(nc) as (ctx, sems):
        def sb(name, shape, dt=F32):
            return ctx.enter_context(nc.sbuf_tensor("d2_" + name, shape, dt))

        def sem(name):
            s = ctx.enter_context(nc.semaphore("d2_" + name))
            sems.append(s)
            return s

        u, x3, xT = sb("u", [P, RG, PER, D]), sb("x3", [P, RG, PER, D]), sb("xT", [D, RG, GROUP])
        pre, sc = sb("pre", [P, RG, PER, HC]), sb("sc", [P, RG, PER, 2 * H1])
        pT = ctx.enter_context(nc.psum_tensor("d2_pT", [P, 2, GROUP], F32))
        pP = ctx.enter_context(nc.psum_tensor("d2_pP", [P, PER, 512], F32))
        norm = Norm(sb, sem, "")
        s_ld = [sem(f"ld{b}") for b in range(RG)]
        s_stx, s_stp, s_sts = ([sem(f"st{c}{b}") for b in range(RG)] for c in "xps")
        s_x3 = sem("x3")
        s_turn, s_xT = sem("turn"), sem("xT")
        s_mm, s_half = sem("mm"), sem("half")
        s_v = sem("v")
        with nc.Block() as block:
            pg, xg, og, sg = (grouped(K[t]) for t in ("pre2", "x3", "pre3", "sc3"))

            @block.sync
            def _(sp):
                stream(sp, s_ld, s_x3,
                       [lambda g, b: sp.dma_start(flat(u[:, b]), pg[g])],
                       [(3, s_x3, upto, s_stx, lambda g, b: sp.dma_start(xg[g], flat(x3[:, b]))),
                        (4, s_half, last_half, s_stp, lambda g, b: sp.dma_start(og[g], flat(pre[:, b]))),
                        (4, s_half, last_half, s_sts, lambda g, b: sp.dma_start(sg[g], flat(sc[:, b])))])

            @block.vector
            def _(v):
                step = Steps(v, s_v)

                def stats(i, b):
                    v.wait_ge(s_ld[b], 16 * i + 16)
                    norm.stats(v, step, b, u[:, b])

                def rows(i, b):
                    v.wait_ge(s_stx[b], 16 * i + 16)
                    norm.rows(v, step, i, b, x3[:, b], u[:, b]).then_inc(s_x3, 1)

                def product(i, b):
                    v.wait_ge(s_stp[b], 16 * i + 16)
                    v.wait_ge(s_sts[b], 16 * i + 16)
                    for half in range(2):
                        v.wait_ge(s_mm, half_upto(i, b, half))
                        js = slice(half * PER // 2, (half + 1) * PER // 2)
                        v.tensor_copy(sc[:, b, js], pP[:, js, HC:W])
                        v.tensor_tensor(pre[:, b, js], pP[:, js, 0:HC], rows_of(K["g1b"][:, :], PER // 2), ALU.add).then_inc(s_half, 1)

                prime(v, s_x3, norm.s_mv)
                v.sem_inc(s_half, 2 * RG)
                turns(v, GROUPS, RG, [(stats, 0), (rows, 1), (product, 3)], step, 2)

            @block.tensor
            def _(pe):
                def turn(i, b):
                    pe.wait_ge(s_x3, upto(i, b))
                    pe.wait_ge(s_xT, upto(i, b, 2))
                    for j in range(PER):
                        last = pe.transpose(pT[:, b % 2, j * P:(j + 1) * P], x3[:, b, j, :], K["ident"][:, :])
                    last.then_inc(s_turn, 1)

                def product(i, b):
                    pe.wait_ge(s_xT, upto(i, b))
                    for half in range(2):
                        pe.wait_ge(s_half, half_upto(i, b, half, 1))
                        for j in range(half * PER // 2, (half + 1) * PER // 2):
                            last = pe.matmul(pP[:, j, 0:W], xT[:, b, j * P:(j + 1) * P], K["g1d"][:, :], start=True, stop=True)
                        last.then_inc(s_mm, 1)

                prime(pe, s_turn)
                pe.sem_inc(s_mm, 2 * RG)
                turns(pe, GROUPS, RG, [(turn, 0), (product, 1)])

            @block.scalar
            def _(act):
                def take(i, b):
                    act.wait_ge(s_turn, upto(i, b))
                    act.wait_ge(s_half, half_upto(i, b, 1, RG))
                    act.copy(xT[:, b, :], pT[:, b % 2, :]).then_inc(s_xT, 1)

                prime(act, s_xT, norm.s_sd)
                turns(act, GROUPS, RG, [(lambda i, b: norm.root(act, K, i, b), 0), (take, 1)])


def edge_scores(nc, K, n, H, scores, alpha):
    with phase(nc) as (ctx, sems):
        def sb(name, shape, dt=F32):
            return ctx.enter_context(nc.sbuf_tensor(f"es{n}_{name}", shape, dt))

        def sem(name):
            s = ctx.enter_context(nc.semaphore(f"es{n}_{name}"))
            sems.append(s)
            return s

        slot = sb("slot", [P, RING, 2], I32)
        got = sb("got", [P, RING, 2, 2 * H])
        rows = sb("rows", [P, T, 2, 2 * H])
        s, sf, F, B, M, junk = (sb(c, [P, H, T]) for c in ("s", "self", "F", "B", "M", "junk"))
        bc = sb("bc", [P, 2 * H, P])
        ends = sb("ends", [P, 2, H])
        mx = sb("mx", [P, 4, H])
        pb = ctx.enter_context(nc.psum_tensor(f"es{n}_pb", [P, 2 * H, P], F32))
        pt = ctx.enter_context(nc.psum_tensor(f"es{n}_pt", [P, 2, 512], F32))
        s_got = [K["dma_sem"](f"es{n}_got{k}") for k in range(RING)]
        s_slot, s_v, s_go, s_bc, s_pb, s_ends, s_pt = (sem("slot"), sem("v"), sem("go"), sem("bc"), sem("pb"),
                                                       sem("ends"), sem("pt"))
        s_arg, s_exp = sem("arg"), sem("exp")
        with nc.Block() as block:

            @block.gpsimd
            def _(pool):
                def fetch(i, k):
                    pool.wait_ge(s_slot, i * RING + (k + 1))
                    pool.sem_inc(s_go, 1)
                    for side in range(2):
                        gather(pool, got[:, k, side, :], scores[:, :], slot[:, k, side:side + 1]).then_inc(s_got[k], 16)

                for k in range(RING):
                    fetch(0, k)
                with pool.Fori(1, ITERS) as i:
                    for k in range(RING):
                        fetch(i, k)

            @block.vector
            def _(v):
                v.tensor_copy(slot[:, :, :], K["edge_idx"][:, 0:RING, :]).then_inc(s_slot, RING)
                with v.Fori(0, ITERS) as i:
                    for k in range(RING):
                        v.wait_ge(s_got[k], 32 * i + 32)
                        v.tensor_copy(rows[:, bass.ds(i * RING + k, 1), :, :].rearrange("p t s h -> p (t s h)"),
                                      got[:, k, :, :].rearrange("p s h -> p (s h)"))
                        v.tensor_copy(slot[:, k, :], K["edge_idx"][:, bass.ds(i * RING + (k + RING), 1), :].rearrange("p a b -> p (a b)")).then_inc(s_slot, 1)
                v.wait_ge(s_slot, T + RING)
                step = Steps(v, s_v)

                def part(side, which):
                    return rows[:, :, side, which * H:(which + 1) * H].rearrange("p t h -> p h t")

                v.tensor_tensor(s[:, :, :], part(0, 0), part(1, 1), ALU.add)
                step(v.tensor_tensor(sf[:, :, :], part(1, 0), part(1, 1), ALU.add))
                for a in (s, sf):
                    step(v.scalar_tensor_tensor(a[:, :, :], a[:, :, :], 0.2, a[:, :, :], ALU.mult, ALU.max))
                step(v.tensor_tensor(M[:, :, :], s[:, :, :], sf[:, :, :], ALU.max))
                for h in range(H):
                    v.tensor_tensor_scan(F[:, h, :], K["pcont"][:, :], M[:, h, :], -BIG, ALU.add, ALU.max)
                    last = v.tensor_tensor_scan(B[:, h, ::-1], K["pnext"][:, ::-1], M[:, h, ::-1], -BIG, ALU.add, ALU.max)
                step(last)
                for h in range(H):
                    v.tensor_scalar(bc[:, 2 * h, :], K["ones"][:, :], F[:, h, T - 1:T], None, ALU.mult)
                    v.tensor_scalar(bc[:, 2 * h + 1, :], K["ones"][:, :], B[:, h, 0:1], None, ALU.mult).then_inc(s_bc, 1)
                step(v.tensor_tensor(M[:, :, :], F[:, :, :], B[:, :, :], ALU.max))
                v.wait_ge(s_pb, H)
                for h in range(H):
                    for c, (half, pen) in enumerate(((0, "pLF"), (1, "pFF"), (0, "pLL"), (1, "pFL"))):
                        last = v.tensor_tensor_reduce(junk[:, 0, 0:P], pb[:, 2 * h + half, :], K[pen][:, :], 1.0, -BIG,
                                                      ALU.add, ALU.max, mx[:, c, h:h + 1])
                        step(last)
                step(v.tensor_tensor(mx[:, 0, :], mx[:, 0, :], mx[:, 1, :], ALU.max))
                step(v.tensor_tensor(mx[:, 2, :], mx[:, 2, :], mx[:, 3, :], ALU.max))
                for c, pen in ((0, "plead"), (2, "ptrail")):
                    for h in range(H):
                        last = v.scalar_tensor_tensor(M[:, h, :], K[pen][:, :], mx[:, c, h:h + 1], M[:, h, :], ALU.add, ALU.max)
                    step(last)
                v.tensor_tensor(s[:, :, :], s[:, :, :], M[:, :, :], ALU.subtract)
                v.tensor_tensor(sf[:, :, :], sf[:, :, :], M[:, :, :], ALU.subtract).then_inc(s_arg, 1)
                v.wait_ge(s_exp, 1)
                for h in range(H):
                    v.tensor_tensor_scan(F[:, h, :], K["cont"][:, :], s[:, h, :], 0.0, ALU.mult, ALU.add)
                    last = v.tensor_tensor_scan(B[:, h, ::-1], K["cnext"][:, ::-1], s[:, h, ::-1], 0.0, ALU.mult, ALU.add)
                step(last)
                v.tensor_copy(ends[:, 0, :], F[:, :, T - 1])
                v.tensor_scalar(ends[:, 1, :], B[:, :, 0], K["nosingle"][:, 0:1], None, ALU.mult).then_inc(s_ends, 1)
                step(v.tensor_tensor(M[:, :, :], F[:, :, :], B[:, :, :], ALU.add))
                step(v.tensor_tensor(M[:, :, :], M[:, :, :], s[:, :, :], ALU.subtract))
                step(v.tensor_tensor(M[:, :, :], M[:, :, :], K["inner"][:, :].unsqueeze(1).to_broadcast([P, H, T]), ALU.mult))
                v.wait_ge(s_pt, 1)
                step(v.tensor_copy(mx[:, 0:2, :], pt[:, :, 0:H]))
                for c, mask in enumerate(("lead", "trail")):
                    for h in range(H):
                        last = v.scalar_tensor_tensor(M[:, h, :], K[mask][:, :], mx[:, c, h:h + 1], M[:, h, :], ALU.mult, ALU.add)
                    step(last)
                step(v.tensor_tensor(M[:, :, :], M[:, :, :], sf[:, :, :], ALU.add))
                step(v.tensor_scalar(M[:, :, :], M[:, :, :], 1e-16, None, ALU.add))
                step(v.reciprocal(M[:, :, :], M[:, :, :]))
                v.scalar_tensor_tensor(alpha[:, :, :], s[:, :, :], 1.0 / H if n == 2 else 1.0, M[:, :, :], ALU.mult, ALU.mult)

            @block.tensor
            def _(pe):
                for h in range(H):
                    pe.wait_ge(s_bc, h + 1)
                    pe.transpose(pb[:, 2 * h, :], bc[:, 2 * h, :], K["ident"][:, :])
                    pe.transpose(pb[:, 2 * h + 1, :], bc[:, 2 * h + 1, :], K["ident"][:, :]).then_inc(s_pb, 1)
                pe.wait_ge(s_ends, 1)
                pe.matmul(pt[:, 0, 0:H], K["FL"][:, :], ends[:, 0, :], start=True, stop=False)
                pe.matmul(pt[:, 0, 0:H], K["FF"][:, :], ends[:, 1, :], start=False, stop=True)
                pe.matmul(pt[:, 1, 0:H], K["LL"][:, :], ends[:, 0, :], start=True, stop=False)
                pe.matmul(pt[:, 1, 0:H], K["LF"][:, :], ends[:, 1, :], start=False, stop=True).then_inc(s_pt, 1)

            @block.scalar
            def _(act):
                act.wait_ge(s_arg, 1)
                act.activation(s[:, :, :], s[:, :, :], ACT.Exp)
                act.activation(sf[:, :, :], sf[:, :, :], ACT.Exp).then_inc(s_exp, 1)


def edge_messages(nc, K, n, H, KB, weight, table, target, alpha):
    C = C1 if n < 2 else D
    W = H * C
    O = W if n < 2 else D
    with phase(nc) as (ctx, sems):
        def sb(name, shape, dt=F32):
            return ctx.enter_context(nc.sbuf_tensor(f"em{n}_{name}", shape, dt))

        def sem(name):
            s = ctx.enter_context(nc.semaphore(f"em{n}_{name}"))
            sems.append(s)
            return s

        prime_tile = sb("prime", [P, RING, 4])
        slot, out_slot = sb("slot", [P, RING, 2], I32), sb("oslot", [P, RING, 1], I32)
        xs, xd, diff = (sb(c, [P, RING, KB * D]) for c in ("xs", "xd", "diff"))
        dT = sb("dT", [D, RING, KB, P])
        acc, part = sb("acc", [P, RING, O]), sb("part", [P, 2, O])
        fin = sb("fin", [P, O])
        psT = ctx.enter_context(nc.psum_tensor(f"em{n}_psT", [P, 2, 512], F32))
        psY = ctx.enter_context(nc.psum_tensor(f"em{n}_psY", [P, 2, 512 * (-(-W // 512))], F32))
        psF = ctx.enter_context(nc.psum_tensor(f"em{n}_psF", [P, 512], F32))
        s_got = [K["dma_sem"](f"em{n}_got{k}") for k in range(RING)]
        s_put = [K["dma_sem"](f"em{n}_put{k}") for k in range(RING)]
        s_slot, s_go = sem("slot"), sem("go")
        s_diff = sem("diff")
        s_turn = sem("turn")
        s_evac = sem("evac")
        s_mm = sem("mm")
        s_walk = sem("walk")
        s_oslot, s_v = sem("oslot"), sem("v")
        s_fin, s_finp = sem("fin"), sem("finp")
        s_finput = K["dma_sem"](f"em{n}_finput")
        with nc.Block() as block:

            @block.gpsimd
            def _(pool):
                def fetch(i, k):
                    pool.wait_ge(s_slot, i * RING + (k + 1))
                    pool.sem_inc(s_go, 1)
                    gather(pool, xs[:, k, :], table[:, :], slot[:, k, 0:1]).then_inc(s_got[k], 16)
                    gather(pool, xd[:, k, :], table[:, :], slot[:, k, 1:2]).then_inc(s_got[k], 16)

                def put(i, k):
                    pool.wait_ge(s_oslot, i * RING + (k + 1))
                    pool.wait_ge(s_walk, upto(i, k))
                    pool.sem_inc(s_go, 1)
                    scatter_add(pool, target[:, :], out_slot[:, k, :], acc[:, k, :]).then_inc(s_put[k], 16)

                for k in range(RING):
                    pool.dma_start(prime_tile[:, k, :], K["x"][0:P, 0:4]).then_inc(s_put[k], 16)
                turns(pool, T, RING, [(fetch, 0), (put, RING)])
                for k in range(RING):
                    pool.wait_ge(s_put[k], 16 * (ITERS + 1))
                pool.wait_ge(s_fin, 1)
                scatter_add(pool, target[:, :], K["fin_idx"][:, :], fin[:, :]).then_inc(s_finput, 16)
                pool.wait_ge(s_finput, 16)

            @block.vector
            def _(v):
                step = Steps(v, s_v)

                def difference(i, k):
                    v.wait_ge(s_got[k], 32 * i + 32)
                    v.wait_ge(s_turn, upto(i, k, RING))
                    v.tensor_tensor(diff[:, k, :], xs[:, k, :], xd[:, k, :], ALU.subtract).then_inc(s_diff, 1)
                    v.tensor_copy(slot[:, k, :], next_index(K, i, k)).then_inc(s_slot, 1)

                def walk(i, k):
                    t = bass.ds(i * RING + k, 1)
                    v.wait_ge(s_walk, upto(i, k, 1))
                    a, b = part[:, 0, :], part[:, 1, :]
                    step(v.tensor_scalar(a, acc[:, (k - 1) % RING, :], K["cont"][:, t], None, ALU.mult))
                    v.wait_ge(s_put[k], 16 * i + 16)
                    v.wait_ge(s_mm, upto(i, k))
                    for h in range(H):
                        prod = psY[:, k % 2, h * C:(h + 1) * C]
                        scale = alpha[:, h, t]
                        if n < 2:
                            c = slice(h * C, (h + 1) * C)
                            ins = v.scalar_tensor_tensor(acc[:, k, c], prod, scale, a[:, c], ALU.mult, ALU.add)
                        else:
                            o = acc[:, k, :] if h == H - 1 else b
                            ins = v.scalar_tensor_tensor(o, prod, scale, a, ALU.mult, ALU.add)
                            a, b = b, a
                            if h < H - 1:
                                step(ins)
                    ins.then_inc(s_walk, 1)

                v.tensor_copy(slot[:, :, :], K["edge_idx"][:, 0:RING, :]).then_inc(s_slot, RING)
                step(v.memset(acc[:, RING - 1, :], 0.0))
                prime(v, s_walk)
                turns(v, T, RING, [(difference, 0), (walk, 2)], step, 1 if n < 2 else H)
                v.wait_ge(s_finp, 1)
                v.tensor_copy(fin[:, :], psF[:, 0:O]).then_inc(s_fin, 1)

            @block.tensor
            def _(pe):
                def turn(i, k):
                    pe.wait_ge(s_diff, i * RING + (k + 1))
                    pe.wait_ge(s_evac, upto(i, k, 2))
                    for kb in range(KB):
                        last = pe.transpose(psT[:, k % 2, kb * P:(kb + 1) * P], diff[:, k, kb * D:(kb + 1) * D],
                                            K["ident"][:, :])
                    last.then_inc(s_turn, 1)

                def product(i, k):
                    pe.wait_ge(s_evac, upto(i, k))
                    pe.wait_ge(s_walk, upto(i, k, 2))
                    for c0 in range(0, W, 512):
                        c1 = min(W, c0 + 512)
                        for kb in range(KB):
                            rhs = weight[:, c0:c1] if KB == 1 else weight[:, kb, c0:c1]
                            last = pe.matmul(psY[:, k % 2, c0:c1], dT[:, k, kb, :], rhs, start=(kb == 0), stop=(kb == KB - 1))
                    last.then_inc(s_mm, 1)

                prime(pe, s_turn, s_mm)
                turns(pe, T, RING, [(turn, 0), (product, 1)])
                pe.wait_ge(s_walk, T + RING)
                pe.matmul(psF[:, 0:O], K["LL"][:, :], acc[:, RING - 1, :], start=True, stop=True).then_inc(s_finp, 1)

            @block.scalar
            def _(act):
                def take(i, k):
                    act.wait_ge(s_turn, upto(i, k))
                    act.wait_ge(s_mm, upto(i, k, RING))
                    act.copy(dT[:, k].rearrange("d a b -> d (a b)"), psT[:, k % 2, 0:KB * P]).then_inc(s_evac, 1)
                    act.wait_ge(s_put[k], 16 * i + 16)
                    act.copy(out_slot[:, k, :], K["scat_idx"][:, bass.ds(i * RING + k, 1)]).then_inc(s_oslot, 1)

                prime(act, s_evac)
                turns(act, T, RING, [(take, 0)])


def dense_gat(nc, K, n, pre_in, table, weight, bias, pre_out, scores):
    H = (H1, H3)[n]
    O = (HC, D)[n]
    W = O + 2 * H
    with phase(nc) as (ctx, sems):
        def sb(name, shape, dt=F32):
            return ctx.enter_context(nc.sbuf_tensor(f"dg{n}_{name}", shape, dt))

        def sem(name):
            s = ctx.enter_context(nc.semaphore(f"dg{n}_{name}"))
            sems.append(s)
            return s

        x, e, h = (sb(c, [P, RG, PER, HC]) for c in "xeh")
        hT = sb("hT", [D, RG, 2, GROUP])
        pre, sc = sb("pre", [P, RG, PER, O]), sb("sc", [P, RG, PER, 2 * H])
        pT = ctx.enter_context(nc.psum_tensor(f"dg{n}_pT", [P, 2, GROUP], F32))
        pP = ctx.enter_context(nc.psum_tensor(f"dg{n}_pP", [P, PER, 512], F32))
        s_ld = [sem(f"ld{b}") for b in range(RG)]
        s_sth, s_stp, s_sts = ([sem(f"st{c}{b}") for b in range(RG)] for c in "hps")
        s_e = sem("e")
        s_h = sem("h")
        s_turn = sem("turn")
        s_hT = sem("hT")
        s_mm, s_half = sem("mm"), sem("half")
        s_v = sem("v")
        with nc.Block() as block:
            ig, hg, og, sg = grouped(pre_in), grouped(table), grouped(pre_out), grouped(scores)

            @block.sync
            def _(sp):
                stream(sp, s_ld, s_h,
                       [lambda g, b: sp.dma_start(flat(x[:, b]), ig[g])],
                       [(3, s_h, upto, s_sth, lambda g, b: sp.dma_start(hg[g], flat(h[:, b]))),
                        (4, s_half, last_half, s_stp, lambda g, b: sp.dma_start(og[g], flat(pre[:, b]))),
                        (4, s_half, last_half, s_sts, lambda g, b: sp.dma_start(sg[g], flat(sc[:, b])))])

            @block.scalar
            def _(act):
                def exp(i, b):
                    act.wait_ge(s_ld[b], 16 * i + 16)
                    act.wait_ge(s_h, upto(i, b, RG))
                    act.activation(e[:, b], x[:, b], ACT.Exp).then_inc(s_e, 1)

                def take(i, b):
                    act.wait_ge(s_turn, upto(i, b))
                    act.wait_ge(s_mm, half_upto(i, b, 1, RG))
                    act.copy(hT[:, b], pT[:, :, :]).then_inc(s_hT, 1)

                prime(act, s_hT, s_e)
                turns(act, GROUPS, RG, [(exp, 0), (take, 1)])

            @block.vector
            def _(v):
                step = Steps(v, s_v)

                def elu(i, b):
                    v.wait_ge(s_e, upto(i, b))
                    step(v.tensor_scalar(flat(e[:, b]), flat(e[:, b]), 1.0, -1.0, ALU.min, ALU.add))
                    v.wait_ge(s_sth[b], 16 * i + 16)
                    v.wait_ge(s_turn, upto(i, b, RG))
                    v.scalar_tensor_tensor(flat(h[:, b]), flat(x[:, b]), 0.0, flat(e[:, b]), ALU.max, ALU.add).then_inc(s_h, 1)

                def product(i, b):
                    v.wait_ge(s_stp[b], 16 * i + 16)
                    v.wait_ge(s_sts[b], 16 * i + 16)
                    for half in range(2):
                        v.wait_ge(s_mm, half_upto(i, b, half))
                        js = slice(half * PER // 2, (half + 1) * PER // 2)
                        v.tensor_copy(sc[:, b, js], pP[:, js, O:W])
                        v.tensor_tensor(pre[:, b, js], pP[:, js, 0:O], rows_of(bias[:, :], PER // 2), ALU.add).then_inc(s_half, 1)

                prime(v, s_h)
                v.sem_inc(s_half, 2 * RG)
                turns(v, GROUPS, RG, [(elu, 0), (product, 2)], step, 1)

            @block.tensor
            def _(pe):
                def turn(i, b):
                    pe.wait_ge(s_h, upto(i, b))
                    pe.wait_ge(s_hT, upto(i, b, 1))
                    for j in range(PER):
                        for kb in range(2):
                            last = pe.transpose(pT[:, kb, j * P:(j + 1) * P], h[:, b, j, kb * D:(kb + 1) * D], K["ident"][:, :])
                    last.then_inc(s_turn, 1)

                def product(i, b):
                    pe.wait_ge(s_hT, upto(i, b))
                    for half in range(2):
                        pe.wait_ge(s_half, half_upto(i, b, half, 1))
                        for j in range(half * PER // 2, (half + 1) * PER // 2):
                            for kb in range(2):
                                last = pe.matmul(pP[:, j, 0:W], hT[:, b, kb, j * P:(j + 1) * P], weight[:, kb, :],
                                                 start=(kb == 0), stop=(kb == 1))
                        last.then_inc(s_mm, 1)

                prime(pe, s_turn)
                pe.sem_inc(s_mm, 2 * RG)
                turns(pe, GROUPS, RG, [(turn, 0), (product, 1)])


def final(nc, K, out):
    with phase(nc) as (ctx, sems):
        def sb(name, shape, dt=F32):
            return ctx.enter_context(nc.sbuf_tensor("l_" + name, shape, dt))

        def sem(name):
            s = ctx.enter_context(nc.semaphore("l_" + name))
            sems.append(s)
            return s

        x, p, e, u, y = (sb(c, [P, RG, PER, D]) for c in ("x", "p", "e", "u", "y"))
        norm = Norm(sb, sem, "")
        half = sb("half", [P, PER])
        ve = sb("ve", [P, RG, PER])
        s_ld, s_st = [sem(f"ld{b}") for b in range(RG)], [sem(f"st{b}") for b in range(RG)]
        s_e = sem("e")
        s_u = sem("u")
        s_done = sem("done")
        s_v, s_g = sem("v"), sem("g")
        with nc.Block() as block:
            xg, pg, og = grouped(K["x3"]), grouped(K["pre5"]), grouped(out)

            @block.sync
            def _(sp):
                stream(sp, s_ld, s_u,
                       [lambda g, b: sp.dma_start(flat(x[:, b]), xg[g]), lambda g, b: sp.dma_start(flat(p[:, b]), pg[g])],
                       [(3, s_done, upto, s_st, lambda g, b: sp.dma_start(og[g], flat(y[:, b])))])

            @block.scalar
            def _(act):
                def exp(i, b):
                    act.wait_ge(s_ld[b], 32 * i + 32)
                    act.wait_ge(s_u, upto(i, b, RG))
                    act.activation(e[:, b], p[:, b], ACT.Exp).then_inc(s_e, 1)

                prime(act, s_e)
                turns(act, GROUPS, RG, [(exp, 0)])

            @block.gpsimd
            def _(g):
                step = Steps(g, s_g)

                def root(i, b):
                    g.wait_ge(norm.s_mv, upto(i, b))
                    g.sem_inc(norm.s_gate, 1)
                    step(g.tensor_scalar(ve[:, b, :], norm.mv[:, b, :, 1], 1.0, EPS, ALU.mult, ALU.add))
                    g.tensor_tensor(norm.rs[:, b, :], ve[:, b, :], half[:, :], ALU.pow).then_inc(norm.s_sd, 1)

                step(g.memset(half[:, :], -0.5))
                prime(g, norm.s_sd)
                turns(g, GROUPS, RG, [(root, 0)], step, 1)

            @block.vector
            def _(v):
                step = Steps(v, s_v)

                def total(i, b):
                    v.wait_ge(s_e, upto(i, b))
                    step(v.tensor_scalar(flat(e[:, b]), flat(e[:, b]), 1.0, -1.0, ALU.min, ALU.add))
                    v.wait_ge(s_done, upto(i, b, RG))
                    step(v.scalar_tensor_tensor(flat(u[:, b]), flat(p[:, b]), 0.0, flat(e[:, b]), ALU.max, ALU.add))
                    v.tensor_tensor(u[:, b], u[:, b], x[:, b], ALU.add).then_inc(s_u, 1)
                    v.wait_ge(s_u, upto(i, b))
                    norm.stats(v, step, b, u[:, b])

                def rows(i, b):
                    v.wait_ge(norm.s_sd, upto(i, b))
                    v.wait_ge(s_st[b], 16 * i + 16)
                    for j in range(PER):
                        last = v.tensor_scalar(y[:, b, j, :], u[:, b, j, :], norm.mv[:, b, j, 0:1],
                                               norm.rs[:, b, j:j + 1], ALU.subtract, ALU.mult)
                    last.then_inc(s_done, 1)

                prime(v, s_u, s_done, norm.s_mv)
                turns(v, GROUPS, RG, [(total, 0), (rows, 1)], step, 3)


def kernel(**inputs):
    import concourse.bacc as bacc
    from concourse.bass_utils import run_bass_kernel_spmd

    a = {k: np.asarray(v) for k, v in inputs.items()}
    x = np.zeros((NPAD, D), np.float32)
    x[:N] = a["x"]
    src = np.full((EPAD,), N, np.int32)
    src[:E] = a["src"]
    dst = np.full((EPAD + T,), N, np.int32)
    dst[:E] = a["dst"]
    dst[EPAD:] = NPAD
    row = lambda v: np.ascontiguousarray(v).reshape(-1)
    turn = lambda v: np.ascontiguousarray(np.transpose(v))
    arrays = {
        "x": x, "src": src, "dst": dst,
        "w_hhT": turn(a["L0_gnn_W_hh"]), "w_ihT": turn(a["L0_gnn_W_ih"]), "w_msg": a["L0_gnn_W_msg"],
        "w1T": turn(a["L1_gnn_W"]), "w2T": turn(a["L2_gnn_W"]),
        "w_att": row(a["L0_gnn_W_att"]), "b_att": a["L0_gnn_b_att"], "b_msg": a["L0_gnn_b_msg"],
        "b_ih": turn(a["L0_gnn_b_ih"].reshape(3, D)), "b_hh": turn(a["L0_gnn_b_hh"].reshape(3, D)),
        "gamma": a["L0_gnn_gamma"].reshape(D, 1), "beta": a["L0_gnn_beta"].reshape(D, 1),
        "b1": a["L1_gnn_b"], "ln_g": a["L2_gnn_ln_gamma"], "ln_b": a["L2_gnn_ln_beta"], "b2": a["L2_gnn_b"],
    }
    for n in (1, 2, 3):
        arrays.update({f"g{n}w": a[f"L3_gnn_W{n}"], f"s{n}w": a[f"L3_gnn_s{n}W"], f"as{n}": row(a[f"L3_gnn_as{n}"]),
                       f"ad{n}": row(a[f"L3_gnn_ad{n}"]), f"g{n}b": a[f"L3_gnn_b{n}"], f"s{n}b": a[f"L3_gnn_s{n}b"]})
    nc = bacc.Bacc("TRN2", target_bir_lowering=False, num_devices=1)
    A = {k: nc.dram_tensor("in_" + k, v.shape, mybir.dt.from_np(v.dtype), kind="ExternalInput").ap()
         for k, v in arrays.items()}
    out = nc.dram_tensor("out", (NPAD, D), F32, kind="ExternalOutput").ap()
    build(nc, A, out)
    r = run_bass_kernel_spmd(nc, [{"in_" + k: v for k, v in arrays.items()}], core_ids=[0])
    return r.results[0]["out"][:N]
```

```python
from contextlib import ExitStack, contextmanager

import numpy as np

import concourse.bass as bass
from concourse import mybir

P = 128
N = 50000
E = 25000
D = 128
PER = 4
GROUP = P * PER
GROUPS = -(-N // GROUP)
NPAD = GROUPS * GROUP
LAST_VALID = (N - (GROUPS - 1) * GROUP) // PER
T = 196
EPAD = P * T
RING = 4
ITERS = T // RING
NROW = NPAD + RING * P
RG = RING
H1, C1 = 4, 64
HC = H1 * C1
H3 = 6
HELD = 84
EPS = 1e-5
BIG = 1e30

F32 = mybir.dt.float32
F16 = mybir.dt.float16
I32 = mybir.dt.int32
ALU = mybir.AluOpType
ACT = mybir.ActivationFunctionType
AX = mybir.AxisListType

assert T % RING == 0 and EPAD >= E and (N - (GROUPS - 1) * GROUP) % PER == 0


@contextmanager
def phase(nc):
    sems = []
    with ExitStack() as ctx:
        yield ctx, sems
        with nc.Block() as block:
            @block.gpsimd
            def _(pool):
                for s in sems:
                    pool.sem_clear(s)


class Steps:

    def __init__(self, eng, sem):
        self.eng, self.sem, self.n, self.base = eng, sem, 0, 0

    def __call__(self, ins):
        ins.then_inc(self.sem, 1)
        self.n += 1
        self.eng.wait_ge(self.sem, self.base + self.n)

    def loop(self, i, per):
        self.base, self.per, self.start = i * per, per, self.n

    def done(self, times):
        assert self.n - self.start == self.per, (self.n - self.start, self.per)
        self.base, self.n = 0, self.start + self.per * times


def grouped(table):
    return table[0:NPAD, :].rearrange("(g p j) d -> g p (j d)", g=GROUPS, p=P, j=PER)


def build(nc, A, out):
    ctx = ExitStack()
    with ctx:
        def sb(name, shape, dt=F32):
            return ctx.enter_context(nc.sbuf_tensor(name, shape, dt))

        def sem(name):
            return ctx.enter_context(nc.semaphore(name))

        def dram(name, shape):
            return nc.dram_tensor(name, shape, F32).ap()

        K = {"x": A["x"], "dma_sem": sem}
        K["agg0"] = dram("agg0", (NROW, D))
        K["agg1"] = dram("agg1", (NROW, D))
        K["hT"] = dram("hT", (D, NPAD))
        K["x1"] = dram("x1", (NPAD, D))
        K["msg"] = dram("msg", (NPAD, D))
        K["pre2"] = dram("pre2", (NROW, D))
        K["x3"] = dram("x3", (NPAD, D + 2 * H1))
        K["pre3"] = dram("pre3", (NROW, HC))
        K["h4"] = dram("h4", (NPAD, HC + 2 * H1))
        K["pre4"] = dram("pre4", (NROW, HC))
        K["h5"] = dram("h5", (NPAD, HC + 2 * H3))
        K["pre5"] = dram("pre5", (NROW, D))
        K["ident"] = sb("ident", [P, P])
        K["ones"] = sb("ones", [P, P])
        K["eps"] = sb("eps", [P, 1])
        K["mhalf"] = sb("mhalf", [P, PER])
        K["edge_idx"] = sb("edge_idx", [P, T + RING, 2], I32)
        K["scat_idx"] = sb("scat_idx", [P, T], I32)
        K["fin_idx"] = sb("fin_idx", [P, 1], I32)
        for m in ("cont", "cnext", "pcont", "pnext", "lead", "trail", "inner", "plead", "ptrail", "isq_in"):
            K[m] = sb(m, [P, T])
        for m in ("LF", "FF", "LL", "FL", "pLF", "pFF", "pLL", "pFL"):
            K[m] = sb("m" + m, [P, P])
        K["nosingle"] = sb("nosingle", [P, 1])
        K["isq_out"] = sb("isq_out", [P, GROUPS * PER])
        K["whh"] = sb("whh", [D, 3 * D])
        K["wih"] = sb("wih", [D, 3 * D])
        K["wmsg"] = sb("wmsg", [D, D])
        K["w1"] = sb("w1", [D, D])
        K["w2a"] = sb("w2a", [D, D])
        K["w2b"] = sb("w2b", [D, D])
        K["att"] = sb("att", [P, 2 * D])
        K["batt"] = sb("batt", [P, 1])
        K["bmsg"] = sb("bmsg", [P, D])
        K["brz"] = sb("brz", [D, 4])
        K["bn"] = sb("bn", [D, 2])
        K["bnss"] = sb("bnss", [D, 2])
        K["b1"] = sb("b1", [P, D])
        K["ln_g"] = sb("ln_g", [P, D])
        K["ln_b"] = sb("ln_b", [P, D])
        K["b2"] = sb("b2", [1, PER, D])
        K["g1w"] = sb("g1w", [D, HC])
        K["g1d"] = sb("g1d", [D, HC + 2 * H1])
        K["g1b"] = sb("g1b", [P, HC])
        K["g2w"] = sb("g2w", [D, 2, HC])
        K["g2d"] = sb("g2d", [D, 2, HC + 2 * H1])
        K["g2b"] = sb("g2b", [P, HC])
        K["g3w"] = sb("g3w", [D, 2, H3 * D])
        K["g3d"] = sb("g3d", [D, 2, D + 2 * H3])
        K["g3b"] = sb("g3b", [P, D])
        K["stats"] = sb("stats", [D, GROUPS, 6])

        prepare(nc, A, K)
        edges(nc, K, "e0", A["x"], K["wmsg"], K["agg0"])
        gru(nc, A, K)
        norm0(nc, A, K)
        edges(nc, K, "e1", K["x1"], K["w1"], K["agg1"])
        dense1(nc, K)
        edges(nc, K, "e2", K["msg"], K["w2b"], K["pre2"])
        dense2(nc, K)
        for n, (h, kb, w) in enumerate(((H1, 1, K["g1w"]), (H1, 2, K["g2w"]), (H3, 2, K["g3w"]))):
            table = (K["x3"], K["h4"], K["h5"])[n]
            pre, held = K[f"pre{n + 3}"], (T, HELD, HELD)[n]
            with (nc.sbuf_tensor(f"alpha{n}", [P, h, T], F32) as alpha,
                  nc.sbuf_tensor(f"hold{n}", [D, held, kb, P], F32) as hold):
                edge_scores(nc, K, n, h, kb, table, alpha, hold, held)
                edge_messages(nc, K, n, h, kb, w, table, pre, alpha, hold, held)
            if n < 2:
                dense_gat(nc, K, n, pre, K[f"h{n + 4}"], (K["g2d"], K["g3d"])[n], (K["g2b"], K["g3b"])[n],
                          K[f"pre{n + 4}"])
        final(nc, K, out)


ZERO_PARTS = 12
ZC = NROW * D // P // ZERO_PARTS
assert ZC * ZERO_PARTS * P == NROW * D


def zero_stores(table, zero):
    cells = table.rearrange("(p r) d -> p (r d)", p=P)
    return [(cells[:, c * ZC:(c + 1) * ZC], zero) for c in range(ZERO_PARTS)]


def prepare(nc, A, K):
    with phase(nc) as (ctx, sems):
        def sb(name, shape, dt=F32):
            return ctx.enter_context(nc.sbuf_tensor("prep_" + name, shape, dt))

        def sem(name):
            s = ctx.enter_context(nc.semaphore("prep_" + name))
            sems.append(s)
            return s

        zero = sb("zero", [P, ZC])
        dstF = sb("dstF", [P, T])
        nxtI = sb("nxtI", [P, T], I32)
        nxtF = sb("nxtF", [P, 1])
        dumI = sb("dumI", [P, T], I32)
        dum = sb("dum", [P, T])
        tmp = sb("tmp", [P, T])
        tmp2 = sb("tmp2", [P, T])
        idx = sb("idx", [P, 2, T], I32)
        lb = sb("lb", [P, P])
        fb = sb("fb", [P, P])
        bt = sb("bt", [D, 6])
        ts = sb("ts", [P, 2])
        s1w = sb("s1w", [D, HC])
        s2w = sb("s2w", [D, 2, HC])
        s3w = sb("s3w", [D, 2, D])
        avs = sb("avs", [P, 2, HC])
        avs2 = sb("avs2", [P, 2, HC])
        avs3 = sb("avs3", [P, 2, H3 * D])
        prod = sb("prod", [D, H3 * D])
        sbias = [sb(f"sbias{i}", [P, w]) for i, w in enumerate((HC, HC, D))]
        pfirst = ctx.enter_context(nc.psum_tensor("prep_pfirst", [P, 512], F32))
        plast = ctx.enter_context(nc.psum_tensor("prep_plast", [P, 512], F32))
        ptot = ctx.enter_context(nc.psum_tensor("prep_ptot", [P, 2, 512], F32))
        s_zero, s_ld, s_idx, s_zst, s_iota = sem("zero"), sem("ld"), sem("idx"), sem("zst"), sem("iota")
        s_id, s_fl, s_flT, s_tot, s_totp, s_sq, s_sqd, s_v = (
            sem("id"), sem("fl"), sem("flT"), sem("tot"), sem("totp"), sem("sq"), sem("sqd"), sem("v"))

        loads = [
            (K["whh"][:, :], A["w_hhT"]), (K["wih"][:, :], A["w_ihT"]), (K["wmsg"][:, :], A["w_msg"]),
            (K["w1"][:, :], A["w1T"]), (K["w2a"][:, :], A["w2T"][0:D, :]), (K["w2b"][:, :], A["w2T"][D:2 * D, :]),
            (K["att"][:, 0:D], A["w_att"][D:2 * D].partition_broadcast(P)),
            (K["att"][:, D:2 * D], A["w_att"][0:D].partition_broadcast(P)), (K["batt"][:, :], A["b_att"].partition_broadcast(P)),
            (K["bmsg"][:, :], A["b_msg"].partition_broadcast(P)),
            (bt[:, 0:3], A["b_ih"]), (bt[:, 3:6], A["b_hh"]),
            (K["bn"][:, 0:1], A["gamma"]), (K["bn"][:, 1:2], A["beta"]),
            (K["b1"][:, :], A["b1"].partition_broadcast(P)), (K["ln_g"][:, :], A["ln_g"].partition_broadcast(P)),
            (K["ln_b"][:, :], A["ln_b"].partition_broadcast(P)),
            *((K["b2"][:, j, :], A["b2"].partition_broadcast(1)) for j in range(PER)),
            (K["g1w"][:, :], A["g1w"]), (s1w[:, :], A["s1w"]),
            (K["g2w"][:, :, :], A["g2w"].rearrange("(k p) n -> p k n", p=D)),
            (s2w[:, :, :], A["s2w"].rearrange("(k p) n -> p k n", p=D)),
            (K["g3w"][:, :, :], A["g3w"].rearrange("(k p) n -> p k n", p=D)),
            (s3w[:, :, :], A["s3w"].rearrange("(k p) n -> p k n", p=D)),
            (avs[:, 0, :], A["as1"].partition_broadcast(P)), (avs[:, 1, :], A["ad1"].partition_broadcast(P)),
            (avs2[:, 0, :], A["as2"].partition_broadcast(P)), (avs2[:, 1, :], A["ad2"].partition_broadcast(P)),
            (avs3[:, 0, :], A["as3"].partition_broadcast(P)), (avs3[:, 1, :], A["ad3"].partition_broadcast(P)),
            (K["g1b"][:, :], A["g1b"].partition_broadcast(P)), (sbias[0][:, :], A["s1b"].partition_broadcast(P)),
            (K["g2b"][:, :], A["g2b"].partition_broadcast(P)), (sbias[1][:, :], A["s2b"].partition_broadcast(P)),
            (K["g3b"][:, :], A["g3b"].partition_broadcast(P)), (sbias[2][:, :], A["s3b"].partition_broadcast(P)),
        ]
        zeros = zero_stores(K["agg0"], zero[:, :])
        for name, w in (("pre2", D), ("pre3", HC), ("pre4", HC), ("pre5", D)):
            spare = K[name][NPAD:NROW, :].rearrange("(p r) d -> p (r d)", p=P)
            zeros.append((spare, zero[:, 0:RING * w]))

        with nc.Block() as block:

            @block.sync
            def _(sp):
                sp.dma_start(idx[:, 0, :], A["src"][0:EPAD].rearrange("(p t) -> p t", t=T)).then_inc(s_idx, 16)
                sp.dma_start(idx[:, 1, :], A["dst"][0:EPAD].rearrange("(p t) -> p t", t=T)).then_inc(s_idx, 16)
                sp.dma_start(nxtI[:, :], A["dst"][T:T + EPAD].rearrange("(p t) -> p t", t=T)).then_inc(s_idx, 16)
                for dst, src in loads:
                    sp.dma_start(dst, src).then_inc(s_ld, 16)
                sp.wait_ge(s_zero, 1)
                for dst, src in zeros:
                    sp.dma_start(dst, src).then_inc(s_zst, 16)
                sp.wait_ge(s_zst, 16 * len(zeros))

            @block.gpsimd
            def _(pool):
                pool.memset(zero[:, :], 0.0).then_inc(s_zero, 1)
                pool.memset(K["ident"][:, :], 0.0).then_inc(s_id, 1)
                pool.iota(dumI[:, :], pattern=[[0, ITERS], [P, RING]], base=NPAD, channel_multiplier=1).then_inc(s_iota, 1)
                pool.wait_ge(s_id, 1)
                pool.affine_select(out=K["ident"][:, :], in_=K["ident"][:, :], compare_op=ALU.not_equal, fill=1.0,
                                   base=0, pattern=[[-1, P]], channel_multiplier=1).then_inc(s_id, 1)

            @block.vector
            def _(v):
                step = Steps(v, s_v)
                v.memset(K["ones"][:, :], 1.0)
                v.memset(K["eps"][:, :], EPS)
                v.memset(K["mhalf"][:, :], -0.5)
                step(v.memset(K["edge_idx"][:, :, :], 0))
                v.wait_ge(s_idx, 48)
                v.tensor_copy(K["edge_idx"][:, 0:T, :], idx[:, :, :].rearrange("p s t -> p t s"))
                v.tensor_copy(dstF[:, :], idx[:, 1, :])
                step(v.tensor_copy(nxtF[:, :], nxtI[:, T - 1:T]))
                first, last = dstF[:, 0:1], dstF[:, T - 1:T]
                v.tensor_scalar(lb[:, :], K["ones"][:, :], last, None, ALU.mult)
                v.tensor_scalar(fb[:, :], K["ones"][:, :], first, None, ALU.mult).then_inc(s_fl, 1)
                v.memset(K["cont"][:, 0:1], 0.0)
                v.memset(K["cnext"][:, T - 1:T], 0.0)
                v.tensor_tensor(K["cont"][:, 1:T], dstF[:, 1:T], dstF[:, 0:T - 1], ALU.is_equal)
                step(v.tensor_tensor(K["cnext"][:, 0:T - 1], dstF[:, 1:T], dstF[:, 0:T - 1], ALU.is_equal))
                v.tensor_scalar(K["pcont"][:, :], K["cont"][:, :], -1.0, BIG, ALU.add, ALU.mult)
                v.tensor_scalar(K["pnext"][:, :], K["cnext"][:, :], -1.0, BIG, ALU.add, ALU.mult)
                v.wait_ge(s_iota, 1)
                step(v.tensor_copy(dum[:, :], dumI[:, :]))
                v.tensor_scalar(tmp2[:, :], K["cnext"][:, :], -1.0, 1.0, ALU.mult, ALU.add)
                step(v.tensor_tensor(tmp[:, :], dstF[:, :], dum[:, :], ALU.subtract))
                step(v.memset(tmp2[:, T - 1:T], 0.0))
                step(v.tensor_tensor(tmp2[:, :], tmp[:, :], tmp2[:, :], ALU.mult))
                step(v.tensor_tensor(K["scat_idx"][:, :], tmp2[:, :], dum[:, :], ALU.add))
                step(v.tensor_tensor(ts[:, 0:1], nxtF[:, :], last, ALU.not_equal))
                step(v.tensor_tensor(ts[:, 1:2], last, dum[:, 0:1], ALU.subtract))
                step(v.tensor_tensor(ts[:, 1:2], ts[:, 0:1], ts[:, 1:2], ALU.mult))
                step(v.tensor_tensor(K["fin_idx"][:, :], ts[:, 1:2], dum[:, 0:1], ALU.add))
                v.tensor_scalar(K["lead"][:, :], dstF[:, :], first, None, ALU.is_equal)
                step(v.tensor_scalar(tmp[:, :], dstF[:, :], last, None, ALU.is_equal))
                v.tensor_scalar(K["ptrail"][:, :], tmp[:, :], -1.0, BIG, ALU.add, ALU.mult)
                v.tensor_scalar(K["plead"][:, :], K["lead"][:, :], -1.0, BIG, ALU.add, ALU.mult)
                step(v.tensor_tensor(tmp2[:, :], tmp[:, :], K["lead"][:, :], ALU.mult))
                step(v.tensor_tensor(K["trail"][:, :], tmp[:, :], tmp2[:, :], ALU.subtract))
                step(v.tensor_tensor(tmp2[:, :], K["trail"][:, :], K["lead"][:, :], ALU.add))
                v.tensor_scalar(K["inner"][:, :], tmp2[:, :], -1.0, 1.0, ALU.mult, ALU.add)
                v.tensor_tensor(K["nosingle"][:, :], first, last, ALU.not_equal)
                v.wait_ge(s_flT, 1)
                for m, ps, s in (("LF", plast, first), ("FF", pfirst, first), ("LL", plast, last), ("FL", pfirst, last)):
                    ins = v.tensor_scalar(K[m][:, :], ps[:, 0:P], s, None, ALU.is_equal)
                step(ins)
                for m in ("LF", "FF", "LL", "FL"):
                    ins = v.tensor_scalar(K["p" + m][:, :], K[m][:, :], -1.0, BIG, ALU.add, ALU.mult)
                step(ins)
                v.tensor_tensor_scan(tmp[:, :], K["cont"][:, :], K["ones"][:, 0:1].to_broadcast([P, T]), 0.0, ALU.mult, ALU.add)
                step(v.tensor_tensor_scan(tmp2[:, ::-1], K["cnext"][:, ::-1], K["ones"][:, 0:1].to_broadcast([P, T]), 0.0, ALU.mult, ALU.add))
                v.tensor_copy(ts[:, 0:1], tmp[:, T - 1:T])
                step(v.tensor_tensor(ts[:, 1:2], tmp2[:, 0:1], K["nosingle"][:, :], ALU.mult))
                step(v.tensor_tensor(tmp[:, :], tmp[:, :], tmp2[:, :], ALU.add))
                step(v.tensor_scalar(tmp[:, :], tmp[:, :], -1.0, None, ALU.add))
                v.tensor_tensor(tmp[:, :], tmp[:, :], K["inner"][:, :], ALU.mult).then_inc(s_tot, 1)
                v.wait_ge(s_tot, 1)
                v.wait_ge(s_totp, 1)
                step(v.tensor_copy(ts[:, 0:2], ptot[:, :, 0]))
                step(v.scalar_tensor_tensor(tmp[:, :], K["lead"][:, :], ts[:, 0:1], tmp[:, :], ALU.mult, ALU.add))
                step(v.scalar_tensor_tensor(tmp[:, :], K["trail"][:, :], ts[:, 1:2], tmp[:, :], ALU.mult, ALU.add))
                v.tensor_scalar(tmp[:, :], tmp[:, :], 1.0, None, ALU.max).then_inc(s_sq, 1)
                v.wait_ge(s_sqd, 1)
                step(v.reciprocal(K["isq_in"][:, :], tmp2[:, :]))
                v.wait_ge(s_ld, 16 * len(loads))
                v.tensor_tensor(K["brz"][:, 0:2], bt[:, 0:2], bt[:, 3:5], ALU.add)
                v.tensor_copy(K["brz"][:, 2:3], bt[:, 2:3])
                v.tensor_copy(K["brz"][:, 3:4], bt[:, 5:6])
                v.tensor_tensor(K["g1b"][:, :], K["g1b"][:, :], sbias[0][:, :], ALU.add)
                v.tensor_tensor(K["g2b"][:, :], K["g2b"][:, :], sbias[1][:, :], ALU.add)
                v.tensor_tensor(K["g3b"][:, :], K["g3b"][:, :], sbias[2][:, :], ALU.add)
                v.tensor_tensor(K["g1d"][:, 0:HC], K["g1w"][:, :], s1w[:, :], ALU.add)
                step(v.tensor_tensor(K["g2d"][:, :, 0:HC], K["g2w"][:, :, :], s2w[:, :, :], ALU.add))
                for kb in range(2):
                    w = K["g3w"][:, kb, :]
                    step(v.tensor_reduce(prod[:, 0:D], w.rearrange("p (h c) -> p c h", h=H3), AX.X, ALU.add))
                    step(v.scalar_tensor_tensor(K["g3d"][:, kb, 0:D], prod[:, 0:D], 1.0 / H3, s3w[:, kb, :], ALU.mult, ALU.add))
                for w, a, h, o in ([(K["g1w"][:, :], avs, H1, K["g1d"][:, HC:])]
                                   + [(K["g2w"][:, kb, :], avs2, H1, K["g2d"][:, kb, HC:]) for kb in range(2)]
                                   + [(K["g3w"][:, kb, :], avs3, H3, K["g3d"][:, kb, D:]) for kb in range(2)]):
                    n = w.shape[1]
                    for side in range(2):
                        step(v.tensor_tensor(prod[:, 0:n], w, a[:, side, :], ALU.mult))
                        step(v.tensor_reduce(o[:, side * h:(side + 1) * h], prod[:, 0:n].rearrange("p (h c) -> p h c", h=h),
                                             AX.X, ALU.add))

            @block.tensor
            def _(pe):
                pe.wait_ge(s_id, 2)
                pe.wait_ge(s_fl, 1)
                pe.transpose(plast[:, 0:P], lb[:, :], K["ident"][:, :])
                pe.transpose(pfirst[:, 0:P], fb[:, :], K["ident"][:, :]).then_inc(s_flT, 1)
                pe.wait_ge(s_tot, 1)
                pe.matmul(ptot[:, 0, 0:1], K["FL"][:, :], ts[:, 0:1], start=True, stop=False)
                pe.matmul(ptot[:, 0, 0:1], K["FF"][:, :], ts[:, 1:2], start=False, stop=True)
                pe.matmul(ptot[:, 1, 0:1], K["LL"][:, :], ts[:, 0:1], start=True, stop=False)
                pe.matmul(ptot[:, 1, 0:1], K["LF"][:, :], ts[:, 1:2], start=False, stop=True).then_inc(s_totp, 1)

            @block.scalar
            def _(act):
                act.wait_ge(s_sq, 1)
                act.activation(tmp2[:, :], tmp[:, :], ACT.Sqrt).then_inc(s_sqd, 1)


def turns(eng, count, ring, stages, step=None, per=0, start=0):
    if start == count:
        return
    lags = max(lag for _, lag in stages)
    first, peel = start // ring, -(-lags // ring)

    def whole(i, k, edge):
        for f, lag in stages:
            back, slot = divmod(k - lag, ring)
            if not edge or start <= ring * (i + back) + slot < count:
                f(i + back, slot)

    for i in range(first, first + peel):
        for k in range(ring):
            whole(i, k, True)
    with eng.Fori(first + peel, count // ring) as i:
        if step:
            step.loop(i - (first + peel), per * ring)
        for k in range(ring):
            whole(i, k, False)
    if step:
        step.done(count // ring - first - peel)
    for i in range(count // ring, -(-(count + lags) // ring)):
        for k in range(ring):
            whole(i, k, True)


def prime(eng, *sems):
    for s in sems:
        eng.sem_inc(s, RG)


def upto(i, k, before=0):
    return RG * i + (k + 1 + RG - before)


def half_upto(i, k, half, before=0):
    return 2 * RG * i + (2 * k + half + 1 + 2 * RG - 2 * before)


def gather(pool, dst, table, idx):
    return pool.indirect_dma_start(dst, None, table, bass.IndirectOffsetOnAxis(idx, 0))


def next_index(K, i, k):
    return K["edge_idx"][:, bass.ds(i * RING + (k + RING), 1), :].rearrange("p a b -> p (a b)")


def scatter_add(pool, table, idx, src):
    return pool.indirect_dma_start(table, bass.IndirectOffsetOnAxis(idx, 0), src, None, compute_op=ALU.add)


def edges(nc, K, tag, table, weight, target):
    gated = tag == "e0"
    X = D if gated else 0
    W = D + 1 if gated else D
    with phase(nc) as (ctx, sems):
        def sb(name, shape, dt=F32):
            return ctx.enter_context(nc.sbuf_tensor(f"{tag}_{name}", shape, dt))

        def sem(name):
            s = ctx.enter_context(nc.semaphore(f"{tag}_{name}"))
            sems.append(s)
            return s

        prime_tile = sb("prime", [P, RING, 4])
        slot, out_slot = sb("slot", [P, RING, 2], I32), sb("oslot", [P, RING, 1], I32)
        xs = sb("xs", [P, RING, X + W])
        m, acc = sb("m", [P, RING, W]), sb("acc", [P, RING, W])
        accT, res = sb("accT", [D, RING, P]), sb("res", [P, RING, D])
        fin = sb("fin", [P, D])
        junk, logit, att = sb("junk", [P, RING, 2 * D]), sb("logit", [P, RING]), sb("attv", [P, RING])
        psT = ctx.enter_context(nc.psum_tensor(f"{tag}_psT", [P, 2, 512], F32))
        psY = ctx.enter_context(nc.psum_tensor(f"{tag}_psY", [P, RING, 512], F32))
        psF = ctx.enter_context(nc.psum_tensor(f"{tag}_psF", [P, 512], F32))
        s_got = [K["dma_sem"](f"{tag}_got{k}") for k in range(RING)]
        s_put = [K["dma_sem"](f"{tag}_put{k}") for k in range(RING)]
        s_finput = K["dma_sem"](f"{tag}_finput")
        s_slot = sem("slot")
        s_oslot = sem("oslot")
        s_logit, s_att = sem("logit"), sem("att_s")
        s_walk, s_turn, s_evac = sem("walk"), sem("turn"), sem("evac")
        s_mm, s_res = sem("mm"), sem("res")
        s_fin, s_finp, s_go, s_v = sem("fin"), sem("finp"), sem("go"), sem("v")
        tile_count = 32 if gated else 16

        s_code, s_counted = sem("code"), sem("counted")
        if gated:
            HI = GROUPS * PER
            zero, zero_row = sb("zero", [P, ZC]), sb("zero_row", [1, HI], F16)
            loI, hiI, lowI = sb("loI", [P, T], I32), sb("hiI", [P, T], I32), sb("lowI", [P, T], I32)
            lo, hi = sb("lo", [P, T]), sb("hi", [P, T])
            iotaI, iota = sb("iotaI", [P, HI], I32), sb("iota", [P, HI], F16)
            oh_lo, oh_hi = sb("oh_lo", [P, RING, P], F16), sb("oh_hi", [P, RING, HI], F16)
            deg = sb("deg", [P, HI])
            count = ctx.enter_context(nc.psum_tensor("e0_count", [P, 512], F32))
            s_zero, s_zst, s_iota, s_deg, s_root = sem("zero"), sem("zst"), sem("iota"), sem("deg"), sem("root")
        with nc.Block() as block:

            if gated:
                @block.sync
                def _(sp):
                    stores = zero_stores(K["agg1"], zero[:, :])
                    sp.wait_ge(s_zero, 1)
                    for dst, src in stores:
                        sp.dma_start(dst, src).then_inc(s_zst, 16)
                    sp.wait_ge(s_zst, 16 * len(stores))

            @block.gpsimd
            def _(pool):
                def fetch(i, k):
                    pool.wait_ge(s_slot, i * RING + (k + 1))
                    pool.sem_inc(s_go, 1)
                    if gated:
                        gather(pool, xs[:, k, 0:X], table, slot[:, k, 1:2]).then_inc(s_got[k], 16)
                    gather(pool, xs[:, k, X:X + D], table, slot[:, k, 0:1]).then_inc(s_got[k], 16)

                def put(i, k):
                    pool.wait_ge(s_oslot, i * RING + (k + 1))
                    pool.wait_ge(s_res, upto(i, k))
                    pool.sem_inc(s_go, 1)
                    scatter_add(pool, target, out_slot[:, k, :], res[:, k, :]).then_inc(s_put[k], 16)

                if gated:
                    pool.iota(iotaI[:, :], pattern=[[1, HI]], base=0, channel_multiplier=0).then_inc(s_iota, 1)
                for k in range(RING):
                    pool.dma_start(prime_tile[:, k, :], K["x"][0:P, 0:4]).then_inc(s_put[k], 16)
                turns(pool, T, RING, [(fetch, 0), (put, RING)])
                for k in range(RING):
                    pool.wait_ge(s_put[k], 16 * (ITERS + 1))
                pool.wait_ge(s_fin, 1)
                scatter_add(pool, target, K["fin_idx"][:, :], fin[:, :]).then_inc(s_finput, 16)
                pool.wait_ge(s_finput, 16)

            @block.vector
            def _(v):
                step = Steps(v, s_v)

                def dot(i, k):
                    v.wait_ge(s_got[k], tile_count * i + tile_count)
                    v.tensor_tensor_reduce(junk[:, k, :], xs[:, k, 0:2 * D], K["att"][:, :], 1.0, 0.0, ALU.mult, ALU.add,
                                           logit[:, k:k + 1]).then_inc(s_logit, 1)

                def walk(i, k):
                    message = m[:, k, :] if gated else xs[:, k, :]
                    if gated:
                        v.wait_ge(s_att, upto(i, k))
                        step(v.tensor_scalar(message, xs[:, k, X:X + W], att[:, k:k + 1], None, ALU.mult))
                        v.wait_ge(s_res, upto(i, k, RING))
                    else:
                        v.wait_ge(s_got[k], tile_count * i + tile_count)
                    v.wait_ge(s_turn, upto(i, k, RING))
                    v.wait_ge(s_walk, upto(i, k, 1))
                    v.scalar_tensor_tensor(acc[:, k, :], acc[:, (k - 1) % RING, :], K["cont"][:, bass.ds(i * RING + k, 1)],
                                           message, ALU.mult, ALU.add).then_inc(s_walk, 1)
                    v.tensor_copy(slot[:, k, :], next_index(K, i, k)).then_inc(s_slot, 1)

                def result(i, k):
                    v.wait_ge(s_mm, upto(i, k))
                    v.wait_ge(s_put[k], 16 * i + 16)
                    v.scalar_tensor_tensor(res[:, k, :], K["bmsg"][:, :], acc[:, k, D:W], psY[:, k, 0:D],
                                           ALU.mult, ALU.add).then_inc(s_res, 1)

                v.tensor_copy(slot[:, :, :], K["edge_idx"][:, 0:RING, :]).then_inc(s_slot, RING)
                def codes(i, k):
                    t = bass.ds(i * RING + k, 1)
                    v.wait_ge(s_counted, upto(i, k, RING))
                    v.tensor_scalar(oh_lo[:, k, :], iota[:, 0:P], lo[:, t], None, ALU.is_equal)
                    v.tensor_scalar(oh_hi[:, k, :], iota[:, :], hi[:, t], None, ALU.is_equal).then_inc(s_code, 1)

                if gated:
                    v.memset(xs[:, :, X + D:X + W], 1.0)
                    v.memset(zero_row[:, :], 0.0)
                    prime(v, s_code)
                    src = K["edge_idx"][:, 0:T, 0]
                    v.tensor_scalar(loI[:, :], src, 2, P - 1, ALU.logical_shift_right, ALU.bitwise_and)
                    v.tensor_scalar(hiI[:, :], src, 9, 2, ALU.logical_shift_right, ALU.logical_shift_left)
                    step(v.tensor_scalar(lowI[:, :], src, 3, None, ALU.bitwise_and))
                    v.tensor_copy(lo[:, :], loI[:, :])
                    v.tensor_tensor(hi[:, :], hiI[:, :], lowI[:, :], ALU.add)
                    v.wait_ge(s_iota, 1)
                    step(v.tensor_copy(iota[:, :], iotaI[:, :]))
                    v.memset(zero[:, :], 0.0).then_inc(s_zero, 1)
                step(v.memset(acc[:, RING - 1, :], 0.0))
                prime(v, s_walk)
                turns(v, T, RING, [(walk, 1), (result, 3), (codes, 0), (dot, 0)] if gated else [(walk, 0)], step, int(gated))
                if gated:
                    v.wait_ge(s_counted, T + RING)
                    v.tensor_scalar(deg[:, :], count[:, 0:HI], 1.0, None, ALU.max).then_inc(s_deg, 1)
                    v.wait_ge(s_root, 1)
                    v.reciprocal(K["isq_out"][:, :], deg[:, :])
                v.wait_ge(s_finp, 1)
                v.tensor_copy(fin[:, :], psF[:, 0:D]).then_inc(s_fin, 1)

            @block.tensor
            def _(pe):
                def turn(i, k):
                    pe.wait_ge(s_walk, upto(i, k))
                    pe.wait_ge(s_evac, upto(i, k, 2))
                    pe.transpose(psT[:, k % 2, 0:P], acc[:, k, 0:D], K["ident"][:, :]).then_inc(s_turn, 1)

                def product(i, k):
                    pe.wait_ge(s_evac, upto(i, k))
                    pe.wait_ge(s_res, upto(i, k, RING))
                    pe.matmul(psY[:, k, 0:D], accT[:, k, :], weight[:, :], start=True, stop=True).then_inc(s_mm, 1)

                def tally(i, k):
                    pe.wait_ge(s_code, upto(i, k))
                    pe.matmul(count[:, 0:HI], oh_lo[:, k, :], oh_hi[:, k, :], start=False, stop=False,
                              skip_group_check=True).then_inc(s_counted, 1)

                prime(pe, s_turn, s_mm)
                if gated:
                    prime(pe, s_counted)
                    pe.wait_ge(s_zero, 1)
                    pe.matmul(count[:, 0:HI], zero_row[:, 0:P], zero_row[:, :], start=True, stop=False, skip_group_check=True)
                turns(pe, T, RING, [(turn, 0), (product, 1)] + ([(tally, 0)] if gated else []))
                pe.wait_ge(s_res, T + RING)
                pe.matmul(psF[:, 0:D], K["LL"][:, :], res[:, RING - 1, :], start=True, stop=True).then_inc(s_finp, 1)

            @block.scalar
            def _(act):
                def gate(i, k):
                    act.wait_ge(s_logit, i * RING + (k + 1))
                    act.activation(att[:, k:k + 1], logit[:, k:k + 1], ACT.Sigmoid, bias=K["batt"][:, 0:1]).then_inc(s_att, 1)

                def take(i, k):
                    act.wait_ge(s_turn, upto(i, k))
                    act.wait_ge(s_mm, upto(i, k, RING))
                    act.copy(accT[:, k, :], psT[:, k % 2, 0:P]).then_inc(s_evac, 1)
                    act.wait_ge(s_put[k], 16 * i + 16)
                    act.copy(out_slot[:, k, :], K["scat_idx"][:, bass.ds(i * RING + k, 1)]).then_inc(s_oslot, 1)

                def result(i, k):
                    act.wait_ge(s_mm, upto(i, k))
                    act.wait_ge(s_put[k], 16 * i + 16)
                    if tag == "e1":
                        act.copy(res[:, k, :], psY[:, k, 0:D]).then_inc(s_res, 1)
                    else:
                        act.activation(res[:, k, :], psY[:, k, 0:D], ACT.Copy,
                                       scale=K["isq_in"][:, bass.ds(i * RING + k, 1)]).then_inc(s_res, 1)

                prime(act, s_evac, s_res, s_att)
                turns(act, T, RING, [(take, 2), (gate, 0)] if gated else [(take, 0), (result, 2)])
                if gated:
                    act.wait_ge(s_deg, 1)
                    act.activation(deg[:, :], deg[:, :], ACT.Sqrt).then_inc(s_root, 1)


def gru(nc, A, K):
    with phase(nc) as (ctx, sems):
        def sb(name, shape, dt=F32):
            return ctx.enter_context(nc.sbuf_tensor("gru_" + name, shape, dt))

        def ps(name, ring=1):
            return ctx.enter_context(nc.psum_tensor("gru_" + name, [P, ring, GROUP], F32))

        def sem(name):
            s = ctx.enter_context(nc.semaphore("gru_" + name))
            sems.append(s)
            return s

        x, agg = sb("x", [P, RG, PER, D]), sb("agg", [P, RG, PER, D])
        xT, aT = sb("xT", [D, RG, GROUP]), sb("aT", [D, RG, GROUP])
        r, z, n, t, h = (sb(c, [D, RG, GROUP]) for c in "rznth")
        pxT, paT = ps("pxT", 2), ps("paT", 2)
        pr, pz, pi, ph = (ps(c) for c in ("pr", "pz", "pi", "ph"))
        mv = sb("mv", [D, 2])
        sd = sb("sd", [D, 2])
        s_ld = [sem(f"ld{b}") for b in range(RG)]
        s_st = [sem(f"st{b}") for b in range(RG)]
        s_turn = sem("turn")
        s_xT, s_aT = sem("xT"), sem("aT")
        s_mr, s_mz, s_mi = sem("mr"), sem("mz"), sem("mi")
        s_r, s_z = sem("r"), sem("z")
        s_n = sem("n")
        s_t = sem("t")
        s_h = sem("h")
        s_v, s_var, s_sd = sem("v"), sem("var"), sem("sd")
        with nc.Block() as block:
            xg, ag = grouped(A["x"]), grouped(K["agg0"])
            hg = K["hT"].rearrange("d (g n) -> g d n", g=GROUPS)

            @block.sync
            def _(sp):
                def load(i, b):
                    sp.wait_ge(s_turn, upto(i, b, RG))
                    sp.dma_start(flat(x[:, b]), xg[RG * i + b]).then_inc(s_ld[b], 16)
                    sp.dma_start(flat(agg[:, b]), ag[RG * i + b]).then_inc(s_ld[b], 16)

                def store(i, b):
                    sp.wait_ge(s_h, upto(i, b))
                    sp.dma_start(hg[RG * i + b], h[:, b]).then_inc(s_st[b], 16)

                for b in range(RG):
                    sp.sem_inc(s_st[b], 16)
                turns(sp, GROUPS, RG, [(load, 0), (store, 4)])
                stored(sp, s_st)

            @block.tensor
            def _(pe):
                def turn(i, b):
                    pe.wait_ge(s_ld[b], 32 * i + 32)
                    pe.wait_ge(s_xT, upto(i, b, 2))
                    pe.wait_ge(s_aT, upto(i, b, 2))
                    for j in range(PER):
                        pe.transpose(pxT[:, b % 2, j * P:(j + 1) * P], x[:, b, j, :], K["ident"][:, :])
                        last = pe.transpose(paT[:, b % 2, j * P:(j + 1) * P], agg[:, b, j, :], K["ident"][:, :])
                    last.then_inc(s_turn, 1)

                def product(i, b):
                    pe.wait_ge(s_xT, upto(i, b))
                    pe.wait_ge(s_aT, upto(i, b))
                    for c, p, free, done in ((0, pr, s_r, s_mr), (1, pz, s_z, s_mz)):
                        pe.wait_ge(free, upto(i, b, 1))
                        pe.matmul(p[:, 0, :], K["wih"][:, c * D:(c + 1) * D], aT[:, b, :], start=True, stop=False)
                        pe.matmul(p[:, 0, :], K["whh"][:, c * D:(c + 1) * D], xT[:, b, :], start=False,
                                  stop=True).then_inc(done, 1)
                    pe.wait_ge(s_t, upto(i, b, 1))
                    pe.matmul(ph[:, 0, :], K["whh"][:, 2 * D:3 * D], xT[:, b, :], start=True, stop=True)
                    pe.matmul(pi[:, 0, :], K["wih"][:, 2 * D:3 * D], aT[:, b, :], start=True, stop=True).then_inc(s_mi, 1)

                prime(pe, s_turn, s_mr, s_mz, s_mi)
                turns(pe, GROUPS, RG, [(turn, 0), (product, 1)])

            @block.scalar
            def _(act):
                def take(i, b):
                    act.wait_ge(s_turn, upto(i, b))
                    act.wait_ge(s_h, upto(i, b, RG))
                    act.copy(xT[:, b, :], pxT[:, b % 2, :]).then_inc(s_xT, 1)
                    act.copy(aT[:, b, :], paT[:, b % 2, :]).then_inc(s_aT, 1)

                def gates(i, b):
                    act.wait_ge(s_mr, upto(i, b))
                    act.activation(r[:, b, :], pr[:, 0, :], ACT.Sigmoid, bias=K["brz"][:, 0:1]).then_inc(s_r, 1)
                    act.wait_ge(s_mz, upto(i, b))
                    act.activation(z[:, b, :], pz[:, 0, :], ACT.Sigmoid, bias=K["brz"][:, 1:2]).then_inc(s_z, 1)

                def tanh(i, b):
                    act.wait_ge(s_t, upto(i, b))
                    act.activation(n[:, b, :], t[:, b, :], ACT.Tanh, bias=K["brz"][:, 2:3]).then_inc(s_n, 1)

                prime(act, s_xT, s_aT, s_r, s_z, s_n)
                turns(act, GROUPS, RG, [(take, 0), (gates, 1), (tanh, 1)])
                act.wait_ge(s_var, 1)
                act.activation(sd[:, 0:1], mv[:, 1:2], ACT.Sqrt, bias=K["eps"][:, 0:1]).then_inc(s_sd, 1)

            @block.vector
            def _(v):
                step = Steps(v, s_v)

                def argument(i, b):
                    v.wait_ge(s_mi, upto(i, b))
                    v.wait_ge(s_r, upto(i, b))
                    step(v.scalar_tensor_tensor(t[:, b, :], ph[:, 0, :], K["brz"][:, 3:4], r[:, b, :], ALU.add, ALU.mult))
                    v.tensor_tensor(t[:, b, :], t[:, b, :], pi[:, 0, :], ALU.add).then_inc(s_t, 1)

                def state(i, b):
                    v.wait_ge(s_n, upto(i, b))
                    step(v.tensor_tensor(r[:, b, :], xT[:, b, :], n[:, b, :], ALU.subtract))
                    v.wait_ge(s_z, upto(i, b))
                    step(v.tensor_tensor(r[:, b, :], r[:, b, :], z[:, b, :], ALU.mult))
                    v.wait_ge(s_st[b], 16 * i + 16)
                    v.tensor_tensor(h[:, b, :], r[:, b, :], n[:, b, :], ALU.add).then_inc(s_h, 1)

                def stats(i, b):
                    v.wait_ge(s_h, upto(i, b))
                    v.bn_stats(K["stats"][:, g_slot(i, b), :].rearrange("p a b -> p (a b)"), h[:, b, :])

                prime(v, s_t, s_h)
                turns(v, GROUPS, RG, [(argument, 1), (state, 2), (stats, 2)], step, 3)
                v.drain()
                valid = h[:, (GROUPS - 1) % RG, :].rearrange("d (j p) -> d j p", j=PER)[:, :, 0:LAST_VALID]
                step(v.bn_stats(K["stats"][:, GROUPS - 1, :], valid))
                v.bn_aggr(mv[:, :], K["stats"][:, :, :].rearrange("p a b -> p (a b)")).then_inc(s_var, 1)
                v.wait_ge(s_sd, 1)
                step(v.reciprocal(sd[:, 1:2], sd[:, 0:1]))
                step(v.tensor_tensor(K["bnss"][:, 0:1], sd[:, 1:2], K["bn"][:, 0:1], ALU.mult))
                step(v.tensor_tensor(mv[:, 0:1], mv[:, 0:1], K["bnss"][:, 0:1], ALU.mult))
                step(v.tensor_tensor(K["bnss"][:, 1:2], K["bn"][:, 1:2], mv[:, 0:1], ALU.subtract))


def g_slot(i, b):
    return bass.ds(RG * i + b, 1)


class Norm:

    def __init__(self, sb, sem, tag):
        self.st, self.mv = sb(tag + "st", [P, RG, PER, 6]), sb(tag + "mv", [P, RG, PER, 2])
        self.sd, self.rs, self.shift, self.negative = (sb(tag + c, [P, RG, PER]) for c in ("sd", "rs", "shift", "negative"))
        self.s_mv, self.s_sd, self.s_rs = sem(tag + "mv"), sem(tag + "sd"), sem(tag + "rs")
        self.s_gate = sem(tag + "gate")

    def stats(self, v, step, b, u):
        for j in range(PER):
            last = v.bn_stats(self.st[:, b, j, :], u[:, j, :])
        step(last)
        v.sem_inc(self.s_gate, 1)
        for j in range(PER):
            last = v.bn_aggr(self.mv[:, b, j, :], self.st[:, b, j, :])
        last.then_inc(self.s_mv, 1)

    def scale_shift(self, g, K, step, i, b):
        g.wait_ge(self.s_mv, upto(i, b))
        g.sem_inc(self.s_gate, 1)
        g.tensor_scalar(self.negative[:, b, :], self.mv[:, b, :, 0], -1.0, None, ALU.mult)
        step(g.tensor_scalar(self.sd[:, b, :], self.mv[:, b, :, 1], 1.0, EPS, ALU.mult, ALU.add))
        step(g.tensor_tensor(self.rs[:, b, :], self.sd[:, b, :], K["mhalf"][:, :], ALU.pow))
        g.tensor_tensor(self.shift[:, b, :], self.negative[:, b, :], self.rs[:, b, :], ALU.mult).then_inc(self.s_rs, 1)

    def root(self, act, K, i, b):
        act.wait_ge(self.s_mv, upto(i, b))
        act.activation(self.sd[:, b, :], self.mv[:, b, :, 1], ACT.Sqrt, bias=K["eps"][:, 0:1]).then_inc(self.s_sd, 1)

    def inverse(self, v, step, i, b):
        v.wait_ge(self.s_sd, upto(i, b))
        step(v.reciprocal(self.rs[:, b, :], self.sd[:, b, :]))
        v.scalar_tensor_tensor(self.shift[:, b, :], self.mv[:, b, :, 0], -1.0, self.rs[:, b, :], ALU.mult,
                               ALU.mult).then_inc(self.s_rs, 1)

    def rows_scalar(self, act, i, b, out, u):
        act.wait_ge(self.s_rs, upto(i, b))
        for j in range(PER):
            last = act.activation(out[:, j, :], u[:, j, :], ACT.Identity, scale=self.rs[:, b, j:j + 1],
                                  bias=self.shift[:, b, j:j + 1])
        return last

    def rows_vector(self, v, step, i, b, out, u):
        v.wait_ge(self.s_sd, upto(i, b))
        step(v.reciprocal(self.rs[:, b, :], self.sd[:, b, :]))
        for j in range(PER):
            last = v.tensor_scalar(out[:, j, :], u[:, j, :], self.mv[:, b, j, 0:1], self.rs[:, b, j:j + 1],
                                   ALU.subtract, ALU.mult)
        return last


def last_half(i, k):
    return half_upto(i, k, 1)


def stored(sp, s_st):
    for b in range(RG):
        sp.wait_ge(s_st[b], 16 * (len(range(b, GROUPS, RG)) + 1))


def stream(sp, s_ld, s_used, loads, stores):
    def load(i, b):
        sp.wait_ge(s_used, upto(i, b, RG))
        for f in loads:
            f(RG * i + b, b).then_inc(s_ld[b], 16)

    stages = [(load, 0)]
    for lag, s_ready, value, s_st, f in stores:
        def store(i, b, s_ready=s_ready, value=value, s_st=s_st, f=f):
            sp.wait_ge(s_ready, value(i, b))
            f(RG * i + b, b).then_inc(s_st[b], 16)

        for b in range(RG):
            sp.sem_inc(s_st[b], 16)
        stages.append((store, lag))
    turns(sp, GROUPS, RG, stages)
    for _, _, _, s_st, _ in stores:
        stored(sp, s_st)


def flat(ap):
    return ap.rearrange("p j d -> p (j d)")


def rows_of(ap, n=PER):
    return ap.unsqueeze(1).to_broadcast([P, n, ap.shape[1]])


def norm0(nc, A, K):
    with phase(nc) as (ctx, sems):
        def sb(name, shape, dt=F32):
            return ctx.enter_context(nc.sbuf_tensor("n0_" + name, shape, dt))

        def sem(name):
            s = ctx.enter_context(nc.semaphore("n0_" + name))
            sems.append(s)
            return s

        x, hT, bT = sb("x", [P, RG, PER, D]), sb("hT", [D, RG, GROUP]), sb("bT", [D, RG, GROUP])
        u, y = sb("u", [P, RG, PER, D]), sb("y", [P, RG, PER, D])
        pb = ctx.enter_context(nc.psum_tensor("n0_pb", [P, 2, PER, D], F32))
        norm = Norm(sb, sem, "")
        s_ld, s_st = [sem(f"ld{b}") for b in range(RG)], [sem(f"st{b}") for b in range(RG)]
        s_bT = sem("bT")
        s_turn = sem("turn")
        s_sum = sem("sum")
        s_done = sem("done")
        s_v, s_g = sem("v"), sem("g")
        with nc.Block() as block:
            xg, yg = grouped(A["x"]), grouped(K["x1"])
            hg = K["hT"].rearrange("d (g n) -> g d n", g=GROUPS)

            @block.sync
            def _(sp):
                stream(sp, s_ld, s_sum,
                       [lambda g, b: sp.dma_start(flat(x[:, b]), xg[g]), lambda g, b: sp.dma_start(hT[:, b], hg[g])],
                       [(4, s_done, upto, s_st, lambda g, b: sp.dma_start(yg[g], flat(y[:, b])))])

            @block.scalar
            def _(act):
                def affine(i, b):
                    act.wait_ge(s_ld[b], 32 * i + 32)
                    act.wait_ge(s_turn, upto(i, b, RG))
                    act.activation(bT[:, b, :], hT[:, b, :], ACT.Identity, scale=K["bnss"][:, 0:1],
                                   bias=K["bnss"][:, 1:2]).then_inc(s_bT, 1)

                def rows(i, b):
                    act.wait_ge(s_st[b], 16 * i + 16)
                    norm.rows_scalar(act, i, b, y[:, b], u[:, b]).then_inc(s_done, 1)

                prime(act, s_bT, s_done)
                turns(act, GROUPS, RG, [(affine, 0), (rows, 2)])

            @block.gpsimd
            def _(g):
                step = Steps(g, s_g)
                prime(g, norm.s_rs)
                turns(g, GROUPS, RG, [(lambda i, b: norm.scale_shift(g, K, step, i, b), 0)], step, 2)

            @block.tensor
            def _(pe):
                def turn(i, b):
                    pe.wait_ge(s_bT, upto(i, b))
                    pe.wait_ge(s_sum, upto(i, b, 2))
                    for j in range(PER):
                        last = pe.transpose(pb[:, b % 2, j, :], bT[:, b, j * P:(j + 1) * P], K["ident"][:, :])
                    last.then_inc(s_turn, 1)

                prime(pe, s_turn)
                turns(pe, GROUPS, RG, [(turn, 0)])

            @block.vector
            def _(v):
                step = Steps(v, s_v)

                def total(i, b):
                    v.wait_ge(s_ld[b], 32 * i + 32)
                    v.wait_ge(s_turn, upto(i, b))
                    v.wait_ge(s_done, upto(i, b, RG))
                    v.tensor_tensor(u[:, b], pb[:, b % 2], x[:, b], ALU.add).then_inc(s_sum, 1)
                    v.wait_ge(s_sum, upto(i, b))
                    norm.stats(v, step, b, u[:, b])

                prime(v, s_sum, norm.s_mv)
                turns(v, GROUPS, RG, [(total, 0)], step, 1)


def dense1(nc, K):
    with phase(nc) as (ctx, sems):
        def sb(name, shape, dt=F32):
            return ctx.enter_context(nc.sbuf_tensor("d1_" + name, shape, dt))

        def sem(name):
            s = ctx.enter_context(nc.semaphore("d1_" + name))
            sems.append(s)
            return s

        x, agg, u, x2, w, hn, msg, pre = (sb(c, [P, RG, PER, D]) for c in ("x", "agg", "u", "x2", "w", "hn", "msg", "pre"))
        hT = sb("hT", [D, RG, GROUP])
        pT = ctx.enter_context(nc.psum_tensor("d1_pT", [P, 2, GROUP], F32))
        pP = ctx.enter_context(nc.psum_tensor("d1_pP", [P, 2, GROUP], F32))
        na, nb = Norm(sb, sem, "a"), Norm(sb, sem, "b")
        s_ld = [sem(f"ld{b}") for b in range(RG)]
        s_stm, s_stp = ([sem(f"st{c}{b}") for b in range(RG)] for c in "mp")
        s_biased = sem("biased")
        s_used = sem("used")
        s_w = sem("w")
        s_hn, s_msg = sem("hn"), sem("msg")
        s_turn, s_hT, s_mm = sem("turn"), sem("hT"), sem("mm")
        s_done = sem("done")
        s_v, s_g = sem("v"), sem("g")
        with nc.Block() as block:
            xg, ag, mg, pg = (grouped(K[t]) for t in ("x1", "agg1", "msg", "pre2"))

            @block.sync
            def _(sp):
                stream(sp, s_ld, s_used,
                       [lambda g, b: sp.dma_start(flat(agg[:, b]), ag[g]), lambda g, b: sp.dma_start(flat(x[:, b]), xg[g])],
                       [(5, s_msg, upto, s_stm, lambda g, b: sp.dma_start(mg[g], flat(msg[:, b]))),
                        (5, s_done, upto, s_stp, lambda g, b: sp.dma_start(pg[g], flat(pre[:, b])))])

            @block.vector
            def _(v):
                step = Steps(v, s_v)

                def total(i, b):
                    v.wait_ge(s_ld[b], 32 * i + 32)
                    v.wait_ge(s_biased, upto(i, b))
                    ins = v.scalar_tensor_tensor(flat(u[:, b]), flat(u[:, b]), 0.0, flat(x[:, b]), ALU.max, ALU.add)
                    ins.then_inc(s_used, 1)
                    v.wait_ge(s_used, upto(i, b))
                    na.stats(v, step, b, u[:, b])

                def first(i, b):
                    v.wait_ge(s_done, upto(i, b, RG))
                    step(na.rows_vector(v, step, i, b, x2[:, b], u[:, b]))
                    nb.stats(v, step, b, x2[:, b])

                def total2(i, b):
                    v.wait_ge(s_mm, upto(i, b))
                    v.wait_ge(s_stp[b], 16 * i + 16)
                    v.tensor_tensor(flat(pre[:, b]), pP[:, b % 2, :], flat(x2[:, b]), ALU.add).then_inc(s_done, 1)

                prime(v, s_used, s_done, na.s_mv, nb.s_mv, nb.s_rs)
                turns(v, GROUPS, RG, [(total, 0), (first, 1), (lambda i, b: nb.inverse(v, step, i, b), 2), (total2, 4)], step, 5)

            @block.gpsimd
            def _(g):
                step = Steps(g, s_g)

                def bias(i, b):
                    g.wait_ge(s_ld[b], 32 * i + 32)
                    g.wait_ge(nb.s_mv, upto(i, b, RG))
                    g.tensor_tensor(u[:, b], agg[:, b], rows_of(K["b1"][:, :]), ALU.add).then_inc(s_biased, 1)

                def affine(i, b):
                    g.wait_ge(s_w, upto(i, b))
                    step(g.tensor_tensor(w[:, b], w[:, b], rows_of(K["ln_g"][:, :]), ALU.mult))
                    g.wait_ge(s_turn, upto(i, b, RG))
                    g.wait_ge(s_msg, upto(i, b, RG))
                    g.tensor_tensor(hn[:, b], w[:, b], rows_of(K["ln_b"][:, :]), ALU.add).then_inc(s_hn, 1)

                prime(g, s_biased, s_hn)
                turns(g, GROUPS, RG, [(bias, 0), (affine, 3)], step, 1)

            @block.tensor
            def _(pe):
                def turn(i, b):
                    pe.wait_ge(s_hn, upto(i, b))
                    pe.wait_ge(s_hT, upto(i, b, 2))
                    for j in range(PER):
                        last = pe.transpose(pT[:, b % 2, j * P:(j + 1) * P], hn[:, b, j, :], K["ident"][:, :])
                    last.then_inc(s_turn, 1)

                def product(i, b):
                    pe.wait_ge(s_hT, upto(i, b))
                    pe.wait_ge(s_done, upto(i, b, 2))
                    pe.matmul(pP[:, b % 2, :], K["ones"][0:1, :], K["b2"][0:1, :, :].rearrange("p j d -> p (j d)"), start=True, stop=False,
                              skip_group_check=True)
                    for j in range(PER):
                        last = pe.matmul(pP[:, b % 2, j * D:(j + 1) * D], hT[:, b, j * P:(j + 1) * P], K["w2a"][:, :],
                                         start=False, stop=(j == PER - 1), skip_group_check=True)
                    last.then_inc(s_mm, 1)

                prime(pe, s_turn, s_mm)
                turns(pe, GROUPS, RG, [(product, 1), (turn, 0)])

            @block.scalar
            def _(act):
                def take(i, b):
                    act.wait_ge(s_turn, upto(i, b))
                    act.wait_ge(s_mm, upto(i, b, RG))
                    act.copy(hT[:, b, :], pT[:, b % 2, :]).then_inc(s_hT, 1)

                def messages(i, b):
                    act.wait_ge(s_hn, upto(i, b))
                    act.wait_ge(s_stm[b], 16 * i + 16)
                    for j in range(PER):
                        last = act.activation(msg[:, b, j, :], hn[:, b, j, :], ACT.Copy,
                                              scale=K["isq_out"][:, bass.ds(PER * RG * i + (PER * b + j), 1)])
                    last.then_inc(s_msg, 1)

                def rows(i, b):
                    act.wait_ge(s_hn, upto(i, b, RG))
                    nb.rows_scalar(act, i, b, w[:, b], x2[:, b]).then_inc(s_w, 1)

                prime(act, s_hT, s_w, s_msg, na.s_sd, nb.s_sd)
                turns(act, GROUPS, RG, [(take, 4), (messages, 4), (lambda i, b: na.root(act, K, i, b), 0),
                                        (lambda i, b: nb.root(act, K, i, b), 1), (rows, 2)])


def dense2(nc, K):
    W = HC + 2 * H1
    W3 = D + 2 * H1
    with phase(nc) as (ctx, sems):
        def sb(name, shape, dt=F32):
            return ctx.enter_context(nc.sbuf_tensor("d2_" + name, shape, dt))

        def sem(name):
            s = ctx.enter_context(nc.semaphore("d2_" + name))
            sems.append(s)
            return s

        u, xT = sb("u", [P, RG, PER, D]), sb("xT", [D, RG, GROUP])
        x3 = sb("x3", [P, RG, PER, W3])
        pre = sb("pre", [P, RG, PER, HC])
        pT = ctx.enter_context(nc.psum_tensor("d2_pT", [P, 2, GROUP], F32))
        pP = ctx.enter_context(nc.psum_tensor("d2_pP", [P, PER, 512], F32))
        norm = Norm(sb, sem, "")
        s_ld = [sem(f"ld{b}") for b in range(RG)]
        s_stx, s_stp = ([sem(f"st{c}{b}") for b in range(RG)] for c in "xp")
        s_x3 = sem("x3")
        s_turn, s_xT = sem("turn"), sem("xT")
        s_mm, s_half = sem("mm"), sem("half")
        s_v, s_g = sem("v"), sem("g")
        with nc.Block() as block:
            pg, xg, og = (grouped(K[t]) for t in ("pre2", "x3", "pre3"))

            @block.sync
            def _(sp):
                stream(sp, s_ld, s_x3,
                       [lambda g, b: sp.dma_start(flat(u[:, b]), pg[g])],
                       [(4, s_half, last_half, s_stx, lambda g, b: sp.dma_start(xg[g], flat(x3[:, b]))),
                        (4, s_half, last_half, s_stp, lambda g, b: sp.dma_start(og[g], flat(pre[:, b])))])

            @block.vector
            def _(v):
                step = Steps(v, s_v)

                def stats(i, b):
                    v.wait_ge(s_ld[b], 16 * i + 16)
                    norm.stats(v, step, b, u[:, b])

                def product(i, b):
                    v.wait_ge(s_stp[b], 16 * i + 16)
                    for half in range(2):
                        v.wait_ge(s_mm, half_upto(i, b, half))
                        js = slice(half * PER // 2, (half + 1) * PER // 2)
                        v.tensor_copy(x3[:, b, js, D:W3], pP[:, js, HC:W])
                        v.tensor_tensor(pre[:, b, js], pP[:, js, 0:HC], rows_of(K["g1b"][:, :], PER // 2), ALU.add).then_inc(s_half, 1)

                prime(v, norm.s_mv)
                v.sem_inc(s_half, 2 * RG)
                turns(v, GROUPS, RG, [(stats, 0), (product, 3)], step, 1)

            @block.gpsimd
            def _(g):
                step = Steps(g, s_g)
                prime(g, norm.s_rs)
                turns(g, GROUPS, RG, [(lambda i, b: norm.scale_shift(g, K, step, i, b), 0)], step, 2)

            @block.tensor
            def _(pe):
                def turn(i, b):
                    pe.wait_ge(s_x3, upto(i, b))
                    pe.wait_ge(s_xT, upto(i, b, 2))
                    for j in range(PER):
                        last = pe.transpose(pT[:, b % 2, j * P:(j + 1) * P], x3[:, b, j, 0:D], K["ident"][:, :])
                    last.then_inc(s_turn, 1)

                def product(i, b):
                    pe.wait_ge(s_xT, upto(i, b))
                    for half in range(2):
                        pe.wait_ge(s_half, half_upto(i, b, half, 1))
                        for j in range(half * PER // 2, (half + 1) * PER // 2):
                            last = pe.matmul(pP[:, j, 0:W], xT[:, b, j * P:(j + 1) * P], K["g1d"][:, :], start=True, stop=True)
                        last.then_inc(s_mm, 1)

                prime(pe, s_turn)
                pe.sem_inc(s_mm, 2 * RG)
                turns(pe, GROUPS, RG, [(turn, 0), (product, 1)])

            @block.scalar
            def _(act):
                def take(i, b):
                    act.wait_ge(s_turn, upto(i, b))
                    act.wait_ge(s_half, half_upto(i, b, 1, RG))
                    act.copy(xT[:, b, :], pT[:, b % 2, :]).then_inc(s_xT, 1)

                def rows(i, b):
                    act.wait_ge(s_stx[b], 16 * i + 16)
                    act.wait_ge(s_turn, upto(i, b, RG))
                    norm.rows_scalar(act, i, b, x3[:, b, :, 0:D], u[:, b]).then_inc(s_x3, 1)

                prime(act, s_xT, s_x3)
                turns(act, GROUPS, RG, [(rows, 1), (take, 2)])


def edge_scores(nc, K, n, H, KB, table, alpha, hold, held):
    R = KB * D
    with phase(nc) as (ctx, sems):
        def sb(name, shape, dt=F32):
            return ctx.enter_context(nc.sbuf_tensor(f"es{n}_{name}", shape, dt))

        def sem(name):
            s = ctx.enter_context(nc.semaphore(f"es{n}_{name}"))
            sems.append(s)
            return s

        slot = sb("slot", [P, RING, 2], I32)
        got = sb("got", [P, RING, 2, R + 2 * H])
        diff = sb("diff", [P, RING, R])
        rows = sb("rows", [P, T, 2, 2 * H])
        s, sf, F, B, M = (sb(c, [P, H, T]) for c in ("s", "self", "F", "B", "M"))
        junk = sb("junk", [P, P])
        bc = sb("bc", [P, 2 * H, P])
        ends = sb("ends", [P, 2, H])
        mx = sb("mx", [P, 4, H])
        pb = ctx.enter_context(nc.psum_tensor(f"es{n}_pb", [P, 2 * H, P], F32))
        pt = ctx.enter_context(nc.psum_tensor(f"es{n}_pt", [P, 2, 512], F32))
        psT = ctx.enter_context(nc.psum_tensor(f"es{n}_psT", [P, 2, 512], F32))
        s_got = [K["dma_sem"](f"es{n}_got{k}") for k in range(RING)]
        s_slot, s_v, s_go, s_bc, s_pb, s_ends, s_pt = (sem("slot"), sem("v"), sem("go"), sem("bc"), sem("pb"),
                                                       sem("ends"), sem("pt"))
        s_diff, s_turn, s_evac = sem("diff"), sem("turn"), sem("evac")
        s_arg, s_exp = sem("arg"), sem("exp")
        with nc.Block() as block:

            @block.gpsimd
            def _(pool):
                def fetch(i, k):
                    pool.wait_ge(s_slot, i * RING + (k + 1))
                    pool.sem_inc(s_go, 1)
                    for side in range(2):
                        gather(pool, got[:, k, side, :], table[:, :], slot[:, k, side:side + 1]).then_inc(s_got[k], 16)

                turns(pool, T, RING, [(fetch, 0)])

            @block.vector
            def _(v):
                def scores(i, k):
                    v.wait_ge(s_got[k], 32 * i + 32)
                    v.tensor_copy(rows[:, bass.ds(i * RING + k, 1), :, :].rearrange("p t s h -> p (t s) h"), got[:, k, :, R:])
                    v.tensor_copy(slot[:, k, :], next_index(K, i, k)).then_inc(s_slot, 1)

                def difference(i, k):
                    v.wait_ge(s_got[k], 32 * i + 32)
                    v.wait_ge(s_turn, upto(i, k, RING))
                    v.tensor_tensor(diff[:, k, :], got[:, k, 0, 0:R], got[:, k, 1, 0:R], ALU.subtract).then_inc(s_diff, 1)

                v.tensor_copy(slot[:, :, :], K["edge_idx"][:, 0:RING, :]).then_inc(s_slot, RING)
                turns(v, held, RING, [(difference, 0), (scores, 0)])
                turns(v, T, RING, [(scores, 0)], start=held)
                v.wait_ge(s_slot, T + RING)
                step = Steps(v, s_v)

                def part(side, which):
                    return rows[:, :, side, which * H:(which + 1) * H].rearrange("p t h -> p h t")

                v.tensor_tensor(s[:, :, :], part(0, 0), part(1, 1), ALU.add)
                step(v.tensor_tensor(sf[:, :, :], part(1, 0), part(1, 1), ALU.add))
                for a in (s, sf):
                    step(v.scalar_tensor_tensor(a[:, :, :], a[:, :, :], 0.2, a[:, :, :], ALU.mult, ALU.max))
                step(v.tensor_tensor(M[:, :, :], s[:, :, :], sf[:, :, :], ALU.max))
                for h in range(H):
                    v.tensor_tensor_scan(F[:, h, :], K["pcont"][:, :], M[:, h, :], -BIG, ALU.add, ALU.max)
                    last = v.tensor_tensor_scan(B[:, h, ::-1], K["pnext"][:, ::-1], M[:, h, ::-1], -BIG, ALU.add, ALU.max)
                step(last)
                for h in range(H):
                    v.tensor_scalar(bc[:, 2 * h, :], K["ones"][:, :], F[:, h, T - 1:T], None, ALU.mult)
                    v.tensor_scalar(bc[:, 2 * h + 1, :], K["ones"][:, :], B[:, h, 0:1], None, ALU.mult).then_inc(s_bc, 1)
                step(v.tensor_tensor(M[:, :, :], F[:, :, :], B[:, :, :], ALU.max))
                v.wait_ge(s_pb, H)
                for h in range(H):
                    for c, (half, pen) in enumerate(((0, "pLF"), (1, "pFF"), (0, "pLL"), (1, "pFL"))):
                        last = v.tensor_tensor_reduce(junk[:, :], pb[:, 2 * h + half, :], K[pen][:, :], 1.0, -BIG,
                                                      ALU.add, ALU.max, mx[:, c, h:h + 1])
                        step(last)
                step(v.tensor_tensor(mx[:, 0, :], mx[:, 0, :], mx[:, 1, :], ALU.max))
                step(v.tensor_tensor(mx[:, 2, :], mx[:, 2, :], mx[:, 3, :], ALU.max))
                for c, pen in ((0, "plead"), (2, "ptrail")):
                    for h in range(H):
                        last = v.scalar_tensor_tensor(M[:, h, :], K[pen][:, :], mx[:, c, h:h + 1], M[:, h, :], ALU.add, ALU.max)
                    step(last)
                v.tensor_tensor(s[:, :, :], s[:, :, :], M[:, :, :], ALU.subtract)
                v.tensor_tensor(sf[:, :, :], sf[:, :, :], M[:, :, :], ALU.subtract).then_inc(s_arg, 1)
                v.wait_ge(s_exp, 1)
                for h in range(H):
                    v.tensor_tensor_scan(F[:, h, :], K["cont"][:, :], s[:, h, :], 0.0, ALU.mult, ALU.add)
                    last = v.tensor_tensor_scan(B[:, h, ::-1], K["cnext"][:, ::-1], s[:, h, ::-1], 0.0, ALU.mult, ALU.add)
                step(last)
                v.tensor_copy(ends[:, 0, :], F[:, :, T - 1])
                v.tensor_scalar(ends[:, 1, :], B[:, :, 0], K["nosingle"][:, 0:1], None, ALU.mult).then_inc(s_ends, 1)
                step(v.tensor_tensor(M[:, :, :], F[:, :, :], B[:, :, :], ALU.add))
                step(v.tensor_tensor(M[:, :, :], M[:, :, :], s[:, :, :], ALU.subtract))
                step(v.tensor_tensor(M[:, :, :], M[:, :, :], K["inner"][:, :].unsqueeze(1).to_broadcast([P, H, T]), ALU.mult))
                v.wait_ge(s_pt, 1)
                step(v.tensor_copy(mx[:, 0:2, :], pt[:, :, 0:H]))
                for c, mask in enumerate(("lead", "trail")):
                    for h in range(H):
                        last = v.scalar_tensor_tensor(M[:, h, :], K[mask][:, :], mx[:, c, h:h + 1], M[:, h, :], ALU.mult, ALU.add)
                    step(last)
                step(v.tensor_tensor(M[:, :, :], M[:, :, :], sf[:, :, :], ALU.add))
                step(v.tensor_scalar(M[:, :, :], M[:, :, :], 1e-16, None, ALU.add))
                step(v.reciprocal(M[:, :, :], M[:, :, :]))
                v.scalar_tensor_tensor(alpha[:, :, :], s[:, :, :], 1.0 / H if n == 2 else 1.0, M[:, :, :], ALU.mult, ALU.mult)

            @block.tensor
            def _(pe):
                def turn(i, k):
                    pe.wait_ge(s_diff, i * RING + (k + 1))
                    pe.wait_ge(s_evac, upto(i, k, 2))
                    for kb in range(KB):
                        last = pe.transpose(psT[:, k % 2, kb * P:(kb + 1) * P], diff[:, k, kb * D:(kb + 1) * D],
                                            K["ident"][:, :])
                    last.then_inc(s_turn, 1)

                prime(pe, s_turn)
                turns(pe, held, RING, [(turn, 0)])
                for h in range(H):
                    pe.wait_ge(s_bc, h + 1)
                    pe.transpose(pb[:, 2 * h, :], bc[:, 2 * h, :], K["ident"][:, :])
                    pe.transpose(pb[:, 2 * h + 1, :], bc[:, 2 * h + 1, :], K["ident"][:, :]).then_inc(s_pb, 1)
                pe.wait_ge(s_ends, 1)
                pe.matmul(pt[:, 0, 0:H], K["FL"][:, :], ends[:, 0, :], start=True, stop=False)
                pe.matmul(pt[:, 0, 0:H], K["FF"][:, :], ends[:, 1, :], start=False, stop=True)
                pe.matmul(pt[:, 1, 0:H], K["LL"][:, :], ends[:, 0, :], start=True, stop=False)
                pe.matmul(pt[:, 1, 0:H], K["LF"][:, :], ends[:, 1, :], start=False, stop=True).then_inc(s_pt, 1)

            @block.scalar
            def _(act):
                def take(i, k):
                    act.wait_ge(s_turn, upto(i, k))
                    act.copy(hold[:, bass.ds(i * RING + k, 1)].rearrange("d t a b -> d (t a b)"),
                             psT[:, k % 2, 0:R]).then_inc(s_evac, 1)

                prime(act, s_evac)
                turns(act, held, RING, [(take, 0)])
                act.wait_ge(s_arg, 1)
                act.activation(s[:, :, :], s[:, :, :], ACT.Exp)
                act.activation(sf[:, :, :], sf[:, :, :], ACT.Exp).then_inc(s_exp, 1)


def edge_messages(nc, K, n, H, KB, weight, table, target, alpha, hold, held):
    C = C1 if n < 2 else D
    W = H * C
    O = W if n < 2 else D
    with phase(nc) as (ctx, sems):
        def sb(name, shape, dt=F32):
            return ctx.enter_context(nc.sbuf_tensor(f"em{n}_{name}", shape, dt))

        def sem(name):
            s = ctx.enter_context(nc.semaphore(f"em{n}_{name}"))
            sems.append(s)
            return s

        prime_tile = sb("prime", [P, RING, 4])
        slot, out_slot = sb("slot", [P, RING, 2], I32), sb("oslot", [P, RING, 1], I32)
        R = KB * D
        got = sb("got", [P, RING, 2, table.shape[1]])
        diff = sb("diff", [P, RING, R])
        dT = sb("dT", [D, RING, KB, P])
        acc, y = sb("acc", [P, RING, O]), sb("y", [P, RING, O])
        heads = sb("heads", [P, RING, H, C]) if n == 2 else None
        fin = sb("fin", [P, O])
        psT = ctx.enter_context(nc.psum_tensor(f"em{n}_psT", [P, 2, 512], F32))
        psY = ctx.enter_context(nc.psum_tensor(f"em{n}_psY", [P, 2, 512 * (-(-W // 512))], F32))
        psF = ctx.enter_context(nc.psum_tensor(f"em{n}_psF", [P, 512], F32))
        s_got = [K["dma_sem"](f"em{n}_got{k}") for k in range(RING)]
        s_put = [K["dma_sem"](f"em{n}_put{k}") for k in range(RING)]
        s_slot, s_go = sem("slot"), sem("go")
        s_diff = sem("diff")
        s_turn = sem("turn")
        s_evac = sem("evac")
        s_mm = sem("mm")
        s_walk = sem("walk")
        s_oslot, s_v = sem("oslot"), sem("v")
        s_fin, s_finp = sem("fin"), sem("finp")
        s_finput = K["dma_sem"](f"em{n}_finput")
        s_y = sem("y")
        s_heads = sem("heads")
        s_psY = s_y if n < 2 else s_heads
        with nc.Block() as block:

            @block.gpsimd
            def _(pool):
                def fetch(i, k):
                    pool.wait_ge(s_slot, i * RING + (k + 1))
                    pool.sem_inc(s_go, 1)
                    for side in range(2):
                        gather(pool, got[:, k, side, :], table[:, :], slot[:, k, side:side + 1]).then_inc(s_got[k], 16)

                def put(i, k):
                    pool.wait_ge(s_oslot, i * RING + (k + 1))
                    pool.wait_ge(s_walk, upto(i, k))
                    pool.sem_inc(s_go, 1)
                    scatter_add(pool, target[:, :], out_slot[:, k, :], acc[:, k, :]).then_inc(s_put[k], 16)

                for k in range(RING):
                    pool.dma_start(prime_tile[:, k, :], K["x"][0:P, 0:4]).then_inc(s_put[k], 16)
                turns(pool, held, RING, [(put, 0)])
                turns(pool, T, RING, [(fetch, 0), (put, RING)], start=held)
                for k in range(RING):
                    pool.wait_ge(s_put[k], 16 * (ITERS + 1))
                pool.wait_ge(s_fin, 1)
                scatter_add(pool, target[:, :], K["fin_idx"][:, :], fin[:, :]).then_inc(s_finput, 16)
                pool.wait_ge(s_finput, 16)

            @block.vector
            def _(v):
                step = Steps(v, s_v)

                def difference(i, k):
                    v.wait_ge(s_got[k], 32 * i + (32 - 32 * (held // RING)))
                    v.wait_ge(s_turn, upto(i, k, RING))
                    v.tensor_tensor(diff[:, k, :], got[:, k, 0, 0:R], got[:, k, 1, 0:R], ALU.subtract).then_inc(s_diff, 1)
                    v.tensor_copy(slot[:, k, :], next_index(K, i, k)).then_inc(s_slot, 1)

                def weigh(i, k):
                    v.wait_ge(s_mm, upto(i, k))
                    v.wait_ge(s_walk, upto(i, k, RING))
                    prod = psY[:, k % 2, 0:W].rearrange("p (h c) -> p h c", h=H)
                    scale = alpha[:, :, bass.ds(i * RING + k, 1)].to_broadcast([P, H, C])
                    v.tensor_tensor(y[:, k, :].rearrange("p (h c) -> p h c", h=H), prod, scale, ALU.mult).then_inc(s_y, 1)

                def total(i, k):
                    v.wait_ge(s_heads, upto(i, k))
                    v.wait_ge(s_walk, upto(i, k, RING))
                    v.tensor_reduce(y[:, k, :], heads[:, k].rearrange("p h c -> p c h"), AX.X, ALU.add).then_inc(s_y, 1)

                def walk(i, k):
                    v.wait_ge(s_y, upto(i, k))
                    v.wait_ge(s_walk, upto(i, k, 1))
                    v.wait_ge(s_put[k], 16 * i + 16)
                    v.scalar_tensor_tensor(acc[:, k, :], acc[:, (k - 1) % RING, :], K["cont"][:, bass.ds(i * RING + k, 1)],
                                           y[:, k, :], ALU.mult, ALU.add).then_inc(s_walk, 1)

                v.tensor_copy(slot[:, :, :], K["edge_idx"][:, held:held + RING, :]).then_inc(s_slot, RING)
                v.sem_inc(s_slot, held)
                v.sem_inc(s_diff, held)
                step(v.memset(acc[:, RING - 1, :], 0.0))
                prime(v, s_walk, s_y)
                message = weigh if n < 2 else total
                turns(v, held, RING, [(message, 0), (walk, 1)])
                turns(v, T, RING, [(message, 2 if n < 2 else 3), (walk, 3), (difference, 0)], start=held)
                v.wait_ge(s_finp, 1)
                v.tensor_copy(fin[:, :], psF[:, 0:O]).then_inc(s_fin, 1)

            @block.tensor
            def _(pe):
                def turn(i, k):
                    pe.wait_ge(s_diff, i * RING + (k + 1))
                    pe.wait_ge(s_evac, upto(i, k, 2))
                    for kb in range(KB):
                        last = pe.transpose(psT[:, k % 2, kb * P:(kb + 1) * P], diff[:, k, kb * D:(kb + 1) * D],
                                            K["ident"][:, :])
                    last.then_inc(s_turn, 1)

                def product(i, k):
                    pe.wait_ge(s_evac, upto(i, k))
                    pe.wait_ge(s_psY, upto(i, k, 2))
                    for c0 in range(0, W, 512):
                        c1 = min(W, c0 + 512)
                        for kb in range(KB):
                            rhs = weight[:, c0:c1] if KB == 1 else weight[:, kb, c0:c1]
                            last = pe.matmul(psY[:, k % 2, c0:c1], dT[:, k, kb, :], rhs, start=(kb == 0), stop=(kb == KB - 1))
                    last.then_inc(s_mm, 1)

                prime(pe, s_turn, s_mm)
                pe.sem_inc(s_turn, held)
                turns(pe, held, RING, [(product, 0)])
                turns(pe, T, RING, [(product, 1), (turn, 0)], start=held)
                pe.wait_ge(s_walk, T + RING)
                pe.matmul(psF[:, 0:O], K["LL"][:, :], acc[:, RING - 1, :], start=True, stop=True).then_inc(s_finp, 1)

            @block.scalar
            def _(act):
                def take(i, k):
                    act.wait_ge(s_turn, upto(i, k))
                    act.wait_ge(s_mm, upto(i, k, RING))
                    act.copy(dT[:, k].rearrange("d a b -> d (a b)"), psT[:, k % 2, 0:KB * P]).then_inc(s_evac, 1)

                def take_held(i, k):
                    act.wait_ge(s_mm, upto(i, k, RING))
                    act.copy(dT[:, k].rearrange("d a b -> d (a b)"),
                             hold[:, bass.ds(i * RING + k, 1)].rearrange("d t a b -> d (t a b)")).then_inc(s_evac, 1)

                def index(i, k):
                    act.wait_ge(s_put[k], 16 * i + 16)
                    act.copy(out_slot[:, k, :], K["scat_idx"][:, bass.ds(i * RING + k, 1)]).then_inc(s_oslot, 1)

                def weigh(i, k):
                    act.wait_ge(s_mm, upto(i, k))
                    act.wait_ge(s_y, upto(i, k, RING))
                    for h in range(H):
                        last = act.activation(heads[:, k, h, :], psY[:, k % 2, h * C:(h + 1) * C], ACT.Copy,
                                              scale=alpha[:, h, bass.ds(i * RING + k, 1)])
                    last.then_inc(s_heads, 1)

                prime(act, s_evac, s_heads)
                turns(act, held, RING, [(take_held, 0)] + ([(weigh, 1)] if n == 2 else []) + [(index, 1)])
                turns(act, T, RING, ([(weigh, 2)] if n == 2 else []) + [(index, 3), (take, 0)], start=held)


def dense_gat(nc, K, n, pre_in, table, weight, bias, pre_out):
    H = (H1, H3)[n]
    O = (HC, D)[n]
    W = O + 2 * H
    with phase(nc) as (ctx, sems):
        def sb(name, shape, dt=F32):
            return ctx.enter_context(nc.sbuf_tensor(f"dg{n}_{name}", shape, dt))

        def sem(name):
            s = ctx.enter_context(nc.semaphore(f"dg{n}_{name}"))
            sems.append(s)
            return s

        x, e = (sb(c, [P, RG, PER, HC]) for c in "xe")
        h = sb("h", [P, RG, PER, HC + 2 * H])
        hT = sb("hT", [D, RG, 2, GROUP])
        pre = sb("pre", [P, RG, PER, O])
        pT = ctx.enter_context(nc.psum_tensor(f"dg{n}_pT", [P, 2, GROUP], F32))
        pP = ctx.enter_context(nc.psum_tensor(f"dg{n}_pP", [P, PER, 512], F32))
        s_ld = [sem(f"ld{b}") for b in range(RG)]
        s_sth, s_stp = ([sem(f"st{c}{b}") for b in range(RG)] for c in "hp")
        s_e = sem("e")
        s_h = sem("h")
        s_turn = sem("turn")
        s_hT = sem("hT")
        s_mm, s_half = sem("mm"), sem("half")
        s_v = sem("v")
        with nc.Block() as block:
            ig, hg, og = grouped(pre_in), grouped(table), grouped(pre_out)

            @block.sync
            def _(sp):
                stream(sp, s_ld, s_h,
                       [lambda g, b: sp.dma_start(flat(x[:, b]), ig[g])],
                       [(4, s_half, last_half, s_sth, lambda g, b: sp.dma_start(hg[g], flat(h[:, b]))),
                        (4, s_half, last_half, s_stp, lambda g, b: sp.dma_start(og[g], flat(pre[:, b])))])

            @block.scalar
            def _(act):
                def exp(i, b):
                    act.wait_ge(s_ld[b], 16 * i + 16)
                    act.wait_ge(s_h, upto(i, b, RG))
                    act.activation(e[:, b], x[:, b], ACT.Exp).then_inc(s_e, 1)

                def take(i, b):
                    act.wait_ge(s_turn, upto(i, b))
                    act.wait_ge(s_mm, half_upto(i, b, 1, RG))
                    act.copy(hT[:, b], pT[:, :, :]).then_inc(s_hT, 1)

                prime(act, s_hT, s_e)
                turns(act, GROUPS, RG, [(exp, 0), (take, 1)])

            @block.vector
            def _(v):
                step = Steps(v, s_v)

                def elu(i, b):
                    v.wait_ge(s_e, upto(i, b))
                    step(v.tensor_scalar(flat(e[:, b]), flat(e[:, b]), 1.0, -1.0, ALU.min, ALU.add))
                    v.wait_ge(s_sth[b], 16 * i + 16)
                    v.wait_ge(s_turn, upto(i, b, RG))
                    v.scalar_tensor_tensor(h[:, b, :, 0:HC], x[:, b], 0.0, e[:, b], ALU.max, ALU.add).then_inc(s_h, 1)

                def product(i, b):
                    v.wait_ge(s_stp[b], 16 * i + 16)
                    for half in range(2):
                        v.wait_ge(s_mm, half_upto(i, b, half))
                        js = slice(half * PER // 2, (half + 1) * PER // 2)
                        v.tensor_copy(h[:, b, js, HC:], pP[:, js, O:W])
                        v.tensor_tensor(pre[:, b, js], pP[:, js, 0:O], rows_of(bias[:, :], PER // 2), ALU.add).then_inc(s_half, 1)

                prime(v, s_h)
                v.sem_inc(s_half, 2 * RG)
                turns(v, GROUPS, RG, [(elu, 0), (product, 2)], step, 1)

            @block.tensor
            def _(pe):
                def turn(i, b):
                    pe.wait_ge(s_h, upto(i, b))
                    pe.wait_ge(s_hT, upto(i, b, 1))
                    for j in range(PER):
                        for kb in range(2):
                            last = pe.transpose(pT[:, kb, j * P:(j + 1) * P], h[:, b, j, kb * D:(kb + 1) * D], K["ident"][:, :])
                    last.then_inc(s_turn, 1)

                def product(i, b):
                    pe.wait_ge(s_hT, upto(i, b))
                    for half in range(2):
                        pe.wait_ge(s_half, half_upto(i, b, half, 1))
                        for j in range(half * PER // 2, (half + 1) * PER // 2):
                            for kb in range(2):
                                last = pe.matmul(pP[:, j, 0:W], hT[:, b, kb, j * P:(j + 1) * P], weight[:, kb, :],
                                                 start=(kb == 0), stop=(kb == 1))
                        last.then_inc(s_mm, 1)

                prime(pe, s_turn)
                pe.sem_inc(s_mm, 2 * RG)
                turns(pe, GROUPS, RG, [(turn, 0), (product, 1)])


def final(nc, K, out):
    with phase(nc) as (ctx, sems):
        def sb(name, shape, dt=F32):
            return ctx.enter_context(nc.sbuf_tensor("l_" + name, shape, dt))

        def sem(name):
            s = ctx.enter_context(nc.semaphore("l_" + name))
            sems.append(s)
            return s

        x, p, e, u, y = (sb(c, [P, RG, PER, D]) for c in ("x", "p", "e", "u", "y"))
        norm = Norm(sb, sem, "")
        s_ld, s_st = [sem(f"ld{b}") for b in range(RG)], [sem(f"st{b}") for b in range(RG)]
        s_e = sem("e")
        s_u = sem("u")
        s_done = sem("done")
        s_v, s_g = sem("v"), sem("g")
        with nc.Block() as block:
            pg, og = grouped(K["pre5"]), grouped(out)
            xg = K["x3"].rearrange("(g p j) d -> g p j d", g=GROUPS, p=P, j=PER)[:, :, :, 0:D]

            @block.sync
            def _(sp):
                stream(sp, s_ld, s_u,
                       [lambda g, b: sp.dma_start(x[:, b], xg[g]), lambda g, b: sp.dma_start(flat(p[:, b]), pg[g])],
                       [(4, s_done, upto, s_st, lambda g, b: sp.dma_start(og[g], flat(y[:, b])))])

            @block.scalar
            def _(act):
                def exp(i, b):
                    act.wait_ge(s_ld[b], 32 * i + 32)
                    act.wait_ge(s_u, upto(i, b, RG))
                    act.activation(e[:, b], p[:, b], ACT.Exp).then_inc(s_e, 1)

                def rows(i, b):
                    act.wait_ge(s_st[b], 16 * i + 16)
                    norm.rows_scalar(act, i, b, y[:, b], u[:, b]).then_inc(s_done, 1)

                prime(act, s_e, s_done)
                turns(act, GROUPS, RG, [(exp, 0), (rows, 2)])

            @block.gpsimd
            def _(g):
                step = Steps(g, s_g)
                prime(g, norm.s_rs)
                turns(g, GROUPS, RG, [(lambda i, b: norm.scale_shift(g, K, step, i, b), 0)], step, 2)

            @block.vector
            def _(v):
                step = Steps(v, s_v)

                def total(i, b):
                    v.wait_ge(s_e, upto(i, b))
                    step(v.tensor_scalar(flat(e[:, b]), flat(e[:, b]), 1.0, -1.0, ALU.min, ALU.add))
                    v.wait_ge(s_done, upto(i, b, RG))
                    step(v.scalar_tensor_tensor(flat(u[:, b]), flat(p[:, b]), 0.0, flat(e[:, b]), ALU.max, ALU.add))
                    v.tensor_tensor(u[:, b], u[:, b], x[:, b], ALU.add).then_inc(s_u, 1)
                    v.wait_ge(s_u, upto(i, b))
                    norm.stats(v, step, b, u[:, b])

                prime(v, s_u, norm.s_mv)
                turns(v, GROUPS, RG, [(total, 0)], step, 3)


def kernel(**inputs):
    import concourse.bacc as bacc
    from concourse.bass_utils import run_bass_kernel_spmd

    a = {k: np.asarray(v) for k, v in inputs.items()}
    x = np.zeros((NPAD, D), np.float32)
    x[:N] = a["x"]
    src = np.full((EPAD,), N, np.int32)
    src[:E] = a["src"]
    dst = np.full((EPAD + T,), N, np.int32)
    dst[:E] = a["dst"]
    dst[EPAD:] = NPAD
    row = lambda v: np.ascontiguousarray(v).reshape(-1)
    turn = lambda v: np.ascontiguousarray(np.transpose(v))
    arrays = {
        "x": x, "src": src, "dst": dst,
        "w_hhT": turn(a["L0_gnn_W_hh"]), "w_ihT": turn(a["L0_gnn_W_ih"]), "w_msg": a["L0_gnn_W_msg"],
        "w1T": turn(a["L1_gnn_W"]), "w2T": turn(a["L2_gnn_W"]),
        "w_att": row(a["L0_gnn_W_att"]), "b_att": a["L0_gnn_b_att"], "b_msg": a["L0_gnn_b_msg"],
        "b_ih": turn(a["L0_gnn_b_ih"].reshape(3, D)), "b_hh": turn(a["L0_gnn_b_hh"].reshape(3, D)),
        "gamma": a["L0_gnn_gamma"].reshape(D, 1), "beta": a["L0_gnn_beta"].reshape(D, 1),
        "b1": a["L1_gnn_b"], "ln_g": a["L2_gnn_ln_gamma"], "ln_b": a["L2_gnn_ln_beta"], "b2": a["L2_gnn_b"],
    }
    for n in (1, 2, 3):
        arrays.update({f"g{n}w": a[f"L3_gnn_W{n}"], f"s{n}w": a[f"L3_gnn_s{n}W"], f"as{n}": row(a[f"L3_gnn_as{n}"]),
                       f"ad{n}": row(a[f"L3_gnn_ad{n}"]), f"g{n}b": a[f"L3_gnn_b{n}"], f"s{n}b": a[f"L3_gnn_s{n}b"]})
    nc = bacc.Bacc("TRN2", target_bir_lowering=False, num_devices=1)
    A = {k: nc.dram_tensor("in_" + k, v.shape, mybir.dt.from_np(v.dtype), kind="ExternalInput").ap()
         for k, v in arrays.items()}
    out = nc.dram_tensor("out", (NPAD, D), F32, kind="ExternalOutput").ap()
    build(nc, A, out)
    r = run_bass_kernel_spmd(nc, [{"in_" + k: v for k, v in arrays.items()}], core_ids=[0])
    return r.results[0]["out"][:N]
```
